# Optimizing a Trainium2 kernel written in Bass

```python
import numpy as np
import jax
import jax.numpy as jnp

def _softmax(x, axis=-1):
    return jax.nn.softmax(x, axis=axis)

def _gelu(x):
    return jax.nn.gelu(x, approximate=True)

def _silu(x):
    return jax.nn.silu(x)

def _sigmoid(x):
    return jax.nn.sigmoid(x)

def _layernorm(x, axis=-1, eps=1e-05):
    m = jnp.mean(x, axis=axis, keepdims=True)
    v = jnp.var(x, axis=axis, keepdims=True)
    return (x - m) / jnp.sqrt(v + eps)

def _scatter_add(tgt, idx, src, axis=0):
    return tgt.at[idx].add(src)

def _segment_sum(src, seg, n):
    return jax.ops.segment_sum(src, seg, n)
kernel_name = 'mk_decoder_preln_d1_seqx_r4_06ee3f'

def setup_inputs(seed: int=0):
    np.random.seed(seed)
    _w = jnp.asarray

    def _rec_inputs():
        import jax
        import jax.numpy as jnp
        _rk = jax.random.key(seed)
        x = -0.0002928 + 1 * jax.random.normal(jax.random.fold_in(_rk, 1), (2, 1024, 256), jnp.float32)
        _lenS = 1024 - jax.random.randint(jax.random.fold_in(_rk, 7), (2,), 0, max(1, 1024 // 4) + 1, jnp.int32)
        _lenS2 = 77 - jax.random.randint(jax.random.fold_in(_rk, 8), (2,), 0, max(1, 77 // 4) + 1, jnp.int32)
        _ctx_1024P = jax.random.normal(jax.random.fold_in(_rk, 11), (2, 16, 256), jnp.float32)
        _ctx_1024c = jax.random.dirichlet(jax.random.fold_in(_rk, 511), 0.3 * jnp.ones((16,), jnp.float32), (2, 77))
        _ctx_1024t = jnp.einsum('bsk,bkd->bsd', _ctx_1024c, _ctx_1024P)
        _ctx_1024t = _ctx_1024t * jax.lax.rsqrt(jnp.mean(jnp.square(_ctx_1024t)) + 1e-12) * 0.953939
        ctx_1024 = -1.39393e-06 + 0.999914 * (_ctx_1024t + 0.3 * jax.random.normal(jax.random.fold_in(_rk, 611), (2, 77, 256), jnp.float32))
        _validS = jnp.arange(1024)[None, :] < _lenS[:, None]
        _validS2 = jnp.arange(77)[None, :] < _lenS2[:, None]
        _causal = jnp.tril(jnp.ones((1024, 1024), dtype=bool))
        mask_BxS2_ik0 = jnp.where(jnp.broadcast_to(_validS2[:, :], (2, 77)), 0, 1).astype(jnp.int32)
        return (x, ctx_1024, mask_BxS2_ik0)
    x, ctx_1024, mask_BxS2_ik0 = _rec_inputs()

    def _L0_attn_setup():
        import jax, jax.numpy as jnp
        import numpy as np
        HEADS = 16
        DIMS = [64, 64, 64, 64]
        EPS = 0.0001
        P_POW = 2

        def _cdist(Q, K):
            q2 = jnp.sum(Q * Q, axis=-1)
            k2 = jnp.sum(K * K, axis=-1)
            qk = jnp.einsum('hbtd,hbsd->hbts', Q, K)
            d2 = q2[..., :, None] + k2[..., None, :] - 2.0 * qk
            return jnp.sqrt(jnp.maximum(d2, 0.0))
        key = jax.random.key(seed)
        ks = jax.random.split(key, 4)
        b, t, d_in = (2, 512, 256)
        d_proj = HEADS * sum(DIMS)
        X = jax.random.normal(ks[0], (b, t, d_in), dtype=jnp.float32)
        W_in = jax.random.normal(ks[1], (d_in, d_proj), dtype=jnp.float32) * d_in ** (-0.5)
        b_in = jnp.zeros((d_proj,), dtype=jnp.float32)
        W_out = jax.random.normal(ks[2], (HEADS * DIMS[2], d_in), dtype=jnp.float32) * (HEADS * DIMS[2]) ** (-0.5)
        b_out = jnp.zeros((d_in,), dtype=jnp.float32)
        return {'X': X, 'W_in': W_in, 'b_in': b_in, 'W_out': W_out, 'b_out': b_out}
    _L0_attn_all = _L0_attn_setup()
    _L0_attn_in = {k: v for k, v in _L0_attn_all.items() if k in ('W_in', 'b_in', 'W_out', 'b_out')}
    del _L0_attn_all

    def _L0_xattn_setup():
        import jax, jax.numpy as jnp
        import numpy as np
        D_MODEL = 256
        NUM_HEADS = 16
        DEPTH = D_MODEL // NUM_HEADS
        B, S = (2, 512)

        def _split_heads(x):
            b, s, _ = x.shape
            return x.reshape(b, s, NUM_HEADS, DEPTH).transpose(0, 2, 1, 3)
        key = jax.random.key(seed)
        ks = jax.random.split(key, 12)
        s = 1.0 / np.sqrt(D_MODEL)
        return {'query': jax.random.normal(ks[0], (B, S, D_MODEL), jnp.float32), 'key': jax.random.normal(ks[1], (B, S, D_MODEL), jnp.float32), 'value': jax.random.normal(ks[2], (B, S, D_MODEL), jnp.float32), 'mask': jax.random.randint(ks[3], (B, S), 0, 2, jnp.int32), 'Wq': jax.random.normal(ks[4], (D_MODEL, D_MODEL), jnp.float32) * s, 'bq': jnp.zeros((D_MODEL,), jnp.float32), 'Wk': jax.random.normal(ks[5], (D_MODEL, D_MODEL), jnp.float32) * s, 'bk': jnp.zeros((D_MODEL,), jnp.float32), 'Wv': jax.random.normal(ks[6], (D_MODEL, D_MODEL), jnp.float32) * s, 'bv': jnp.zeros((D_MODEL,), jnp.float32), 'Wo': jax.random.normal(ks[7], (D_MODEL, D_MODEL), jnp.float32) * s, 'bo': jnp.zeros((D_MODEL,), jnp.float32)}
    _L0_xattn_all = _L0_xattn_setup()
    _L0_xattn_in = {k: v for k, v in _L0_xattn_all.items() if k in ('Wq', 'bq', 'Wk', 'bk', 'Wv', 'bv', 'Wo', 'bo')}
    del _L0_xattn_all

    def _L0_ffn_setup():
        import jax, jax.numpy as jnp
        import numpy as np
        E, K = (8, 2)
        DM, DE = (256, 704)
        B, S = (1, 512)
        EPS = 1e-06

        def _rmsnorm(x, w):
            var = jnp.mean(jnp.square(x), axis=-1, keepdims=True)
            return x * jax.lax.rsqrt(var + EPS) * w
        key = jax.random.key(seed)
        kx, kg, k1, k2, k3 = jax.random.split(key, 5)

        def kaiming_uniform(k, shape, fan_in):
            bound = 1.0 / np.sqrt(fan_in)
            return jax.random.uniform(k, shape, jnp.float32, -bound, bound)
        return {'x': jax.random.normal(kx, (B, S, DM), jnp.float32), 'gate_w': kaiming_uniform(kg, (E, DM), DM), 'rms_w': jnp.ones((DM,), jnp.float32), 'W1': kaiming_uniform(k1, (E, DE, DM), DE * DM), 'W2': kaiming_uniform(k2, (E, DE, DM), DE * DM), 'W3': kaiming_uniform(k3, (E, DM, DE), DM * DE)}
    _L0_ffn_all = _L0_ffn_setup()
    _L0_ffn_in = {k: v for k, v in _L0_ffn_all.items() if k in ('gate_w', 'rms_w', 'W1', 'W2', 'W3')}
    del _L0_ffn_all
    return {'x': x, 'ctx_1024': ctx_1024, 'mask_BxS2_ik0': mask_BxS2_ik0, 'L0_attn_W_in': _L0_attn_in['W_in'], 'L0_attn_b_in': _L0_attn_in['b_in'], 'L0_attn_W_out': _L0_attn_in['W_out'], 'L0_attn_b_out': _L0_attn_in['b_out'], 'L0_xattn_Wq': _L0_xattn_in['Wq'], 'L0_xattn_bq': _L0_xattn_in['bq'], 'L0_xattn_Wk': _L0_xattn_in['Wk'], 'L0_xattn_bk': _L0_xattn_in['bk'], 'L0_xattn_Wv': _L0_xattn_in['Wv'], 'L0_xattn_bv': _L0_xattn_in['bv'], 'L0_xattn_Wo': _L0_xattn_in['Wo'], 'L0_xattn_bo': _L0_xattn_in['bo'], 'L0_ffn_gate_w': _L0_ffn_in['gate_w'], 'L0_ffn_rms_w': _L0_ffn_in['rms_w'], 'L0_ffn_W1': _L0_ffn_in['W1'], 'L0_ffn_W2': _L0_ffn_in['W2'], 'L0_ffn_W3': _L0_ffn_in['W3']}

def reference(x, ctx_1024, mask_BxS2_ik0, L0_attn_W_in, L0_attn_b_in, L0_attn_W_out, L0_attn_b_out, L0_xattn_Wq, L0_xattn_bq, L0_xattn_Wk, L0_xattn_bk, L0_xattn_Wv, L0_xattn_bv, L0_xattn_Wo, L0_xattn_bo, L0_ffn_gate_w, L0_ffn_rms_w, L0_ffn_W1, L0_ffn_W2, L0_ffn_W3):
    import jax
    import jax.numpy as jnp

    def _L0_attn_ref(X, W_in, b_in, W_out, b_out):
        import jax, jax.numpy as jnp
        import numpy as np
        HEADS = 16
        DIMS = [64, 64, 64, 64]
        EPS = 0.0001
        P_POW = 2

        def _cdist(Q, K):
            q2 = jnp.sum(Q * Q, axis=-1)
            k2 = jnp.sum(K * K, axis=-1)
            qk = jnp.einsum('hbtd,hbsd->hbts', Q, K)
            d2 = q2[..., :, None] + k2[..., None, :] - 2.0 * qk
            return jnp.sqrt(jnp.maximum(d2, 0.0))
        b, t, _ = X.shape
        P = X @ W_in + b_in
        P = P.reshape(b, t, HEADS, sum(DIMS))
        P = jnp.transpose(P, (2, 0, 1, 3))
        splits = np.cumsum(DIMS)[:-1]
        Q, K, V, G = jnp.split(P, splits, axis=-1)
        W = jnp.power(EPS + _cdist(Q, K), -P_POW)
        W = W / (EPS + jnp.sum(W, axis=-1, keepdims=True))
        A = jnp.einsum('hbts,hbse->hbte', W, V)
        H = G * A
        H = jnp.transpose(H, (1, 2, 0, 3)).reshape(b, t, HEADS * DIMS[2])
        return H @ W_out + b_out

    def _L0_xattn_ref(query, key, value, mask, Wq, bq, Wk, bk, Wv, bv, Wo, bo):
        import jax, jax.numpy as jnp
        import numpy as np
        D_MODEL = 256
        NUM_HEADS = 16
        DEPTH = D_MODEL // NUM_HEADS
        B, S = (2, 512)

        def _split_heads(x):
            b, s, _ = x.shape
            return x.reshape(b, s, NUM_HEADS, DEPTH).transpose(0, 2, 1, 3)
        q = _split_heads(query @ Wq.T + bq)
        k = _split_heads(key @ Wk.T + bk)
        v = _split_heads(value @ Wv.T + bv)
        scale = 1.0 / jnp.sqrt(jnp.float32(DEPTH))
        logits = jnp.einsum('bhqd,bhkd->bhqk', q, k) * scale
        logits = logits + mask.astype(logits.dtype)[:, None, None, :] * -1000000000.0
        attn = jax.nn.softmax(logits, axis=-1)
        out = jnp.einsum('bhqk,bhkd->bhqd', attn, v)
        out = out.transpose(0, 2, 1, 3).reshape(query.shape[0], -1, D_MODEL)
        return out @ Wo.T + bo

    def _L0_ffn_ref(x, gate_w, rms_w, W1, W2, W3):
        import jax, jax.numpy as jnp
        import numpy as np
        E, K = (8, 2)
        DM, DE = (256, 704)
        B, S = (1, 512)
        EPS = 1e-06

        def _rmsnorm(x, w):
            var = jnp.mean(jnp.square(x), axis=-1, keepdims=True)
            return x * jax.lax.rsqrt(var + EPS) * w
        y = _rmsnorm(x, rms_w)
        logits = jnp.einsum('bsd,ed->bse', y, gate_w)
        vals, idx = jax.lax.top_k(logits, K)
        w = jax.nn.softmax(vals, axis=-1)
        w_full = jnp.einsum('bsk,bske->bse', w, jax.nn.one_hot(idx, E, dtype=x.dtype))
        up = jnp.einsum('bsd,end->bsen', y, W1)
        gate = jnp.einsum('bsd,end->bsen', y, W2)
        h = jax.nn.silu(up) * gate
        out = jnp.einsum('bsen,emn->bsem', h, W3)
        comb = jnp.einsum('bsem,bse->bsm', out, w_full)
        return x + comb
    x = x + _L0_attn_ref(_layernorm(x, axis=-1), L0_attn_W_in, L0_attn_b_in, L0_attn_W_out, L0_attn_b_out)
    x = x + _L0_xattn_ref(_layernorm(x, axis=-1), ctx_1024, ctx_1024, mask_BxS2_ik0, L0_xattn_Wq, L0_xattn_bq, L0_xattn_Wk, L0_xattn_bk, L0_xattn_Wv, L0_xattn_bv, L0_xattn_Wo, L0_xattn_bo)
    x = x + _L0_ffn_ref(_layernorm(x, axis=-1), L0_ffn_gate_w, L0_ffn_rms_w, L0_ffn_W1, L0_ffn_W2, L0_ffn_W3)
    return x

_drawn_inputs = setup_inputs


def setup_inputs(seed=0):
    import zlib

    import numpy as np

    out = dict(_drawn_inputs(seed))
    spreads = {'L0_attn_b_in': (0.0, 0.1),
     'L0_attn_b_out': (0.0, 0.1),
     'L0_xattn_bq': (0.0, 0.388),
     'L0_xattn_bk': (0.0, 2.0),
     'L0_xattn_bv': (0.0, 0.1),
     'L0_xattn_bo': (0.0, 0.1),
     'L0_ffn_rms_w': (1.0, 0.6)}
    factors = {'L0_ffn_gate_w': 64.0, 'L0_ffn_W1': 64.0, 'L0_ffn_W2': 64.0, 'L0_ffn_W3': 64.0}
    for name, (base, spread) in spreads.items():
        noise = np.random.default_rng([zlib.crc32(name.encode()), seed]).standard_normal(out[name].shape)
        drawn = base * np.exp(spread * noise) if base else spread * noise
        out[name] = jnp.asarray(drawn.astype(out[name].dtype))
    for name, factor in factors.items():
        out[name] = (out[name] * factor).astype(out[name].dtype)
    return out
```

```python
from contextlib import ExitStack

import concourse.bass as bass
from concourse import mybir

ALU = mybir.AluOpType
ACT = mybir.ActivationFunctionType
AX = mybir.AxisListType
F32 = mybir.dt.float32
F32R = mybir.dt.float32r
U32 = mybir.dt.uint32

P = 128
B, T, D = 2, 1024, 256
H, DH = 16, 64
DC = D // P
NT = B * T // P
SB = T // P
HALF = T // 2
G = B * H
PAIRS = G // 2
EPS_D, EPS_LN, EPS_RMS = 1e-4, 1e-5, 1e-6
XH, XD = 16, D // 16
KC = 77
HPB = 4
HPC = XH // DC
E, DE = 8, 704
NC = -(-DE // P)
TG = 512
NG = B * T // TG
NEG = -1e9

C_ID, C_SEL, C_SCALE, C_ONE, C_LO, C_HM, C_IOTA, C_W = 0, 128, 192, 193, 194, 195, 203, 211


def constants(np):
    c = np.zeros((P, C_W), np.float32)
    c[:, C_ID:C_ID + P] = np.eye(P)
    c[0:64, C_SEL:C_SEL + 2] = 0.25
    c[64:128, C_SEL + 34:C_SEL + 36] = 1.0
    c[0:64, C_SCALE] = -2.0
    c[64:128, C_SCALE] = 1.0
    c[[66, 67, 96, 97], C_ONE] = 1.0
    c[[65, 99], C_LO] = -1.0
    c[np.arange(P), C_HM + np.arange(P) // XD] = 1.0
    c[:, C_IOTA:C_IOTA + E] = np.arange(E)
    return c


def program(nc, x, ctx_t, mask, w_in, b_in, w_out, w_x, b_cols, rows_in, gate_w, w1, w2, w3, consts, out):
    with ExitStack() as ctx:
        def sb(name, shape, dt=F32):
            return ctx.enter_context(nc.sbuf_tensor(name, shape, dt))

        def psum(name, shape, dt=F32):
            return ctx.enter_context(nc.psum_tensor(name, shape, dt))

        def sem(name):
            return ctx.enter_context(nc.semaphore(name))

        ps_s = psum("ps_s", [P, 2, T])
        ps_o = psum("ps_o", [P, T])
        ps_p = psum("ps_p", [P, T])

        h_t = nc.dram_tensor("h_t", [PAIRS, P, T], F32, kind="Internal").ap()

        cst = sb("cst", [P, C_W])
        x_sb = sb("x_sb", [P, NT, D])
        xn_t = sb("xn_t", [P, DC, B * T])
        stats = sb("stats", [P, NT, 6])
        mean_var = sb("mean_var", [P, NT, 2])
        std = sb("std", [P, NT])
        rstd = sb("rstd", [P, NT])
        w_head = sb("w_head", [P, 2, DC, 4 * DH])
        b_qk = sb("b_qk", [P, H])
        b_vg = sb("b_vg", [P, H])
        qk = sb("qk", [P, T])
        qk_sq = sb("qk_sq", [P, T])
        qa = sb("qa", [P, T], F32R)
        ka = sb("ka", [P, T], F32R)
        qb = sb("qb", [96, T], F32R)
        kb = sb("kb", [96, T], F32R)
        norms = sb("norms", [P, T])
        norms_hi = sb("norms_hi", [P, T], F32R)
        vg = sb("vg", [P, 2, T])
        v_aug = sb("v_aug", [P, 2, SB, P])
        wts = sb("wts", [P, 2, SB, T])
        rinv = sb("rinv", [P, T])
        g_r = sb("g_r", [P, T])
        h_pair = sb("h_pair", [P, T])
        eps_d = sb("eps_d", [P, 1])
        eps_ln = sb("eps_ln", [P, 1])

        w_o = sb("w_o", [P, H // 2, D])
        w_x_sb = sb("w_x_sb", [P, 4, DC, D])
        ctx_sb = sb("ctx_sb", [P, DC, B * KC])
        b_qk_x = sb("b_qk_x", [P, 2 * DC])
        brow = sb("brow", [P, 4, D])
        mask_i = sb("mask_i", [P, B * KC], mybir.dt.int32)
        mask_f = sb("mask_f", [P, B, KC])
        k_raw = sb("k_raw", [P, B * DC, KC])
        k_blk = sb("k_blk", [P, B * DC, HPC, KC])
        v_x = sb("v_x", [KC, B, XH, XD + 1])
        gate_sb = sb("gate_sb", [P, DC, E])
        h_tile = qk[:].rearrange("p (q t) -> p q t", t=P)
        x1s = sb("x1s", [P, D])
        x2s = sb("x2s", [P, D])
        st2 = sb("st2", [P, 2, 6])
        mv2 = sb("mv2", [P, 2, 2])
        r2 = sb("r2", [P, 4])
        xn2 = norms[:, 0:D]
        xn2_t = norms[:, D:2 * D].rearrange("p (c t) -> p c t", t=P)
        q_t = norms[:, 2 * D:3 * D].rearrange("p (c t) -> p c t", t=P)
        o_x = norms[:, 3 * D:4 * D].rearrange("p (h d) -> p h d", d=XD)
        lg = v_aug[:].rearrange("p a b t -> p (a b t)")[:, 0:XH * KC].rearrange("p (h k) -> p h k", k=KC)
        lmax = sb("lmax", [P, XH])
        p_t = vg[0:KC].rearrange("p a t -> p (a t)").rearrange("p (h t) -> p h t", t=P)
        den = sb("den", [P, XH])
        o_t = qk_sq[:, 0:D].rearrange("p (c t) -> p c t", t=P)
        xin = qk_sq[:, D:2 * D]
        sq_junk = qk_sq[:, 2 * D:3 * D]
        y_n = qk_sq[:, 3 * D:4 * D]
        y_tile = rinv[:, 0:D].rearrange("p (c t) -> p c t", t=P)
        gl = sb("gl", [P, NT, E])
        top = sb("top", [P, NT, 8])
        top_i = sb("top_i", [P, NT, 8], U32)
        top_f = sb("top_f", [P, NT, 2])
        pw = sb("pw", [P, 5, NT])
        w_full = sb("w_full", [P, 2, NT, E])
        eps_rms = sb("eps_rms", [P, 1])
        room = wts[:].rearrange("p a b t -> p (a b t)")
        W12, W3, HH = 2 * DC * DE, NC * D, NC * TG
        w12 = room[:, 0:2 * W12].rearrange("p (s k c n) -> p s k c n", s=2, k=2, c=DC)
        w3_sb = room[:, 2 * W12:2 * W12 + 2 * W3].rearrange("p (s n d) -> p s n d", s=2, n=NC)
        at = 2 * (W12 + W3)
        up_s = room[:, at:at + 2 * TG].rearrange("p (s t) -> p s t", s=2)
        h_mid = room[:, at + 2 * TG:at + 2 * TG + 2 * HH].rearrange("p (s n t) -> p s n t", s=2, n=NC)
        y_t = xn_t

        names = ("x_in", "c_in", "stats_ok", "aggr_ok", "std_ok", "rstd_ok", "xn_ok", "tr_ok", "xnt_ok",
                 "w_even", "w_odd", "qk_proj", "vg_proj", "norm_mm", "v_turned", "s_ready", "av_done",
                 "qk_ok", "hi_ok", "vg_ok", "norms_ok", "norms_hi_ok", "split_ok", "v_ok", "max_ok", "h_ok",
                 "sq_ok", "gr_ok", "sqrt_ok", "ln_ok", "w_ok", "rln_ok", "r_ok", "h_out", "eps_ok",
                 "kv_mm", "k_ok", "kv_ok", "mask_ok", "xb_ok",
                 "ht_in", "y_mm", "pt_mm", "xt_mm", "avx_mm", "q_mm", "ot_mm", "lg_mm", "out_mm", "yt_mm", "gl_mm",
                 "x1_ok", "st_ok", "mv_ok", "xn2_ok", "xnt2_ok", "ptd_ok", "den_ok", "o_ok", "qt_ok", "ot_ok", "l_ok",
                 "lmax_ok", "x2_ok", "st2_ok", "mv2_ok", "xin_ok", "y_ok", "yt_ok", "gl_ok",
                 "pta_ok", "lr1", "r1_ok", "lr2", "r2_ok", "ms_ok", "lr3", "r3_ok", "exp_ok",
                 "x1b_ok", "sub_ok", "base_ok", "ytr_ok", "top_ok", "topi_ok", "topf_ok", "dlt_ok", "pe_ok", "pw_ok", "wf_ok",
                 "e_even", "e_odd", "ug_mm", "silu_ok", "hm_ok", "eo_mm", "acc_ok", "done")
        s = {n: sem(n) for n in names}
        S_ = type("Sems", (), s)

        ident = cst[:, C_ID:C_ID + P]
        xn = wts[:, 0, 0:4, :].rearrange("p a (b d) -> p (a b) d", d=D)

        block = ctx.enter_context(nc.Block())

        def rs_rows(par):
            return slice(64, 128) if par == 0 else slice(0, 64)

        def v_rows(par):
            return slice(0, 64) if par == 0 else slice(64, 128)

        @block.sync
        def _(sp):
            sp.dma_start(x_sb[:], x.rearrange("b (n p) d -> p (b n) d", p=P)).then_inc(S_.x_in, 16)
            sp.dma_start(cst[:], consts).then_inc(S_.c_in, 16)
            sp.dma_start(b_qk[:], b_in[0]).then_inc(S_.c_in, 16)
            sp.dma_start(b_vg[:], b_in[1]).then_inc(S_.c_in, 16)
            for c in range(DC):
                sp.dma_start(ctx_sb[:, c], ctx_t[c * P:(c + 1) * P]).then_inc(S_.c_in, 16)
            for k in range(4):
                sp.dma_start(w_x_sb[:, k], w_x[k].rearrange("(c p) n -> p c n", p=P)).then_inc(S_.c_in, 16)
            sp.dma_start(b_qk_x[:], b_cols).then_inc(S_.c_in, 16)
            for k in range(4):
                sp.dma_start(brow[:, k], rows_in[k:k + 1].partition_broadcast(P)).then_inc(S_.c_in, 16)
            sp.dma_start(mask_i[:], mask.partition_broadcast(P)).then_inc(S_.c_in, 16)
            sp.dma_start(gate_sb[:], gate_w.rearrange("(c p) e -> p c e", p=P)).then_inc(S_.c_in, 16)
            sp.dma_start(w_o[:], w_out.rearrange("(q p) n -> p q n", p=P)).then_inc(S_.c_in, 16)

            def load_head(col, par):
                src = w_in.rearrange("(c p) n -> p c n", p=P)[:, :, bass.ds(col, 4 * DH)]
                sp.dma_start(w_head[:, par], src).then_inc((S_.w_even, S_.w_odd)[par], 16)

            def store_pair(p):
                sp.wait_ge(S_.x_in, 16)
                sp.wait_ge(S_.h_ok, 2 * p + 2)
                sp.dma_start(h_t[bass.ds(p, 1)].rearrange("a p t -> p (a t)"), h_pair[:]).then_inc(S_.h_out, 16)

            load_head(0, 0)
            load_head(4 * DH, 1)
            for b in range(B):
                p0 = b * H // 2
                with sp.Fori(max(p0, 1), p0 + H // 2) as p:
                    for par in range(2):
                        sp.wait_ge(S_.vg_proj, 2 * p + par - 1)
                        load_head(((p - p0) * 2 + par) * 4 * DH, par)
                    store_pair(p - 1)
            store_pair(PAIRS - 1)
            sp.wait_ge(S_.h_out, 16 * PAIRS)

            def load_tile(i):
                src = h_t.rearrange("(b q) p t -> b p q t", b=B)[bass.ds((i >> 3) & 1, 1), :, :, bass.ds((i & 7) * P, P)]
                sp.dma_start(h_tile, src.rearrange("b p q t -> p (b q) t")).then_inc(S_.ht_in, 16)

            load_tile(0)
            with sp.Fori(1, NT) as i:
                sp.wait_ge(S_.x_in, 16)
                sp.wait_ge(S_.y_mm, i)
                load_tile(i)

            def load_expert(e, slot):
                q = (S_.e_even, S_.e_odd)[slot]
                for k, w in enumerate((w1, w2)):
                    sp.dma_start(w12[:, slot, k], w[bass.ds(e, 1)].rearrange("e (c p) n -> p (e c) n", p=P)).then_inc(q, 16)
                sp.dma_start(w3_sb[:, slot, 0:NC - 1], w3[bass.ds(e, 1), 0:(NC - 1) * P].rearrange(
                    "e (n p) d -> p (e n) d", p=P)).then_inc(q, 16)
                sp.dma_start(w3_sb[0:DE - (NC - 1) * P, slot, NC - 1], w3[bass.ds(e, 1), (NC - 1) * P:DE].rearrange(
                    "e p d -> p (e d)")).then_inc(q, 16)

            load_expert(0, 0)
            load_expert(1, 1)
            with sp.Fori(1, E // 2) as e2:
                for slot in range(2):
                    sp.wait_ge(S_.x_in, 16)
                    sp.wait_ge(S_.eo_mm, (2 * e2 + slot - 1) * NG * 4)
                    load_expert(2 * e2 + slot, slot)
            sp.wait_ge(S_.acc_ok, E * NT)
            sp.dma_start(out.rearrange("b (n p) d -> p (b n) d", p=P), x_sb[:]).then_inc(S_.done, 16)
            sp.wait_ge(S_.done, 16)

        @block.tensor
        def _(pe):
            pe.wait_ge(S_.c_in, 272)
            for b in range(B):
                for c in range(DC):
                    for cc in range(DC):
                        pe.matmul(ps_p[:, (b * DC + c) * KC:(b * DC + c + 1) * KC], w_x_sb[:, 1, cc, c * P:(c + 1) * P],
                                  ctx_sb[:, cc, b * KC:(b + 1) * KC], start=cc == 0, stop=cc == DC - 1)
            for b in range(B):
                for cc in range(DC):
                    mm = pe.matmul(ps_p[0:KC, HALF + b * D:HALF + (b + 1) * D], ctx_sb[:, cc, b * KC:(b + 1) * KC],
                                   w_x_sb[:, 2, cc, :], start=cc == 0, stop=cc == DC - 1)
            mm.then_inc(S_.kv_mm, 1)
            pe.wait_ge(S_.xn_ok, 1)
            for n in range(NT // 4):
                for c in range(DC):
                    k = n * DC + c
                    if k >= 4:
                        pe.wait_ge(S_.xnt_ok, k - 3)
                    dst = ps_s[:, (k % 4) // 2, (k % 2) * 512:(k % 2) * 512 + 512]
                    for i in range(4):
                        mm = pe.transpose(dst[:, i * P:(i + 1) * P], xn[:, 4 * n + i, c * P:(c + 1) * P], ident)
                    mm.then_inc(S_.tr_ok, 1)
            pe.wait_ge(S_.xnt_ok, NT // 4 * DC)
            pe.wait_ge(S_.kv_ok, 1)

            def project(g, p, par, first):
                tok = ((p >> 3) & 1) * T
                pe.wait_ge((S_.w_even, S_.w_odd)[par], 16 * (p + 1))
                if not first:
                    pe.wait_ge(S_.v_ok, g)
                for th in range(2):
                    for c in range(DC):
                        mm = pe.matmul(ps_p[:, th * HALF:(th + 1) * HALF], w_head[:, par, c, 0:P],
                                       xn_t[:, c, bass.ds(tok + th * HALF, HALF)], start=c == 0, stop=c == DC - 1)
                mm.then_inc(S_.qk_proj, 1)
                pe.wait_ge(S_.qk_ok, g + 1)
                for th in range(2):
                    for c in range(DC):
                        mm = pe.matmul(ps_p[:, th * HALF:(th + 1) * HALF], w_head[:, par, c, P:2 * P],
                                       xn_t[:, c, bass.ds(tok + th * HALF, HALF)], start=c == 0, stop=c == DC - 1)
                mm.then_inc(S_.vg_proj, 1)
                pe.wait_ge(S_.vg_ok, g + 1)
                pe.wait_ge(S_.sq_ok, g + 1)
                for th in range(2):
                    mm = pe.matmul(ps_p[64:128, th * HALF:(th + 1) * HALF], cst[:, C_SEL:C_SEL + 64],
                                   qk_sq[:, th * HALF:(th + 1) * HALF], start=True, stop=True)
                mm.then_inc(S_.norm_mm, 1)
                pe.wait_ge(S_.c_in, 272)
                pe.wait_ge(S_.norms_ok, g + 1)
                for b in range(SB):
                    mm = pe.transpose(ps_p[:, b * DH:(b + 1) * DH], vg[0:64, par, b * P:(b + 1) * P],
                                      cst[0:64, C_ID:C_ID + 64])
                mm.then_inc(S_.v_turned, 1)

            def distances(g, b, first):
                if b == 0:
                    pe.wait_ge(S_.split_ok, g + 1)
                if not first or b >= 2:
                    pe.wait_ge(S_.max_ok, 8 * g + b - 1)
                for th in range(2):
                    t = slice(th * HALF, (th + 1) * HALF)
                    pe.matmul(ps_s[:, b % 2, t], ka[:, b * P:(b + 1) * P], qa[:, t], start=True, stop=False)
                    mm = pe.matmul(ps_s[:, b % 2, t], kb[:, b * P:(b + 1) * P], qb[:, t], start=False, stop=True)
                mm.then_inc(S_.s_ready, 1)

            def values(g, par, b, first):
                if b == 0:
                    pe.wait_ge(S_.v_ok, g + 1)
                    if not first:
                        pe.wait_ge(S_.h_ok, g)
                if b % 2 == 0:
                    pe.wait_ge(S_.w_ok, 4 * g + b // 2 + 1)
                for th in range(2):
                    t = slice(th * HALF, (th + 1) * HALF)
                    mm = pe.matmul(ps_o[:, t], v_aug[:, par, b, :], wts[:, par, b, t], start=b == 0, stop=b == SB - 1)
                if b == SB - 1:
                    mm.then_inc(S_.av_done, 1)

            def head(g, p, par, n):
                project(g, p, par, n == 0)
                for b in range(SB):
                    distances(g, b, n == 0)
                    if n >= 1:
                        values(g - 1, 1 - par, b, n == 1)

            head(0, 0, 0, 0)
            head(1, 0, 1, 1)
            with pe.Fori(1, PAIRS) as p:
                head(2 * p, p, 0, 2)
                head(2 * p + 1, p, 1, 2)
            for b in range(SB):
                values(G - 1, 1, b, False)

            bank0, bank1 = ps_o[:, 0:512], ps_o[:, 512:1024]

            def attn_out(i, n):
                if n == 0:
                    pe.wait_ge(S_.h_ok, G)
                if n >= 2:
                    pe.wait_ge(S_.gl_ok, i - 1)
                pe.wait_ge(S_.ht_in, 16 * (i + 1))
                for q in range(H // 2):
                    mm = pe.matmul(bank0[:, 0:D], h_tile[:, q, :], w_o[:, q, :], start=q == 0, stop=q == H // 2 - 1)
                mm.then_inc(S_.y_mm, 1)

            def turn_p(i, k, n):
                if k == 0:
                    pe.wait_ge(S_.exp_ok, i + 1)
                if n >= 1 or k >= 2:
                    pe.wait_ge((S_.pta_ok, S_.ptd_ok)[k % 2], 2 * i + k // 2)
                for j in range(HPB):
                    mm = pe.transpose(ps_p[0:KC, (k % 2) * HALF + j * P:(k % 2) * HALF + (j + 1) * P], lg[:, HPB * k + j, :], ident)
                mm.then_inc(S_.pt_mm, 1)

            def turn_x(i, n):
                if n >= 2:
                    pe.wait_ge(S_.ytr_ok, i - 1)
                pe.wait_ge(S_.xn2_ok, i + 1)
                for c in range(DC):
                    mm = pe.transpose(bank1[:, c * P:(c + 1) * P], xn2[:, c * P:(c + 1) * P], ident)
                mm.then_inc(S_.xt_mm, 1)

            def x_values(i):
                pe.wait_ge(S_.pta_ok, 2 * i + 2)
                pe.wait_ge(S_.ptd_ok, 2 * i + 2)
                for h in range(XH):
                    mm = pe.matmul(bank0[:, h * (XD + 1):(h + 1) * (XD + 1)], p_t[:, h, :],
                                   v_x[:, bass.ds((i >> 3) & 1, 1), h, :], start=True, stop=True)
                mm.then_inc(S_.avx_mm, 1)

            def query(i):
                pe.wait_ge(S_.xnt2_ok, i + 1)
                for c in range(DC):
                    for cc in range(DC):
                        mm = pe.matmul(bank1[:, c * P:(c + 1) * P], w_x_sb[:, 0, cc, c * P:(c + 1) * P], xn2_t[:, cc, :],
                                       start=cc == 0, stop=cc == DC - 1)
                mm.then_inc(S_.q_mm, 1)

            def turn_o(i):
                pe.wait_ge(S_.o_ok, i + 1)
                for c in range(DC):
                    mm = pe.transpose(bank1[:, c * P:(c + 1) * P], o_x.rearrange("p h d -> p (h d)")[:, c * P:(c + 1) * P], ident)
                mm.then_inc(S_.ot_mm, 1)

            def logits(i, n):
                pe.wait_ge(S_.qt_ok, i + 1)
                if n >= 1:
                    pe.wait_ge(S_.l_ok, i)
                if n == 0:
                    pe.wait_ge(S_.max_ok, 8 * G)
                for j in range(XH // HPB):
                    c, h0 = j * HPB // HPC, j * HPB % HPC
                    rhs = k_blk[:, bass.ds(((i >> 3) & 1) * DC + c, 1), h0:h0 + HPB, :].rearrange("p a h k -> p (a h k)")
                    mm = pe.matmul(ps_s[:, j // 2, (j % 2) * HALF:(j % 2) * HALF + HPB * KC], q_t[:, c, :], rhs,
                                   start=True, stop=True)
                mm.then_inc(S_.lg_mm, 1)

            def x_out(i):
                pe.wait_ge(S_.ot_ok, i + 1)
                for c in range(DC):
                    mm = pe.matmul(bank0[:, 0:D], o_t[:, c, :], w_x_sb[:, 3, c, :], start=c == 0, stop=c == DC - 1)
                mm.then_inc(S_.out_mm, 1)

            def turn_y(i):
                pe.wait_ge(S_.y_ok, i + 1)
                for c in range(DC):
                    mm = pe.transpose(bank1[:, c * P:(c + 1) * P], y_n[:, c * P:(c + 1) * P], ident)
                mm.then_inc(S_.yt_mm, 1)

            def gates(i):
                pe.wait_ge(S_.yt_ok, i + 1)
                for c in range(DC):
                    mm = pe.matmul(bank0[:, 0:E], y_tile[:, c, :], gate_sb[:, c, :], start=c == 0, stop=c == DC - 1)
                mm.then_inc(S_.gl_mm, 1)

            def tile(i, n, first=True, second=True):
                if first:
                    attn_out(i, n)
                if second:
                    turn_p(i - 1, 0, n - 1)
                    turn_p(i - 1, 1, n - 1)
                if first:
                    turn_x(i, n)
                if second:
                    turn_p(i - 1, 2, n - 1)
                    turn_p(i - 1, 3, n - 1)
                    if first:
                        pe.wait_ge(S_.x1_ok, i + 1)
                    x_values(i - 1)
                if first:
                    query(i)
                if second:
                    if first:
                        pe.wait_ge(S_.qt_ok, i + 1)
                    turn_o(i - 1)
                if first:
                    logits(i, n)
                if second:
                    x_out(i - 1)
                    turn_y(i - 1)
                    gates(i - 1)

            tile(0, 0, second=False)
            tile(1, 1)
            with pe.Fori(2, NT) as i:
                tile(i, 2)
            tile(NT, 2, first=False)

            def up_gate(e, e2, slot, tg, lead):
                step = e * NG + tg
                if tg == 0:
                    pe.wait_ge((S_.e_even, S_.e_odd)[slot], 64 * (e2 + 1))
                for n in range(NC):
                    m = min(P, DE - n * P)
                    if not lead or n >= 2:
                        pe.wait_ge(S_.hm_ok, step * NC + n - 1)
                    for k in range(2):
                        dst = ps_s[0:m, k, (n % 2) * HALF:(n % 2 + 1) * HALF]
                        for c in range(DC):
                            mm = pe.matmul(dst, w12[:, slot, k, c, n * P:n * P + m], y_t[:, c, tg * TG:(tg + 1) * TG],
                                           start=c == 0, stop=c == DC - 1)
                    mm.then_inc(S_.ug_mm, 1)

            def down(step, slot, par, lead):
                pe.wait_ge(S_.hm_ok, (step + 1) * NC)
                for j in range(TG // P):
                    if not lead:
                        pe.wait_ge(S_.acc_ok, step * 4 + j - 3)
                    dst = (ps_o, ps_p)[j // 2][:, (j % 2) * HALF:(j % 2) * HALF + D]
                    for n in range(NC):
                        m = min(P, DE - n * P)
                        mm = pe.matmul(dst, h_mid[0:m, par, n, j * P:(j + 1) * P], w3_sb[0:m, slot, n, :],
                                       start=n == 0, stop=n == NC - 1)
                    mm.then_inc(S_.eo_mm, 1)

            pe.wait_ge(S_.ytr_ok, NT)
            pe.wait_ge(S_.gl_ok, NT)

            def expert_pair(e2, lead):
                for slot in range(2):
                    for tg in range(NG):
                        step = (2 * e2 + slot) * NG + tg
                        k = slot * NG + tg
                        up_gate(2 * e2 + slot, e2, slot, tg, lead and k == 0)
                        if not (lead and k == 0):
                            down(step - 1, slot if tg else 1 - slot, (k - 1) % 2, lead and k == 1)

            expert_pair(0, True)
            with pe.Fori(1, E // 2) as e2:
                expert_pair(e2, False)
            down(E * NG - 1, 1, 1, False)

        @block.vector
        def _(dve):
            dve.memset(eps_d[:], EPS_D)
            dve.memset(eps_ln[:], EPS_LN)
            dve.memset(eps_rms[:], EPS_RMS)
            dve.memset(v_x[:], 1.0)
            dve.memset(v_aug[:], 1.0).then_inc(S_.eps_ok, 1)
            dve.wait_ge(S_.x_in, 16)
            for i in range(NT):
                bn = dve.bn_stats(stats[:, i, :], x_sb[:, i, :])
            bn.then_inc(S_.stats_ok, 1)
            dve.wait_ge(S_.stats_ok, 1)
            for i in range(NT):
                bn = dve.bn_aggr(mean_var[:, i, :], stats[:, i, :])
            bn.then_inc(S_.aggr_ok, 1)
            dve.wait_ge(S_.std_ok, 1)
            dve.reciprocal(rstd[:], std[:]).then_inc(S_.rstd_ok, 1)
            dve.wait_ge(S_.rstd_ok, 1)
            for i in range(NT):
                bn = dve.tensor_scalar(xn[:, i, :], x_sb[:, i, :], mean_var[:, i, 0:1], rstd[:, i:i + 1],
                                       ALU.subtract, ALU.mult)
            bn.then_inc(S_.xn_ok, 1)
            for k in range(NT // 4 * DC):
                n, c = k // DC, k % DC
                dve.wait_ge(S_.tr_ok, k + 1)
                dve.tensor_copy(xn_t[:, c, n * 512:(n + 1) * 512],
                                ps_s[:, (k % 4) // 2, (k % 2) * 512:(k % 2) * 512 + 512]).then_inc(S_.xnt_ok, 1)
            dve.wait_ge(S_.c_in, 272)
            dve.tensor_scalar(mask_f[:].rearrange("p b k -> p (b k)"), mask_i[:], NEG, None, ALU.mult)
            dve.wait_ge(S_.kv_mm, 1)
            for b in range(B):
                for c in range(DC):
                    kk = dve.tensor_scalar(k_raw[:, b * DC + c], ps_p[:, (b * DC + c) * KC:(b * DC + c + 1) * KC],
                                           b_qk_x[:, DC + c:DC + c + 1], None, ALU.add)
            kk.then_inc(S_.k_ok, 1)
            dve.wait_ge(S_.k_ok, 1)
            for bc in range(B * DC):
                dve.tensor_tensor(k_blk[:, bc], k_raw[:, bc].unsqueeze(1).broadcast_to([P, HPC, KC]),
                                  cst[:, C_HM:C_HM + HPC].unsqueeze(2).broadcast_to([P, HPC, KC]), ALU.mult)
            for b in range(B):
                vv = dve.tensor_tensor(v_x[:, b, :, 0:XD], ps_p[0:KC, HALF + b * D:HALF + (b + 1) * D].rearrange("p (h d) -> p h d", d=XD),
                                       brow[0:KC, 1].rearrange("p (h d) -> p h d", d=XD), ALU.add)
            vv.then_inc(S_.kv_ok, 1)

            def prepare(g, p, par, n):
                first = n == 0
                hd = (p & (H // 2 - 1)) * 2 + par
                dve.wait_ge(S_.qk_proj, g + 1)
                if not first:
                    dve.wait_ge(S_.sq_ok, g)
                    dve.wait_ge(S_.s_ready, 8 * g)
                dve.tensor_scalar(qk[:], ps_p[:], b_qk[:, bass.ds(hd, 1)], cst[:, C_SCALE:C_SCALE + 1],
                                  ALU.add, ALU.mult).then_inc(S_.qk_ok, 1)
                dve.wait_ge(S_.qk_ok, g + 1)
                dve.tensor_copy(qa[0:64], qk[0:64])
                dve.tensor_copy(ka[64:128], qk[64:128]).then_inc(S_.hi_ok, 1)
                dve.tensor_copy(qb[0:64], qk[0:64])
                dve.tensor_copy(ka[0:64], qk[64:128])
                dve.wait_ge(S_.hi_ok, g + 1)
                dve.tensor_tensor(qa[64:128], qk[0:64], qa[0:64], ALU.subtract)
                dve.tensor_tensor(kb[0:64], qk[64:128], ka[64:128], ALU.subtract)
                dve.wait_ge(S_.vg_proj, g + 1)
                if n >= 2:
                    dve.wait_ge(S_.gr_ok, g - 1)
                dve.tensor_scalar(vg[:, par], ps_p[:], b_vg[:, bass.ds(hd, 1)], None, ALU.add).then_inc(S_.vg_ok, 1)
                dve.wait_ge(S_.norm_mm, g + 1)
                dve.tensor_scalar(norms[64:128], ps_p[64:128], cst[64:128, C_ONE:C_ONE + 1], None,
                                  ALU.add).then_inc(S_.norms_ok, 1)
                dve.wait_ge(S_.norms_ok, g + 1)
                dve.tensor_copy(norms_hi[64:128], norms[64:128]).then_inc(S_.norms_hi_ok, 1)
                dve.wait_ge(S_.norms_hi_ok, g + 1)
                dve.scalar_tensor_tensor(out=qb[64:96], in0=norms_hi[64:96].bitcast(F32), scalar=cst[64:96, C_LO:C_LO + 1],
                                         in1=norms[64:96], op0=ALU.mult, op1=ALU.add)
                dve.scalar_tensor_tensor(out=kb[64:96], in0=norms_hi[96:128].bitcast(F32), scalar=cst[96:128, C_LO:C_LO + 1],
                                         in1=norms[96:128], op0=ALU.mult, op1=ALU.add).then_inc(S_.split_ok, 1)
                dve.wait_ge(S_.v_turned, g + 1)
                dve.tensor_copy(v_aug[:, par, :, v_rows(par)],
                                ps_p[:, 0:SB * DH].rearrange("p (b d) -> p b d", d=DH)).then_inc(S_.v_ok, 1)

            def guard(g, par, b):
                dve.wait_ge(S_.s_ready, 8 * g + b + 1)
                dve.tensor_scalar(wts[:, par, b, :], ps_s[:, b % 2, :], 0.0, None, ALU.max).then_inc(S_.max_ok, 1)

            def gate(g, p, par, first):
                dve.wait_ge(S_.gr_ok, g + 1)
                if par == 0 and not first:
                    dve.wait_ge(S_.h_out, 16 * p)
                dve.tensor_tensor(h_pair[v_rows(par)], ps_o[v_rows(par)], g_r[64:128], ALU.mult).then_inc(S_.h_ok, 1)

            def head(g, p, par, n):
                prepare(g, p, par, n)
                if n >= 2:
                    gate(g - 2, p - 1, par, False if not isinstance(p, int) else p == 1)
                for b in range(SB):
                    guard(g, par, b)

            head(0, 0, 0, 0)
            head(1, 0, 1, 1)
            head(2, 1, 0, 2)
            head(3, 1, 1, 2)
            with dve.Fori(2, PAIRS) as p:
                head(2 * p, p, 0, 2)
                head(2 * p + 1, p, 1, 2)
            gate(G - 2, PAIRS - 1, 0, False)
            gate(G - 1, PAIRS - 1, 1, False)

            bank0, bank1 = ps_o[:, 0:512], ps_o[:, 512:1024]

            def xt(i):
                return x_sb[:, bass.ds(i, 1), :].rearrange("p a d -> p (a d)")

            def residual(i, n):
                dve.wait_ge(S_.y_mm, i + 1)
                if n == 0:
                    dve.wait_ge(S_.xb_ok, 1)
                else:
                    dve.wait_ge(S_.x1b_ok, i)
                dve.tensor_tensor(x1s[:], xt(i), bank0[:, 0:D], ALU.add).then_inc(S_.x1_ok, 1)
                dve.wait_ge(S_.x1_ok, i + 1)
                dve.bn_stats(st2[:, 0, :], x1s[:]).then_inc(S_.st_ok, 1)
                dve.wait_ge(S_.xb_ok, 1)
                if n >= 1:
                    dve.wait_ge(S_.r1_ok, i)
                dve.wait_ge(S_.st_ok, i + 1)
                dve.bn_aggr(mv2[:, 0, :], st2[:, 0, :]).then_inc(S_.mv_ok, 1)

            def probs_t(i, k, n):
                dve.wait_ge(S_.pt_mm, 4 * i + k + 1)
                if n >= 1:
                    dve.wait_ge(S_.avx_mm, i)
                dve.tensor_copy(p_t[:, HPB * k:HPB * (k + 1), :].rearrange("p h t -> p (h t)"),
                                ps_p[0:KC, HALF:2 * HALF]).then_inc(S_.ptd_ok, 1)

            def norm_x(i, n):
                dve.wait_ge(S_.r1_ok, i + 1)
                dve.wait_ge(S_.mv_ok, i + 1)
                if n >= 1:
                    dve.wait_ge(S_.xt_mm, i)
                dve.tensor_scalar(xn2, x1s[:], mv2[:, 0, 0:1], r2[:, 0:1], ALU.subtract, ALU.mult).then_inc(S_.xn2_ok, 1)

            def copy_xt(i):
                dve.wait_ge(S_.xt_mm, i + 1)
                dve.tensor_copy(xn2_t.rearrange("p c t -> p (c t)"), bank1[:, 0:D]).then_inc(S_.xnt2_ok, 1)

            def divide(i, n):
                dve.wait_ge(S_.avx_mm, i + 1)
                av = bank0[:, 0:XH * (XD + 1)].rearrange("p (h d) -> p h d", d=XD + 1)
                dve.reciprocal(den[:], av[:, :, XD]).then_inc(S_.den_ok, 1)
                dve.wait_ge(S_.den_ok, i + 1)
                dve.tensor_tensor(o_x, av[:, :, 0:XD], den[:].unsqueeze(2).broadcast_to([P, XH, XD]), ALU.mult).then_inc(S_.o_ok, 1)

            def copy_q(i):
                dve.wait_ge(S_.q_mm, i + 1)
                for c in range(DC):
                    q = dve.tensor_scalar(q_t[:, c], bank1[:, c * P:(c + 1) * P], b_qk_x[:, c:c + 1], XD ** -0.5, ALU.add, ALU.mult)
                q.then_inc(S_.qt_ok, 1)

            def copy_o(i):
                dve.wait_ge(S_.ot_mm, i + 1)
                dve.tensor_copy(o_t.rearrange("p c t -> p (c t)"), bank1[:, 0:D]).then_inc(S_.ot_ok, 1)

            def mask_max(i, n):
                dve.wait_ge(S_.lg_mm, i + 1)
                if n >= 1:
                    dve.wait_ge(S_.pt_mm, 4 * i)
                m = mask_f[:, bass.ds((i >> 3) & 1, 1), :]
                src = ps_s[:].rearrange("p a (j t) -> p (a j) t", j=2)
                for j in range(XH // HPB):
                    q = dve.tensor_tensor(lg[:, HPB * j:HPB * (j + 1), :], src[:, j, 0:HPB * KC].rearrange("p (h k) -> p h k", k=KC),
                                          m.broadcast_to([P, HPB, KC]), ALU.add)
                q.then_inc(S_.l_ok, 1)
                dve.wait_ge(S_.l_ok, i + 1)
                if n >= 1:
                    dve.wait_ge(S_.sub_ok, i)
                dve.tensor_reduce(lmax[:], lg, AX.X, ALU.max).then_inc(S_.lmax_ok, 1)

            def second_norm(i, n):
                dve.wait_ge(S_.out_mm, i + 1)
                dve.wait_ge(S_.x1b_ok, i + 1)
                if n >= 1:
                    dve.wait_ge(S_.base_ok, i)
                dve.tensor_tensor(x2s[:], xt(i), bank0[:, 0:D], ALU.add).then_inc(S_.x2_ok, 1)
                dve.wait_ge(S_.x2_ok, i + 1)
                dve.bn_stats(st2[:, 1, :], x2s[:]).then_inc(S_.st2_ok, 1)
                dve.wait_ge(S_.xb_ok, 1)
                dve.wait_ge(S_.st2_ok, i + 1)
                dve.bn_aggr(mv2[:, 1, :], st2[:, 1, :]).then_inc(S_.mv2_ok, 1)
                dve.wait_ge(S_.mv2_ok, i + 1)
                dve.wait_ge(S_.r2_ok, i + 1)
                dve.tensor_scalar(xin, x2s[:], mv2[:, 1, 0:1], r2[:, 1:2], ALU.subtract, ALU.mult).then_inc(S_.xin_ok, 1)
                dve.wait_ge(S_.xin_ok, i + 1)
                dve.wait_ge(S_.r3_ok, i + 1)
                dve.scalar_tensor_tensor(out=y_n, in0=xin, scalar=r2[:, 2:3], in1=brow[:, 3], op0=ALU.mult,
                                         op1=ALU.mult).then_inc(S_.y_ok, 1)
                dve.wait_ge(S_.yt_mm, i + 1)
                if n >= 1:
                    dve.wait_ge(S_.ytr_ok, i)
                dve.tensor_copy(y_tile.rearrange("p c t -> p (c t)"), bank1[:, 0:D]).then_inc(S_.yt_ok, 1)
                dve.wait_ge(S_.gl_mm, i + 1)
                dve.tensor_copy(gl[:, bass.ds(i, 1), :].rearrange("p a e -> p (a e)"), bank0[:, 0:E]).then_inc(S_.gl_ok, 1)

            def tile(i, n, first=True, second=True):
                if first:
                    residual(i, n)
                if second:
                    probs_t(i - 1, 1, n - 1)
                if first:
                    norm_x(i, n)
                if second:
                    probs_t(i - 1, 3, n - 1)
                if first:
                    copy_xt(i)
                if second:
                    divide(i - 1, n - 1)
                if first:
                    copy_q(i)
                if second:
                    copy_o(i - 1)
                if first:
                    mask_max(i, n)
                if second:
                    second_norm(i - 1, n - 1)

            tile(0, 0, second=False)
            tile(1, 1)
            with dve.Fori(2, NT) as i:
                tile(i, 2)
            tile(NT, 2, first=False)

            dve.wait_ge(S_.gl_ok, NT)
            for i in range(NT):
                q = dve.max(top[:, i, :], gl[:, i, :])
            q.then_inc(S_.top_ok, 1)
            dve.wait_ge(S_.top_ok, 1)
            dve.tensor_tensor(pw[:, 0], top[:, :, 1], top[:, :, 0], ALU.subtract).then_inc(S_.dlt_ok, 1)
            for i in range(NT):
                q = dve.max_index(top_i[:, i, :], top[:, i, :], gl[:, i, :])
            q.then_inc(S_.topi_ok, 1)
            dve.wait_ge(S_.topi_ok, 1)
            dve.tensor_copy(top_f[:], top_i[:, :, 0:2]).then_inc(S_.topf_ok, 1)
            dve.wait_ge(S_.pe_ok, 1)
            dve.tensor_scalar(pw[:, 2], pw[:, 1], 1.0, None, ALU.add).then_inc(S_.pw_ok, 1)
            dve.wait_ge(S_.pw_ok, 1)
            dve.reciprocal(pw[:, 3], pw[:, 2]).then_inc(S_.pw_ok, 1)
            dve.wait_ge(S_.pw_ok, 2)
            dve.tensor_tensor(pw[:, 4], pw[:, 3], pw[:, 1], ALU.mult).then_inc(S_.pw_ok, 1)
            dve.wait_ge(S_.topf_ok, 1)
            for k in range(2):
                q = dve.tensor_tensor(w_full[:, k], cst[:, C_IOTA:C_IOTA + E].unsqueeze(1).broadcast_to([P, NT, E]),
                                      top_f[:, :, k:k + 1].broadcast_to([P, NT, E]), ALU.is_equal)
            q.then_inc(S_.wf_ok, 1)
            dve.wait_ge(S_.wf_ok, 1)
            dve.wait_ge(S_.pw_ok, 3)
            for k in range(2):
                q = dve.tensor_tensor(w_full[:, k], w_full[:, k], pw[:, 3 + k].unsqueeze(2).broadcast_to([P, NT, E]), ALU.mult)
            q.then_inc(S_.wf_ok, 1)
            dve.wait_ge(S_.wf_ok, 2)
            dve.tensor_tensor(w_full[:, 0], w_full[:, 0], w_full[:, 1], ALU.add).then_inc(S_.wf_ok, 1)
            dve.wait_ge(S_.wf_ok, 3)
            dve.wait_ge(S_.base_ok, NT)

            def gated(step, slot, n, par, lead):
                m = min(P, DE - n * P)
                dve.wait_ge(S_.silu_ok, step * NC + n + 1)
                if n == 0 and not lead:
                    dve.wait_ge(S_.eo_mm, (step - 1) * 4)
                dve.tensor_tensor(h_mid[0:m, par, n, :], up_s[0:m, n % 2, :], ps_s[0:m, 1, (n % 2) * HALF:(n % 2 + 1) * HALF],
                                  ALU.mult).then_inc(S_.hm_ok, 1)

            def add_up(step, e, tg, first):
                for j in range(TG // P):
                    i = tg * (TG // P) + j
                    dve.wait_ge(S_.eo_mm, step * 4 + j + 1)
                    if not first:
                        dve.wait_ge(S_.acc_ok, step * 4 + j + 1 - NT)
                    dve.scalar_tensor_tensor(out=x_sb[:, i], in0=(ps_o, ps_p)[j // 2][:, (j % 2) * HALF:(j % 2) * HALF + D],
                                             scalar=w_full[:, 0, i, bass.ds(e, 1)], in1=x_sb[:, i], op0=ALU.mult,
                                             op1=ALU.add).then_inc(S_.acc_ok, 1)

            def expert_pair(e2, lead):
                for slot in range(2):
                    for tg in range(NG):
                        step = (2 * e2 + slot) * NG + tg
                        k = slot * NG + tg
                        for n in range(NC):
                            gated(step, slot, n, k % 2, lead and k < 2)
                        if not (lead and k == 0):
                            add_up(step - 1, 2 * e2 + slot - (tg == 0), (tg - 1) % NG, lead and k <= NG)

            expert_pair(0, True)
            with dve.Fori(1, E // 2) as e2:
                expert_pair(e2, False)
            add_up(E * NG - 1, E - 1, NG - 1, False)

        @block.scalar
        def _(act):
            act.wait_ge(S_.eps_ok, 1)
            act.wait_ge(S_.aggr_ok, 1)
            act.activation(std[:], mean_var[:, :, 1], ACT.Sqrt, bias=eps_ln[:, 0:1]).then_inc(S_.std_ok, 1)

            def chunk(par, c):
                return wts[:, par, 2 * c:2 * c + 2, :].rearrange("p b t -> p (b t)")

            def rows(g, par, first):
                act.wait_ge(S_.av_done, g + 1)
                if not first:
                    act.wait_ge(S_.gr_ok, g)
                act.activation(rinv[64:128], ps_o[rs_rows(par)], ACT.Ln, bias=eps_d[rs_rows(par), 0:1]).then_inc(S_.rln_ok, 1)
                act.wait_ge(S_.rln_ok, g + 1)
                act.activation(rinv[64:128], rinv[64:128], ACT.Exp, scale=-1.0).then_inc(S_.r_ok, 1)

            def head(g, par, n):
                for c in range(4):
                    act.wait_ge(S_.max_ok, 8 * g + 2 * c + 2)
                    act.activation(chunk(par, c), chunk(par, c), ACT.Sqrt).then_inc(S_.sqrt_ok, 1)
                act.preload_act_table_set("natural_log_exp_and_others")
                if n >= 1:
                    rows(g - 1, 1 - par, n == 1)

                def ln(c):
                    act.wait_ge(S_.sqrt_ok, 4 * g + c + 1)
                    act.activation(chunk(par, c), chunk(par, c), ACT.Ln, bias=eps_d[:, 0:1]).then_inc(S_.ln_ok, 1)

                def exp(c):
                    act.wait_ge(S_.ln_ok, 4 * g + c + 1)
                    act.activation(chunk(par, c), chunk(par, c), ACT.Exp, scale=-2.0).then_inc(S_.w_ok, 1)

                ln(0)
                for c in range(4):
                    if c < 3:
                        ln(c + 1)
                    exp(c)

            head(0, 0, 0)
            head(1, 1, 1)
            with act.Fori(1, PAIRS) as p:
                head(2 * p, 0, 2)
                head(2 * p + 1, 1, 2)
            rows(G - 1, 1, False)

            def probs_t(i, k, n):
                act.wait_ge(S_.pt_mm, 4 * i + k + 1)
                if n >= 1:
                    act.wait_ge(S_.avx_mm, i)
                act.activation(p_t[:, HPB * k:HPB * (k + 1), :].rearrange("p h t -> p (h t)"), ps_p[0:KC, 0:HALF],
                               ACT.Copy).then_inc(S_.pta_ok, 1)

            def rstd_of(i, src, dst, scale, eps, logged, ready):
                act.activation(dst, src, ACT.Ln, bias=eps[:, 0:1], scale=scale).then_inc(logged, 1)
                act.wait_ge(logged, i + 1)
                act.activation(dst, dst, ACT.Exp, scale=-0.5).then_inc(ready, 1)

            def tile(i, n, first=True, second=True):
                if second:
                    probs_t(i - 1, 0, n - 1)
                if first:
                    act.wait_ge(S_.mv_ok, i + 1)
                    if n >= 1:
                        act.wait_ge(S_.xn2_ok, i)
                    rstd_of(i, mv2[:, 0, 1:2], r2[:, 0:1], 1.0, eps_ln, S_.lr1, S_.r1_ok)
                if second:
                    probs_t(i - 1, 2, n - 1)
                    act.wait_ge(S_.mv2_ok, i)
                    if n >= 2:
                        act.wait_ge(S_.xin_ok, i - 1)
                    rstd_of(i - 1, mv2[:, 1, 1:2], r2[:, 1:2], 1.0, eps_ln, S_.lr2, S_.r2_ok)
                if first:
                    act.wait_ge(S_.sub_ok, i + 1)
                    act.activation(lg, lg, ACT.Exp).then_inc(S_.exp_ok, 1)
                if second:
                    act.wait_ge(S_.xin_ok, i)
                    if n >= 2:
                        act.wait_ge(S_.y_ok, i - 1)
                    act.activation(sq_junk, xin, ACT.Square, accum_out=r2[:, 3:4]).then_inc(S_.ms_ok, 1)
                    act.wait_ge(S_.ms_ok, i)
                    rstd_of(i - 1, r2[:, 3:4], r2[:, 2:3], 1.0 / D, eps_rms, S_.lr3, S_.r3_ok)

            tile(0, 0, second=False)
            tile(1, 1)
            with act.Fori(2, NT) as i:
                tile(i, 2)
            tile(NT, 2, first=False)

            act.wait_ge(S_.dlt_ok, 1)
            act.activation(pw[:, 1], pw[:, 0], ACT.Exp).then_inc(S_.pe_ok, 1)

            def expert_pair(e2, lead):
                for k in range(2 * NG):
                    for n in range(NC):
                        idx = (2 * e2 * NG + k) * NC + n
                        m = min(P, DE - n * P)
                        act.wait_ge(S_.ug_mm, idx + 1)
                        if not (lead and k == 0 and n < 2):
                            act.wait_ge(S_.hm_ok, idx - 1)
                        act.activation(up_s[0:m, n % 2, :], ps_s[0:m, 0, (n % 2) * HALF:(n % 2 + 1) * HALF],
                                       ACT.Silu).then_inc(S_.silu_ok, 1)

            expert_pair(0, True)
            with act.Fori(1, E // 2) as e2:
                expert_pair(e2, False)

        @block.gpsimd
        def _(pool):
            def squares(g, first, gated=True):
                pool.wait_ge(S_.qk_ok, g + 1)
                if not first:
                    pool.wait_ge(S_.norm_mm, g)
                if gated:
                    pool.wait_ge(S_.gr_ok, g - 2)
                pool.tensor_tensor(qk_sq[:], qk[:], qk[:], ALU.mult).then_inc(S_.sq_ok, 1)

            def gate_rows(g, par, first, after):
                pool.wait_ge(S_.r_ok, g + 1)
                pool.wait_ge(S_.sq_ok, after)
                if not first:
                    pool.wait_ge(S_.h_ok, g)
                pool.tensor_tensor(g_r[64:128], vg[64:128, par], rinv[64:128], ALU.mult).then_inc(S_.gr_ok, 1)

            pool.wait_ge(S_.xn_ok, 1)
            pool.wait_ge(S_.c_in, 272)
            pool.tensor_tensor(x_sb[:], x_sb[:], brow[:, 0:1].broadcast_to([P, NT, D]), ALU.add).then_inc(S_.xb_ok, 1)
            squares(0, True, gated=False)
            squares(1, False, gated=False)
            squares(2, False, gated=False)
            gate_rows(0, 0, True, 3)
            squares(3, False)
            gate_rows(1, 1, False, 4)
            with pool.Fori(2, PAIRS) as p:
                for par in range(2):
                    squares(2 * p + par, False)
                    gate_rows(2 * p + par - 2, par, False, 2 * p + par + 1)
            gate_rows(G - 2, 0, False, G)
            gate_rows(G - 1, 1, False, G)

            def tile(i, n, first=True, second=True):
                if first:
                    x1 = x_sb[:, bass.ds(i, 1), :].rearrange("p a d -> p (a d)")
                    pool.wait_ge(S_.xn2_ok, i + 1)
                    pool.tensor_tensor(x1, x1s[:], brow[:, 2], ALU.add).then_inc(S_.x1b_ok, 1)
                    pool.wait_ge(S_.lmax_ok, i + 1)
                    pool.tensor_tensor(lg, lg, lmax[:].unsqueeze(2).broadcast_to([P, XH, KC]), ALU.subtract).then_inc(S_.sub_ok, 1)
                if second:
                    x2 = x_sb[:, bass.ds(i - 1, 1), :].rearrange("p a d -> p (a d)")
                    pool.wait_ge(S_.xin_ok, i)
                    pool.tensor_tensor(x2, x2s[:], xin, ALU.add).then_inc(S_.base_ok, 1)
                    pool.wait_ge(S_.yt_ok, i)
                    pool.tensor_copy(y_t[:, :, bass.ds((i - 1) * P, P)], y_tile).then_inc(S_.ytr_ok, 1)

            tile(0, 0, second=False)
            tile(1, 1)
            with pool.Fori(2, NT) as i:
                tile(i, 2)
            tile(NT, 2, first=False)


def kernel(x, ctx_1024, mask_BxS2_ik0, L0_attn_W_in, L0_attn_b_in, L0_attn_W_out, L0_attn_b_out,
           L0_xattn_Wq, L0_xattn_bq, L0_xattn_Wk, L0_xattn_bk, L0_xattn_Wv, L0_xattn_bv, L0_xattn_Wo, L0_xattn_bo,
           L0_ffn_gate_w, L0_ffn_rms_w, L0_ffn_W1, L0_ffn_W2, L0_ffn_W3):
    import numpy as np
    import concourse.bacc as bacc
    from concourse.bass_utils import run_bass_kernel_spmd

    a = np.asarray
    laid_out = {
        "x": a(x),
        "ctx_t": a(ctx_1024).transpose(2, 0, 1).reshape(D, B * KC),
        "mask": a(mask_BxS2_ik0).reshape(1, B * KC),
        "w_in": a(L0_attn_W_in),
        "b_in": a(L0_attn_b_in).reshape(H, 2, P).transpose(1, 2, 0),
        "w_out": a(L0_attn_W_out),
        "w_x": np.stack([a(w).T for w in (L0_xattn_Wq, L0_xattn_Wk, L0_xattn_Wv, L0_xattn_Wo)]),
        "b_cols": np.concatenate([a(b).reshape(DC, P).T for b in (L0_xattn_bq, L0_xattn_bk)], axis=1),
        "rows_in": np.stack([a(b) for b in (L0_attn_b_out, L0_xattn_bv, L0_xattn_bo, L0_ffn_rms_w)]),
        "gate_w": a(L0_ffn_gate_w).T,
        "w1": a(L0_ffn_W1).transpose(0, 2, 1),
        "w2": a(L0_ffn_W2).transpose(0, 2, 1),
        "w3": a(L0_ffn_W3).transpose(0, 2, 1),
        "consts": constants(np),
    }
    nc = bacc.Bacc("TRN2", target_bir_lowering=False, num_devices=1)
    laid_out = {n: np.ascontiguousarray(v) for n, v in laid_out.items()}
    args = [nc.dram_tensor(f"in_{n}", v.shape, mybir.dt.from_np(v.dtype), kind="ExternalInput").ap() for n, v in laid_out.items()]
    out = nc.dram_tensor("out_y", (B, T, D), F32, kind="ExternalOutput").ap()
    program(nc, *args, out)
    r = run_bass_kernel_spmd(nc, [{f"in_{n}": v for n, v in laid_out.items()}], core_ids=[0])
    return r.results[0]["out_y"]
```

```python
from contextlib import ExitStack

import concourse.bass as bass
from concourse import mybir

ALU = mybir.AluOpType
ACT = mybir.ActivationFunctionType
AX = mybir.AxisListType
F32 = mybir.dt.float32
F32R = mybir.dt.float32r
U32 = mybir.dt.uint32

P = 128
B, T, D = 2, 1024, 256
H, DH = 16, 64
DC = D // P
NT = B * T // P
SB = T // P
HALF = T // 2
G = B * H
PAIRS = G // 2
EPS_D, EPS_LN, EPS_RMS = 1e-4, 1e-5, 1e-6
XH, XD = 16, D // 16
KC = 77
HPB = 4
HPC = XH // DC
E, DE = 8, 704
NC = -(-DE // P)
DEH = DE // 2
ET = 2 * NT + E
NEG = -1e9

C_ID, C_SEL, C_SCALE, C_ONE, C_LO, C_HM, C_IOTA, C_W = 0, 128, 192, 193, 194, 195, 203, 211
R_TRI, R_ONES, R_POS, R_TILE, R_STEP, R_EXCL, R_SIGN, R_TOK = 0, P, 2 * P, 3 * P, 3 * P + ET, 3 * P + ET + NT, 3 * P + ET + NT + 9 * E, 3 * P + ET + NT + 10 * E
R_W = R_TOK + NT


def constants(np):
    c = np.zeros((P, C_W), np.float32)
    c[:, C_ID:C_ID + P] = np.eye(P)
    c[0:64, C_SEL:C_SEL + 2] = 0.25
    c[64:128, C_SEL + 34:C_SEL + 36] = 1.0
    c[0:64, C_SCALE] = -2.0
    c[64:128, C_SCALE] = 1.0
    c[[66, 67, 96, 97], C_ONE] = 1.0
    c[[65, 99], C_LO] = -1.0
    c[np.arange(P), C_HM + np.arange(P) // XD] = 1.0
    c[:, C_IOTA:C_IOTA + E] = np.arange(E)
    return c


def router_constants(np):
    c = np.zeros((P, R_W), np.float32)
    c[:, R_TRI:R_TRI + P] = np.triu(np.ones((P, P)), 1)
    c[:, R_ONES:R_ONES + P] = 1.0
    c[:, R_POS:R_POS + P] = np.arange(P)
    c[:, R_TILE:R_TILE + ET] = np.arange(ET)
    c[:, R_STEP:R_STEP + NT] = np.arange(NT) * P
    c[:, R_STEP] = -1.0
    c[:, R_EXCL:R_EXCL + 9 * E] = np.tril(np.ones((9, E)), -1).reshape(-1)
    c[:, R_SIGN:R_SIGN + E - 1] = [(-1) ** k for k in range(E - 1)]
    c[:, R_TOK:R_TOK + NT] = np.arange(P)[:, None] + P * np.arange(NT)
    return c


def program(nc, x, ctx_t, mask, w_in, b_in, w_out, w_x, b_cols, rows_in, gate_w, w1, w2, w3, consts, r_consts, out):
    with ExitStack() as ctx:
        def sb(name, shape, dt=F32):
            return ctx.enter_context(nc.sbuf_tensor(name, shape, dt))

        def psum(name, shape, dt=F32):
            return ctx.enter_context(nc.psum_tensor(name, shape, dt))

        def sem(name):
            return ctx.enter_context(nc.semaphore(name))

        ps_s = psum("ps_s", [P, 2, T])
        ps_o = psum("ps_o", [P, T])
        ps_p = psum("ps_p", [P, T])

        h_t = nc.dram_tensor("h_t", [PAIRS, P, T], F32, kind="Internal").ap()
        y_rows = nc.dram_tensor("y_rows", [NT * P, D], F32, kind="Internal").ap()
        o_rows = nc.dram_tensor("o_rows", [ET * P, D], F32, kind="Internal").ap()

        cst = sb("cst", [P, C_W])
        x_sb = sb("x_sb", [P, NT, D])
        xn_t = sb("xn_t", [P, DC, B * T])
        stats = sb("stats", [P, NT, 6])
        mean_var = sb("mean_var", [P, NT, 2])
        std = sb("std", [P, NT])
        rstd = sb("rstd", [P, NT])
        w_head = sb("w_head", [P, 2, DC, 4 * DH])
        b_qk = sb("b_qk", [P, H])
        b_vg = sb("b_vg", [P, H])
        qk = sb("qk", [P, T])
        qk_sq = sb("qk_sq", [P, T])
        qa = sb("qa", [P, T], F32R)
        ka = sb("ka", [P, T], F32R)
        qb = sb("qb", [96, T], F32R)
        kb = sb("kb", [96, T], F32R)
        norms = sb("norms", [P, T])
        norms_hi = sb("norms_hi", [P, T], F32R)
        vg = sb("vg", [P, 2, T])
        v_aug = sb("v_aug", [P, 2, SB, P])
        wts = sb("wts", [P, 2, SB, T])
        rinv = sb("rinv", [P, T])
        g_r = sb("g_r", [P, T])
        h_pair = sb("h_pair", [P, T])
        eps_d = sb("eps_d", [P, 1])
        eps_ln = sb("eps_ln", [P, 1])

        w_o = sb("w_o", [P, H // 2, D])
        w_x_sb = sb("w_x_sb", [P, 4, DC, D])
        ctx_sb = sb("ctx_sb", [P, DC, B * KC])
        b_qk_x = sb("b_qk_x", [P, 2 * DC])
        brow = sb("brow", [P, 4, D])
        mask_i = sb("mask_i", [P, B * KC], mybir.dt.int32)
        mask_f = sb("mask_f", [P, B, KC])
        k_raw = sb("k_raw", [P, B * DC, KC])
        k_blk = sb("k_blk", [P, B * DC, HPC, KC])
        v_x = sb("v_x", [KC, B, XH, XD + 1])
        gate_sb = sb("gate_sb", [P, DC, E])
        h_tile = qk[:].rearrange("p (q t) -> p q t", t=P)
        x1s = sb("x1s", [P, D])
        x2s = sb("x2s", [P, D])
        st2 = sb("st2", [P, 2, 6])
        mv2 = sb("mv2", [P, 2, 2])
        r2 = sb("r2", [P, 4])
        xn2 = norms[:, 0:D]
        xn2_t = norms[:, D:2 * D].rearrange("p (c t) -> p c t", t=P)
        q_t = norms[:, 2 * D:3 * D].rearrange("p (c t) -> p c t", t=P)
        o_x = norms[:, 3 * D:4 * D].rearrange("p (h d) -> p h d", d=XD)
        lg = v_aug[:].rearrange("p a b t -> p (a b t)")[:, 0:XH * KC].rearrange("p (h k) -> p h k", k=KC)
        lmax = sb("lmax", [P, XH])
        p_t = vg[0:KC].rearrange("p a t -> p (a t)").rearrange("p (h t) -> p h t", t=P)
        den = sb("den", [P, XH])
        o_t = qk_sq[:, 0:D].rearrange("p (c t) -> p c t", t=P)
        xin = qk_sq[:, D:2 * D]
        sq_junk = qk_sq[:, 2 * D:3 * D]
        y_n = qk_sq[:, 3 * D:4 * D]
        y_tile = rinv[:, 0:D].rearrange("p (c t) -> p c t", t=P)
        gl = sb("gl", [P, NT, E])
        top = sb("top", [P, NT, 8])
        top_i = sb("top_i", [P, NT, 8], U32)
        top_f = sb("top_f", [P, NT, 2])
        pw = sb("pw", [P, 5, NT])
        w_full = sb("w_full", [P, 2, NT, E])
        eps_rms = sb("eps_rms", [P, 1])
        room = wts[:].rearrange("p a b t -> p (a b t)")
        room_at = [0]

        def take(n):
            room_at[0] += n
            return room[:, room_at[0] - n:room_at[0]]

        W12, W3 = 2 * DC * DE, NC * D
        w12 = take(2 * W12).rearrange("p (s k c n) -> p s k c n", s=2, k=2, c=DC)
        w3_sb = take(2 * W3).rearrange("p (s n d) -> p s n d", s=2, n=NC)
        w_end = room_at[0]
        y_in = take(2 * D).rearrange("p (s d) -> p s d", s=2)
        y_tt = take(2 * D).rearrange("p (s c t) -> p s c t", s=2, c=DC)
        s_up = take(DE)
        h_sb = take(2 * DE).rearrange("p (s n) -> p s n", s=2)
        h_tt = take(2 * NC * P).rearrange("p (s n t) -> p s n t", s=2, n=NC)
        o_sb = take(2 * D).rearrange("p (s d) -> p s d", s=2)
        room_at[0] = w_end
        oh_lo = take(2 * NT * P).rearrange("p (r s) -> p r s", s=P)
        oh_hi = take(2 * NT * ET).rearrange("p (r e) -> p r e", e=ET)
        rc = take(R_W)
        a17 = take((NT + 1) * E).rearrange("p (n e) -> p n e", e=E)
        over = take(E * NT).rearrange("p (e n) -> p e n", e=E)
        nt_e = take(E)
        ex_t = take(9 * E).rearrange("p (k e) -> p k e", e=E)
        starts = take(9)
        st128 = take(E)
        past = take(ET * (E - 1)).rearrange("p (i e) -> p i e", e=E - 1)
        tab_f = take(2 * ET + 9)
        base = take(NT * E).rearrange("p (n e) -> p n e", e=E)
        pick = take(NT * E).rearrange("p (n e) -> p n e", e=E)
        slot_f = take(2 * NT)
        hl_f = take(4 * NT)
        o_tok = room[:, 0:2 * NT * D].rearrange("p (k n d) -> p k n d", k=2, n=NT)
        tab_i = sb("tab_i", [P, 2 * ET + 9], mybir.dt.int32)
        slot_i = sb("slot_i", [P, 2 * NT], U32)
        hl_i = sb("hl_i", [P, 4 * NT], U32)
        tok_i = sb("tok_i", [P, ET], U32)
        tok_now = sb("tok_now", [P, 2], U32)

        names = ("x_in", "c_in", "stats_ok", "aggr_ok", "std_ok", "rstd_ok", "xn_ok", "tr_ok", "xnt_ok",
                 "w_even", "w_odd", "qk_proj", "vg_proj", "norm_mm", "v_turned", "s_ready", "av_done",
                 "qk_ok", "hi_ok", "vg_ok", "norms_ok", "norms_hi_ok", "split_ok", "v_ok", "max_ok", "h_ok",
                 "sq_ok", "gr_ok", "sqrt_ok", "ln_ok", "w_ok", "rln_ok", "r_ok", "h_out", "eps_ok",
                 "kv_mm", "k_ok", "kv_ok", "mask_ok", "xb_ok",
                 "ht_in", "y_mm", "pt_mm", "xt_mm", "avx_mm", "q_mm", "ot_mm", "lg_mm", "out_mm", "yt_mm", "gl_mm",
                 "x1_ok", "st_ok", "mv_ok", "xn2_ok", "xnt2_ok", "ptd_ok", "den_ok", "o_ok", "qt_ok", "ot_ok", "l_ok",
                 "lmax_ok", "x2_ok", "st2_ok", "mv2_ok", "xin_ok", "y_ok", "yt_ok", "gl_ok", "yr_out",
                 "pta_ok", "lr1", "r1_ok", "lr2", "r2_ok", "ms_ok", "lr3", "r3_ok", "exp_ok",
                 "x1b_ok", "sub_ok", "base_ok", "top_ok", "topi_ok", "topf_ok", "dlt_ok", "pe_ok", "pw_ok", "wf_ok",
                 "rc_in", "oh_ok", "a_ok", "rank_mm", "rt_ok", "tab_ok", "slot_ok", "hl_ok", "oh2_ok", "tok_mm", "tok_ok",
                 "e_in", "now_first", "now_even", "now_odd", "yg_even", "yg_odd", "yt2_mm", "ytt_ok", "ug_mm", "silu_ok", "hm_ok", "th_a", "th_b",
                 "hta_ok", "htd_ok", "w3_mm", "o_ok2", "os_even", "os_odd", "og0", "og1", "og2", "og3", "acc_ok", "sum_ok", "done")
        s = {n: sem(n) for n in names}
        S_ = type("Sems", (), s)

        ident = cst[:, C_ID:C_ID + P]
        xn = wts[:, 0, 0:4, :].rearrange("p a (b d) -> p (a b) d", d=D)

        block = ctx.enter_context(nc.Block())

        def rs_rows(par):
            return slice(64, 128) if par == 0 else slice(0, 64)

        def v_rows(par):
            return slice(0, 64) if par == 0 else slice(64, 128)

        @block.sync
        def _(sp):
            sp.dma_start(x_sb[:], x.rearrange("b (n p) d -> p (b n) d", p=P)).then_inc(S_.x_in, 16)
            sp.dma_start(cst[:], consts).then_inc(S_.c_in, 16)
            sp.dma_start(b_qk[:], b_in[0]).then_inc(S_.c_in, 16)
            sp.dma_start(b_vg[:], b_in[1]).then_inc(S_.c_in, 16)
            for c in range(DC):
                sp.dma_start(ctx_sb[:, c], ctx_t[c * P:(c + 1) * P]).then_inc(S_.c_in, 16)
            for k in range(4):
                sp.dma_start(w_x_sb[:, k], w_x[k].rearrange("(c p) n -> p c n", p=P)).then_inc(S_.c_in, 16)
            sp.dma_start(b_qk_x[:], b_cols).then_inc(S_.c_in, 16)
            for k in range(4):
                sp.dma_start(brow[:, k], rows_in[k:k + 1].partition_broadcast(P)).then_inc(S_.c_in, 16)
            sp.dma_start(mask_i[:], mask.partition_broadcast(P)).then_inc(S_.c_in, 16)
            sp.dma_start(gate_sb[:], gate_w.rearrange("(c p) e -> p c e", p=P)).then_inc(S_.c_in, 16)
            sp.dma_start(w_o[:], w_out.rearrange("(q p) n -> p q n", p=P)).then_inc(S_.c_in, 16)

            def load_head(col, par):
                src = w_in.rearrange("(c p) n -> p c n", p=P)[:, :, bass.ds(col, 4 * DH)]
                sp.dma_start(w_head[:, par], src).then_inc((S_.w_even, S_.w_odd)[par], 16)

            def store_pair(p):
                sp.wait_ge(S_.x_in, 16)
                sp.wait_ge(S_.h_ok, 2 * p + 2)
                sp.dma_start(h_t[bass.ds(p, 1)].rearrange("a p t -> p (a t)"), h_pair[:]).then_inc(S_.h_out, 16)

            load_head(0, 0)
            load_head(4 * DH, 1)
            for b in range(B):
                p0 = b * H // 2
                with sp.Fori(max(p0, 1), p0 + H // 2) as p:
                    for par in range(2):
                        sp.wait_ge(S_.vg_proj, 2 * p + par - 1)
                        load_head(((p - p0) * 2 + par) * 4 * DH, par)
                    store_pair(p - 1)
            store_pair(PAIRS - 1)
            sp.wait_ge(S_.h_out, 16 * PAIRS)

            def load_tile(i):
                src = h_t.rearrange("(b q) p t -> b p q t", b=B)[bass.ds((i >> 3) & 1, 1), :, :, bass.ds((i & 7) * P, P)]
                sp.dma_start(h_tile, src.rearrange("b p q t -> p (b q) t")).then_inc(S_.ht_in, 16)

            def store_rows(i):
                sp.wait_ge(S_.x_in, 16)
                sp.wait_ge(S_.y_ok, i + 1)
                sp.dma_start(y_rows[bass.ds(i * P, P)], y_n).then_inc(S_.yr_out, 16)

            def load_expert(e, slot):
                for k, w in enumerate((w1, w2)):
                    sp.dma_start(w12[:, slot, k], w[bass.ds(e, 1)].rearrange("e (c p) n -> p (e c) n", p=P)).then_inc(S_.e_in, 16)
                sp.dma_start(w3_sb[:, slot, 0:NC - 1], w3[bass.ds(e, 1), 0:(NC - 1) * P].rearrange(
                    "e (n p) d -> p (e n) d", p=P)).then_inc(S_.e_in, 16)
                sp.dma_start(w3_sb[0:DE - (NC - 1) * P, slot, NC - 1], w3[bass.ds(e, 1), (NC - 1) * P:DE].rearrange(
                    "e p d -> p (e d)")).then_inc(S_.e_in, 16)

            load_tile(0)
            sp.wait_ge(S_.av_done, G)
            sp.dma_start(rc, r_consts).then_inc(S_.rc_in, 16)
            load_expert(0, 0)
            sp.wait_ge(S_.e_in, 64)
            load_expert(1, 1)
            sp.wait_ge(S_.y_mm, 1)
            load_tile(1)
            with sp.Fori(2, NT) as i:
                sp.wait_ge(S_.x_in, 16)
                sp.wait_ge(S_.y_mm, i)
                load_tile(i)
                store_rows(i - 2)
            store_rows(NT - 2)
            store_rows(NT - 1)

            sp.wait_ge(S_.tab_ok, 1)
            with sp.Fori(1, E // 2) as e2:
                for slot in range(2):
                    used = sp.value_load(tab_i[0:1, bass.ds(2 * ET + 2 * e2 + slot - 1, 1)], min_val=1, max_val=ET)
                    sp.wait_ge(S_.x_in, 16)
                    sp.wait_ge(S_.e_in, 64 * (2 * e2 + slot))
                    sp.wait_ge(S_.w3_mm, used)
                    load_expert(2 * e2 + slot, slot)
            for k in range(4):
                t = slice(k * NT // 4, (k + 1) * NT // 4)
                sp.wait_ge(S_.acc_ok, k + 1)
                sp.dma_start(out.rearrange("b (n p) d -> p (b n) d", p=P)[:, t], x_sb[:, t]).then_inc(S_.done, 16)
            sp.wait_ge(S_.done, 64)

        @block.tensor
        def _(pe):
            pe.wait_ge(S_.c_in, 272)
            for b in range(B):
                for c in range(DC):
                    for cc in range(DC):
                        pe.matmul(ps_p[:, (b * DC + c) * KC:(b * DC + c + 1) * KC], w_x_sb[:, 1, cc, c * P:(c + 1) * P],
                                  ctx_sb[:, cc, b * KC:(b + 1) * KC], start=cc == 0, stop=cc == DC - 1)
            for b in range(B):
                for cc in range(DC):
                    mm = pe.matmul(ps_p[0:KC, HALF + b * D:HALF + (b + 1) * D], ctx_sb[:, cc, b * KC:(b + 1) * KC],
                                   w_x_sb[:, 2, cc, :], start=cc == 0, stop=cc == DC - 1)
            mm.then_inc(S_.kv_mm, 1)
            pe.wait_ge(S_.xn_ok, 1)
            for n in range(NT // 4):
                for c in range(DC):
                    k = n * DC + c
                    if k >= 4:
                        pe.wait_ge(S_.xnt_ok, k - 3)
                    dst = ps_s[:, (k % 4) // 2, (k % 2) * 512:(k % 2) * 512 + 512]
                    for i in range(4):
                        mm = pe.transpose(dst[:, i * P:(i + 1) * P], xn[:, 4 * n + i, c * P:(c + 1) * P], ident)
                    mm.then_inc(S_.tr_ok, 1)
            pe.wait_ge(S_.xnt_ok, NT // 4 * DC)
            pe.wait_ge(S_.kv_ok, 1)

            def project(g, p, par, first):
                tok = ((p >> 3) & 1) * T
                pe.wait_ge((S_.w_even, S_.w_odd)[par], 16 * (p + 1))
                if not first:
                    pe.wait_ge(S_.v_ok, g)
                for th in range(2):
                    for c in range(DC):
                        mm = pe.matmul(ps_p[:, th * HALF:(th + 1) * HALF], w_head[:, par, c, 0:P],
                                       xn_t[:, c, bass.ds(tok + th * HALF, HALF)], start=c == 0, stop=c == DC - 1)
                mm.then_inc(S_.qk_proj, 1)
                pe.wait_ge(S_.qk_ok, g + 1)
                for th in range(2):
                    for c in range(DC):
                        mm = pe.matmul(ps_p[:, th * HALF:(th + 1) * HALF], w_head[:, par, c, P:2 * P],
                                       xn_t[:, c, bass.ds(tok + th * HALF, HALF)], start=c == 0, stop=c == DC - 1)
                mm.then_inc(S_.vg_proj, 1)
                pe.wait_ge(S_.vg_ok, g + 1)
                pe.wait_ge(S_.sq_ok, g + 1)
                for th in range(2):
                    mm = pe.matmul(ps_p[64:128, th * HALF:(th + 1) * HALF], cst[:, C_SEL:C_SEL + 64],
                                   qk_sq[:, th * HALF:(th + 1) * HALF], start=True, stop=True)
                mm.then_inc(S_.norm_mm, 1)
                pe.wait_ge(S_.c_in, 272)
                pe.wait_ge(S_.norms_ok, g + 1)
                for b in range(SB):
                    mm = pe.transpose(ps_p[:, b * DH:(b + 1) * DH], vg[0:64, par, b * P:(b + 1) * P],
                                      cst[0:64, C_ID:C_ID + 64])
                mm.then_inc(S_.v_turned, 1)

            def distances(g, b, first):
                if b == 0:
                    pe.wait_ge(S_.split_ok, g + 1)
                if not first or b >= 2:
                    pe.wait_ge(S_.max_ok, 8 * g + b - 1)
                for th in range(2):
                    t = slice(th * HALF, (th + 1) * HALF)
                    pe.matmul(ps_s[:, b % 2, t], ka[:, b * P:(b + 1) * P], qa[:, t], start=True, stop=False)
                    mm = pe.matmul(ps_s[:, b % 2, t], kb[:, b * P:(b + 1) * P], qb[:, t], start=False, stop=True)
                mm.then_inc(S_.s_ready, 1)

            def values(g, par, b, first):
                if b == 0:
                    pe.wait_ge(S_.v_ok, g + 1)
                    if not first:
                        pe.wait_ge(S_.h_ok, g)
                if b % 2 == 0:
                    pe.wait_ge(S_.w_ok, 4 * g + b // 2 + 1)
                for th in range(2):
                    t = slice(th * HALF, (th + 1) * HALF)
                    mm = pe.matmul(ps_o[:, t], v_aug[:, par, b, :], wts[:, par, b, t], start=b == 0, stop=b == SB - 1)
                if b == SB - 1:
                    mm.then_inc(S_.av_done, 1)

            def head(g, p, par, n):
                project(g, p, par, n == 0)
                for b in range(SB):
                    distances(g, b, n == 0)
                    if n >= 1:
                        values(g - 1, 1 - par, b, n == 1)

            head(0, 0, 0, 0)
            head(1, 0, 1, 1)
            with pe.Fori(1, PAIRS) as p:
                head(2 * p, p, 0, 2)
                head(2 * p + 1, p, 1, 2)
            for b in range(SB):
                values(G - 1, 1, b, False)

            bank0, bank1 = ps_o[:, 0:512], ps_o[:, 512:1024]

            def attn_out(i, n):
                if n == 0:
                    pe.wait_ge(S_.h_ok, G)
                if n >= 2:
                    pe.wait_ge(S_.gl_ok, i - 1)
                pe.wait_ge(S_.ht_in, 16 * (i + 1))
                for q in range(H // 2):
                    mm = pe.matmul(bank0[:, 0:D], h_tile[:, q, :], w_o[:, q, :], start=q == 0, stop=q == H // 2 - 1)
                mm.then_inc(S_.y_mm, 1)

            def turn_p(i, k, n):
                if k == 0:
                    pe.wait_ge(S_.exp_ok, i + 1)
                if n >= 1 or k >= 2:
                    pe.wait_ge((S_.pta_ok, S_.ptd_ok)[k % 2], 2 * i + k // 2)
                for j in range(HPB):
                    mm = pe.transpose(ps_p[0:KC, (k % 2) * HALF + j * P:(k % 2) * HALF + (j + 1) * P], lg[:, HPB * k + j, :], ident)
                mm.then_inc(S_.pt_mm, 1)

            def turn_x(i, n):
                if n >= 2:
                    pe.wait_ge(S_.yt_ok, i - 1)
                pe.wait_ge(S_.xn2_ok, i + 1)
                for c in range(DC):
                    mm = pe.transpose(bank1[:, c * P:(c + 1) * P], xn2[:, c * P:(c + 1) * P], ident)
                mm.then_inc(S_.xt_mm, 1)

            def x_values(i):
                pe.wait_ge(S_.pta_ok, 2 * i + 2)
                pe.wait_ge(S_.ptd_ok, 2 * i + 2)
                for h in range(XH):
                    mm = pe.matmul(bank0[:, h * (XD + 1):(h + 1) * (XD + 1)], p_t[:, h, :],
                                   v_x[:, bass.ds((i >> 3) & 1, 1), h, :], start=True, stop=True)
                mm.then_inc(S_.avx_mm, 1)

            def query(i):
                pe.wait_ge(S_.xnt2_ok, i + 1)
                for c in range(DC):
                    for cc in range(DC):
                        mm = pe.matmul(bank1[:, c * P:(c + 1) * P], w_x_sb[:, 0, cc, c * P:(c + 1) * P], xn2_t[:, cc, :],
                                       start=cc == 0, stop=cc == DC - 1)
                mm.then_inc(S_.q_mm, 1)

            def turn_o(i):
                pe.wait_ge(S_.o_ok, i + 1)
                for c in range(DC):
                    mm = pe.transpose(bank1[:, c * P:(c + 1) * P], o_x.rearrange("p h d -> p (h d)")[:, c * P:(c + 1) * P], ident)
                mm.then_inc(S_.ot_mm, 1)

            def logits(i, n):
                pe.wait_ge(S_.qt_ok, i + 1)
                if n >= 1:
                    pe.wait_ge(S_.l_ok, i)
                if n == 0:
                    pe.wait_ge(S_.max_ok, 8 * G)
                for j in range(XH // HPB):
                    c, h0 = j * HPB // HPC, j * HPB % HPC
                    rhs = k_blk[:, bass.ds(((i >> 3) & 1) * DC + c, 1), h0:h0 + HPB, :].rearrange("p a h k -> p (a h k)")
                    mm = pe.matmul(ps_s[:, j // 2, (j % 2) * HALF:(j % 2) * HALF + HPB * KC], q_t[:, c, :], rhs,
                                   start=True, stop=True)
                mm.then_inc(S_.lg_mm, 1)

            def x_out(i):
                pe.wait_ge(S_.ot_ok, i + 1)
                for c in range(DC):
                    mm = pe.matmul(bank0[:, 0:D], o_t[:, c, :], w_x_sb[:, 3, c, :], start=c == 0, stop=c == DC - 1)
                mm.then_inc(S_.out_mm, 1)

            def turn_y(i):
                pe.wait_ge(S_.y_ok, i + 1)
                for c in range(DC):
                    mm = pe.transpose(bank1[:, c * P:(c + 1) * P], y_n[:, c * P:(c + 1) * P], ident)
                mm.then_inc(S_.yt_mm, 1)

            def gates(i):
                pe.wait_ge(S_.yt_ok, i + 1)
                for c in range(DC):
                    mm = pe.matmul(bank0[:, 0:E], y_tile[:, c, :], gate_sb[:, c, :], start=c == 0, stop=c == DC - 1)
                mm.then_inc(S_.gl_mm, 1)

            def tile(i, n, first=True, second=True):
                if first:
                    attn_out(i, n)
                if second:
                    turn_p(i - 1, 0, n - 1)
                    turn_p(i - 1, 1, n - 1)
                if first:
                    turn_x(i, n)
                if second:
                    turn_p(i - 1, 2, n - 1)
                    turn_p(i - 1, 3, n - 1)
                    if first:
                        pe.wait_ge(S_.x1_ok, i + 1)
                    x_values(i - 1)
                if first:
                    query(i)
                if second:
                    if first:
                        pe.wait_ge(S_.qt_ok, i + 1)
                    turn_o(i - 1)
                if first:
                    logits(i, n)
                if second:
                    x_out(i - 1)
                    turn_y(i - 1)
                    gates(i - 1)

            tile(0, 0, second=False)
            tile(1, 1)
            with pe.Fori(2, NT) as i:
                tile(i, 2)
            tile(NT, 2, first=False)

            pe.wait_ge(S_.rc_in, 16)
            pe.wait_ge(S_.a_ok, 1)
            pe.wait_ge(S_.l_ok, NT)
            rank = ps_s[:, 0, 0:(NT + 1) * E]
            a_flat = a17.rearrange("p n e -> p (n e)")
            pe.matmul(rank, rc[:, R_TRI:R_TRI + P], a_flat, start=True, stop=True)
            for j in range(1, NT + 1):
                mm = pe.matmul(rank[:, j * E:], rc[:, R_ONES:R_ONES + P], a_flat[:, 0:(NT + 1 - j) * E], start=False,
                               stop=True, skip_group_check=True)
            mm.then_inc(S_.rank_mm, 1)
            pe.wait_ge(S_.oh2_ok, 1)
            for r in range(2 * NT):
                mm = pe.matmul(ps_s[:, 0, 512:512 + ET], oh_lo[:, r], oh_hi[:, r], start=r == 0, stop=r == 2 * NT - 1)
            mm.then_inc(S_.tok_mm, 1)

            def turn_in(i, par, k):
                pe.wait_ge((S_.yg_even, S_.yg_odd)[par], 16 * (k + 1))
                if not (isinstance(i, int) and i == 0):
                    pe.wait_ge(S_.ytt_ok, i)
                for c in range(DC):
                    mm = pe.transpose(ps_o[:, c * P:(c + 1) * P], y_in[:, par, c * P:(c + 1) * P], ident)
                mm.then_inc(S_.yt2_mm, 1)

            def up_gate(i, par, j, slot, lead):
                if not lead:
                    pe.wait_ge(S_.hm_ok, 2 * i + j - 1)
                for k in range(2):
                    for c in range(DC):
                        mm = pe.matmul(ps_s[:, k, j * HALF:j * HALF + DEH], y_tt[:, par, c],
                                       w12[:, bass.ds(slot, 1), k, c, j * DEH:(j + 1) * DEH], start=c == 0, stop=c == DC - 1)
                mm.then_inc(S_.ug_mm, 1)

            def turn_h(i, par, lead):
                pe.wait_ge(S_.c_in, 272)
                pe.wait_ge(S_.hm_ok, 2 * i + 2)
                for n in range(NC):
                    m = min(P, DE - n * P)
                    if n == 0 and not lead:
                        pe.wait_ge(S_.hta_ok, i)
                    if n == 4 and not lead:
                        pe.wait_ge(S_.htd_ok, i)
                    mm = pe.transpose(ps_p[0:m, n * P:(n + 1) * P], h_sb[:, par, n * P:n * P + m], ident)
                    if n == 3:
                        mm.then_inc(S_.th_a, 1)
                mm.then_inc(S_.th_b, 1)

            def down(i, par, slot, lead):
                pe.wait_ge(S_.hta_ok, i + 1)
                pe.wait_ge(S_.htd_ok, i + 1)
                if not lead:
                    pe.wait_ge(S_.o_ok2, i)
                for n in range(NC):
                    m = min(P, DE - n * P)
                    mm = pe.matmul(ps_o[:, HALF:HALF + D], h_tt[0:m, par, n], w3_sb[0:m, bass.ds(slot, 1), n],
                                   start=n == 0, stop=n == NC - 1)
                mm.then_inc(S_.w3_mm, 1)

            def slot_of(i):
                return pe.value_load(tab_i[0:1, bass.ds(ET + i, 1)], min_val=0, max_val=1)

            def expert_tile(i, par, k, n, last=False):
                slot = slot_of(i)
                count = pe.value_load(tab_i[0:1, bass.ds(i, 1)], min_val=64, max_val=64 * E)
                pe.wait_ge(S_.e_in, count)
                pe.wait_ge(S_.ytt_ok, i + 1)
                up_gate(i, par, 0, slot, n == 0)
                if n >= 1:
                    turn_h(i - 1, 1 - par, n == 1)
                up_gate(i, par, 1, slot, n == 0)
                if not last:
                    turn_in(i + 1, 1 - par, k + par)
                if n >= 1:
                    down(i - 1, 1 - par, slot_of(i - 1), n == 1)

            pe.wait_ge(S_.tab_ok, 1)
            pe.wait_ge(S_.gl_ok, NT)
            turn_in(0, 0, 0)
            expert_tile(0, 0, 0, 0)
            expert_tile(1, 1, 0, 1)
            with pe.Fori(1, ET // 2 - 1) as k:
                expert_tile(2 * k, 0, k, 2)
                expert_tile(2 * k + 1, 1, k, 2)
            expert_tile(ET - 2, 0, ET // 2 - 1, 2)
            expert_tile(ET - 1, 1, ET // 2 - 1, 2, last=True)
            turn_h(ET - 1, 1, False)
            down(ET - 1, 1, slot_of(ET - 1), False)

        @block.vector
        def _(dve):
            dve.memset(eps_d[:], EPS_D)
            dve.memset(eps_ln[:], EPS_LN)
            dve.memset(eps_rms[:], EPS_RMS)
            dve.memset(v_x[:], 1.0)
            dve.memset(v_aug[:], 1.0).then_inc(S_.eps_ok, 1)
            dve.wait_ge(S_.x_in, 16)
            for i in range(NT):
                bn = dve.bn_stats(stats[:, i, :], x_sb[:, i, :])
            bn.then_inc(S_.stats_ok, 1)
            dve.wait_ge(S_.stats_ok, 1)
            for i in range(NT):
                bn = dve.bn_aggr(mean_var[:, i, :], stats[:, i, :])
            bn.then_inc(S_.aggr_ok, 1)
            dve.wait_ge(S_.std_ok, 1)
            dve.reciprocal(rstd[:], std[:]).then_inc(S_.rstd_ok, 1)
            dve.wait_ge(S_.rstd_ok, 1)
            for i in range(NT):
                bn = dve.tensor_scalar(xn[:, i, :], x_sb[:, i, :], mean_var[:, i, 0:1], rstd[:, i:i + 1],
                                       ALU.subtract, ALU.mult)
            bn.then_inc(S_.xn_ok, 1)
            for k in range(NT // 4 * DC):
                n, c = k // DC, k % DC
                dve.wait_ge(S_.tr_ok, k + 1)
                dve.tensor_copy(xn_t[:, c, n * 512:(n + 1) * 512],
                                ps_s[:, (k % 4) // 2, (k % 2) * 512:(k % 2) * 512 + 512]).then_inc(S_.xnt_ok, 1)
            dve.wait_ge(S_.c_in, 272)
            dve.tensor_scalar(mask_f[:].rearrange("p b k -> p (b k)"), mask_i[:], NEG, None, ALU.mult)
            dve.wait_ge(S_.kv_mm, 1)
            for b in range(B):
                for c in range(DC):
                    kk = dve.tensor_scalar(k_raw[:, b * DC + c], ps_p[:, (b * DC + c) * KC:(b * DC + c + 1) * KC],
                                           b_qk_x[:, DC + c:DC + c + 1], None, ALU.add)
            kk.then_inc(S_.k_ok, 1)
            dve.wait_ge(S_.k_ok, 1)
            for bc in range(B * DC):
                dve.tensor_tensor(k_blk[:, bc], k_raw[:, bc].unsqueeze(1).broadcast_to([P, HPC, KC]),
                                  cst[:, C_HM:C_HM + HPC].unsqueeze(2).broadcast_to([P, HPC, KC]), ALU.mult)
            for b in range(B):
                vv = dve.tensor_tensor(v_x[:, b, :, 0:XD], ps_p[0:KC, HALF + b * D:HALF + (b + 1) * D].rearrange("p (h d) -> p h d", d=XD),
                                       brow[0:KC, 1].rearrange("p (h d) -> p h d", d=XD), ALU.add)
            vv.then_inc(S_.kv_ok, 1)

            def prepare(g, p, par, n):
                first = n == 0
                hd = (p & (H // 2 - 1)) * 2 + par
                dve.wait_ge(S_.qk_proj, g + 1)
                if not first:
                    dve.wait_ge(S_.sq_ok, g)
                    dve.wait_ge(S_.s_ready, 8 * g)
                dve.tensor_scalar(qk[:], ps_p[:], b_qk[:, bass.ds(hd, 1)], cst[:, C_SCALE:C_SCALE + 1],
                                  ALU.add, ALU.mult).then_inc(S_.qk_ok, 1)
                dve.wait_ge(S_.qk_ok, g + 1)
                dve.tensor_copy(qa[0:64], qk[0:64])
                dve.tensor_copy(ka[64:128], qk[64:128]).then_inc(S_.hi_ok, 1)
                dve.tensor_copy(qb[0:64], qk[0:64])
                dve.tensor_copy(ka[0:64], qk[64:128])
                dve.wait_ge(S_.hi_ok, g + 1)
                dve.tensor_tensor(qa[64:128], qk[0:64], qa[0:64], ALU.subtract)
                dve.tensor_tensor(kb[0:64], qk[64:128], ka[64:128], ALU.subtract)
                dve.wait_ge(S_.vg_proj, g + 1)
                if n >= 2:
                    dve.wait_ge(S_.gr_ok, g - 1)
                dve.tensor_scalar(vg[:, par], ps_p[:], b_vg[:, bass.ds(hd, 1)], None, ALU.add).then_inc(S_.vg_ok, 1)
                dve.wait_ge(S_.norm_mm, g + 1)
                dve.tensor_scalar(norms[64:128], ps_p[64:128], cst[64:128, C_ONE:C_ONE + 1], None,
                                  ALU.add).then_inc(S_.norms_ok, 1)
                dve.wait_ge(S_.norms_ok, g + 1)
                dve.tensor_copy(norms_hi[64:128], norms[64:128]).then_inc(S_.norms_hi_ok, 1)
                dve.wait_ge(S_.norms_hi_ok, g + 1)
                dve.scalar_tensor_tensor(out=qb[64:96], in0=norms_hi[64:96].bitcast(F32), scalar=cst[64:96, C_LO:C_LO + 1],
                                         in1=norms[64:96], op0=ALU.mult, op1=ALU.add)
                dve.scalar_tensor_tensor(out=kb[64:96], in0=norms_hi[96:128].bitcast(F32), scalar=cst[96:128, C_LO:C_LO + 1],
                                         in1=norms[96:128], op0=ALU.mult, op1=ALU.add).then_inc(S_.split_ok, 1)
                dve.wait_ge(S_.v_turned, g + 1)
                dve.tensor_copy(v_aug[:, par, :, v_rows(par)],
                                ps_p[:, 0:SB * DH].rearrange("p (b d) -> p b d", d=DH)).then_inc(S_.v_ok, 1)

            def guard(g, par, b):
                dve.wait_ge(S_.s_ready, 8 * g + b + 1)
                dve.tensor_scalar(wts[:, par, b, :], ps_s[:, b % 2, :], 0.0, None, ALU.max).then_inc(S_.max_ok, 1)

            def gate(g, p, par, first):
                dve.wait_ge(S_.gr_ok, g + 1)
                if par == 0 and not first:
                    dve.wait_ge(S_.h_out, 16 * p)
                dve.tensor_tensor(h_pair[v_rows(par)], ps_o[v_rows(par)], g_r[64:128], ALU.mult).then_inc(S_.h_ok, 1)

            def head(g, p, par, n):
                prepare(g, p, par, n)
                if n >= 2:
                    gate(g - 2, p - 1, par, False if not isinstance(p, int) else p == 1)
                for b in range(SB):
                    guard(g, par, b)

            head(0, 0, 0, 0)
            head(1, 0, 1, 1)
            head(2, 1, 0, 2)
            head(3, 1, 1, 2)
            with dve.Fori(2, PAIRS) as p:
                head(2 * p, p, 0, 2)
                head(2 * p + 1, p, 1, 2)
            gate(G - 2, PAIRS - 1, 0, False)
            gate(G - 1, PAIRS - 1, 1, False)

            bank0, bank1 = ps_o[:, 0:512], ps_o[:, 512:1024]

            def xt(i):
                return x_sb[:, bass.ds(i, 1), :].rearrange("p a d -> p (a d)")

            def residual(i, n):
                dve.wait_ge(S_.y_mm, i + 1)
                if n == 0:
                    dve.wait_ge(S_.xb_ok, 1)
                else:
                    dve.wait_ge(S_.x1b_ok, i)
                dve.tensor_tensor(x1s[:], xt(i), bank0[:, 0:D], ALU.add).then_inc(S_.x1_ok, 1)
                dve.wait_ge(S_.x1_ok, i + 1)
                dve.bn_stats(st2[:, 0, :], x1s[:]).then_inc(S_.st_ok, 1)
                dve.wait_ge(S_.xb_ok, 1)
                if n >= 1:
                    dve.wait_ge(S_.r1_ok, i)
                dve.wait_ge(S_.st_ok, i + 1)
                dve.bn_aggr(mv2[:, 0, :], st2[:, 0, :]).then_inc(S_.mv_ok, 1)

            def probs_t(i, k, n):
                dve.wait_ge(S_.pt_mm, 4 * i + k + 1)
                if n >= 1:
                    dve.wait_ge(S_.avx_mm, i)
                dve.tensor_copy(p_t[:, HPB * k:HPB * (k + 1), :].rearrange("p h t -> p (h t)"),
                                ps_p[0:KC, HALF:2 * HALF]).then_inc(S_.ptd_ok, 1)

            def norm_x(i, n):
                dve.wait_ge(S_.r1_ok, i + 1)
                dve.wait_ge(S_.mv_ok, i + 1)
                if n >= 1:
                    dve.wait_ge(S_.xt_mm, i)
                dve.tensor_scalar(xn2, x1s[:], mv2[:, 0, 0:1], r2[:, 0:1], ALU.subtract, ALU.mult).then_inc(S_.xn2_ok, 1)

            def copy_xt(i):
                dve.wait_ge(S_.xt_mm, i + 1)
                dve.tensor_copy(xn2_t.rearrange("p c t -> p (c t)"), bank1[:, 0:D]).then_inc(S_.xnt2_ok, 1)

            def divide(i, n):
                dve.wait_ge(S_.avx_mm, i + 1)
                av = bank0[:, 0:XH * (XD + 1)].rearrange("p (h d) -> p h d", d=XD + 1)
                dve.reciprocal(den[:], av[:, :, XD]).then_inc(S_.den_ok, 1)
                dve.wait_ge(S_.den_ok, i + 1)
                dve.tensor_tensor(o_x, av[:, :, 0:XD], den[:].unsqueeze(2).broadcast_to([P, XH, XD]), ALU.mult).then_inc(S_.o_ok, 1)

            def copy_q(i):
                dve.wait_ge(S_.q_mm, i + 1)
                for c in range(DC):
                    q = dve.tensor_scalar(q_t[:, c], bank1[:, c * P:(c + 1) * P], b_qk_x[:, c:c + 1], XD ** -0.5, ALU.add, ALU.mult)
                q.then_inc(S_.qt_ok, 1)

            def copy_o(i):
                dve.wait_ge(S_.ot_mm, i + 1)
                dve.tensor_copy(o_t.rearrange("p c t -> p (c t)"), bank1[:, 0:D]).then_inc(S_.ot_ok, 1)

            def mask_max(i, n):
                dve.wait_ge(S_.lg_mm, i + 1)
                if n >= 1:
                    dve.wait_ge(S_.pt_mm, 4 * i)
                m = mask_f[:, bass.ds((i >> 3) & 1, 1), :]
                src = ps_s[:].rearrange("p a (j t) -> p (a j) t", j=2)
                for j in range(XH // HPB):
                    q = dve.tensor_tensor(lg[:, HPB * j:HPB * (j + 1), :], src[:, j, 0:HPB * KC].rearrange("p (h k) -> p h k", k=KC),
                                          m.broadcast_to([P, HPB, KC]), ALU.add)
                q.then_inc(S_.l_ok, 1)
                dve.wait_ge(S_.l_ok, i + 1)
                if n >= 1:
                    dve.wait_ge(S_.sub_ok, i)
                dve.tensor_reduce(lmax[:], lg, AX.X, ALU.max).then_inc(S_.lmax_ok, 1)

            def second_norm(i, n):
                dve.wait_ge(S_.out_mm, i + 1)
                dve.wait_ge(S_.x1b_ok, i + 1)
                if n >= 1:
                    dve.wait_ge(S_.base_ok, i)
                dve.tensor_tensor(x2s[:], xt(i), bank0[:, 0:D], ALU.add).then_inc(S_.x2_ok, 1)
                dve.wait_ge(S_.x2_ok, i + 1)
                dve.bn_stats(st2[:, 1, :], x2s[:]).then_inc(S_.st2_ok, 1)
                dve.wait_ge(S_.xb_ok, 1)
                dve.wait_ge(S_.st2_ok, i + 1)
                dve.bn_aggr(mv2[:, 1, :], st2[:, 1, :]).then_inc(S_.mv2_ok, 1)
                dve.wait_ge(S_.mv2_ok, i + 1)
                dve.wait_ge(S_.r2_ok, i + 1)
                dve.tensor_scalar(xin, x2s[:], mv2[:, 1, 0:1], r2[:, 1:2], ALU.subtract, ALU.mult).then_inc(S_.xin_ok, 1)
                dve.wait_ge(S_.xin_ok, i + 1)
                dve.wait_ge(S_.r3_ok, i + 1)
                if n >= 1:
                    dve.wait_ge(S_.yr_out, 16 * i)
                dve.scalar_tensor_tensor(out=y_n, in0=xin, scalar=r2[:, 2:3], in1=brow[:, 3], op0=ALU.mult,
                                         op1=ALU.mult).then_inc(S_.y_ok, 1)
                dve.wait_ge(S_.yt_mm, i + 1)
                dve.tensor_copy(y_tile.rearrange("p c t -> p (c t)"), bank1[:, 0:D]).then_inc(S_.yt_ok, 1)
                dve.wait_ge(S_.gl_mm, i + 1)
                dve.tensor_copy(gl[:, bass.ds(i, 1), :].rearrange("p a e -> p (a e)"), bank0[:, 0:E]).then_inc(S_.gl_ok, 1)

            def tile(i, n, first=True, second=True):
                if first:
                    residual(i, n)
                if second:
                    probs_t(i - 1, 1, n - 1)
                if first:
                    norm_x(i, n)
                if second:
                    probs_t(i - 1, 3, n - 1)
                if first:
                    copy_xt(i)
                if second:
                    divide(i - 1, n - 1)
                if first:
                    copy_q(i)
                if second:
                    copy_o(i - 1)
                if first:
                    mask_max(i, n)
                if second:
                    second_norm(i - 1, n - 1)

            tile(0, 0, second=False)
            tile(1, 1)
            with dve.Fori(2, NT) as i:
                tile(i, 2)
            tile(NT, 2, first=False)

            dve.wait_ge(S_.gl_ok, NT)
            for i in range(NT):
                q = dve.max(top[:, i, :], gl[:, i, :])
            q.then_inc(S_.top_ok, 1)
            dve.wait_ge(S_.top_ok, 1)
            dve.tensor_tensor(pw[:, 0], top[:, :, 1], top[:, :, 0], ALU.subtract).then_inc(S_.dlt_ok, 1)
            for i in range(NT):
                q = dve.max_index(top_i[:, i, :], top[:, i, :], gl[:, i, :])
            q.then_inc(S_.topi_ok, 1)
            dve.wait_ge(S_.topi_ok, 1)
            dve.tensor_copy(top_f[:], top_i[:, :, 0:2]).then_inc(S_.topf_ok, 1)
            dve.wait_ge(S_.pe_ok, 1)
            dve.tensor_scalar(pw[:, 2], pw[:, 1], 1.0, None, ALU.add).then_inc(S_.pw_ok, 1)
            dve.wait_ge(S_.pw_ok, 1)
            dve.reciprocal(pw[:, 3], pw[:, 2]).then_inc(S_.pw_ok, 1)
            dve.wait_ge(S_.pw_ok, 2)
            dve.tensor_tensor(pw[:, 4], pw[:, 3], pw[:, 1], ALU.mult).then_inc(S_.pw_ok, 1)
            dve.wait_ge(S_.topf_ok, 1)
            for k in range(2):
                q = dve.tensor_tensor(w_full[:, k], cst[:, C_IOTA:C_IOTA + E].unsqueeze(1).broadcast_to([P, NT, E]),
                                      top_f[:, :, k:k + 1].broadcast_to([P, NT, E]), ALU.is_equal)
            q.then_inc(S_.oh_ok, 1)
            dve.wait_ge(S_.oh_ok, 1)
            dve.memset(a17[:, NT], 0.0)
            dve.tensor_tensor(a17[:, 0:NT], w_full[:, 0], w_full[:, 1], ALU.add).then_inc(S_.a_ok, 1)
            dve.wait_ge(S_.rc_in, 16)
            dve.wait_ge(S_.rank_mm, 1)
            dve.tensor_tensor(over, ps_s[:, 0, NT * E:(NT + 1) * E].unsqueeze(2).broadcast_to([P, E, NT]),
                              rc[:, R_STEP:R_STEP + NT].unsqueeze(1).broadcast_to([P, E, NT]), ALU.is_gt).then_inc(S_.rt_ok, 1)
            dve.wait_ge(S_.rt_ok, 1)
            dve.tensor_reduce(nt_e, over, AX.X, ALU.add).then_inc(S_.rt_ok, 1)
            dve.wait_ge(S_.rt_ok, 2)
            dve.tensor_tensor(ex_t, nt_e.unsqueeze(1).broadcast_to([P, 9, E]),
                              rc[:, R_EXCL:R_EXCL + 9 * E].rearrange("p (k e) -> p k e", e=E), ALU.mult).then_inc(S_.rt_ok, 1)
            dve.wait_ge(S_.rt_ok, 3)
            dve.tensor_reduce(starts, ex_t, AX.X, ALU.add).then_inc(S_.rt_ok, 1)
            dve.wait_ge(S_.rt_ok, 4)
            dve.tensor_scalar(st128, starts[:, 0:E], float(P), None, ALU.mult).then_inc(S_.rt_ok, 1)
            dve.tensor_tensor(past, rc[:, R_TILE:R_TILE + ET].unsqueeze(2).broadcast_to([P, ET, E - 1]),
                              starts[:, 1:E].unsqueeze(1).broadcast_to([P, ET, E - 1]), ALU.is_ge).then_inc(S_.rt_ok, 1)
            dve.wait_ge(S_.rt_ok, 5)
            dve.tensor_tensor(base, ps_s[:, 0, 0:NT * E].rearrange("p (n e) -> p n e", e=E),
                              st128.unsqueeze(1).broadcast_to([P, NT, E]), ALU.add).then_inc(S_.rt_ok, 1)
            dve.wait_ge(S_.rt_ok, 7)
            dve.tensor_reduce(tab_f[:, 0:ET], past, AX.X, ALU.add).then_inc(S_.rt_ok, 1)
            dve.tensor_tensor(pick, w_full[:, 0], base, ALU.mult).then_inc(S_.rt_ok, 1)
            dve.wait_ge(S_.rt_ok, 9)
            dve.tensor_scalar(tab_f[:, 0:ET], tab_f[:, 0:ET], 1.0, 64.0, ALU.add, ALU.mult)
            dve.tensor_tensor(past, past, rc[:, R_SIGN:R_SIGN + E - 1].unsqueeze(1).broadcast_to([P, ET, E - 1]), ALU.mult)
            dve.tensor_reduce(slot_f[:, 0:NT], pick, AX.X, ALU.add).then_inc(S_.rt_ok, 1)
            dve.wait_ge(S_.rt_ok, 10)
            dve.tensor_reduce(tab_f[:, ET:2 * ET], past, AX.X, ALU.add)
            dve.tensor_copy(tab_f[:, 2 * ET:], starts)
            dve.tensor_tensor(pick, w_full[:, 1], base, ALU.mult).then_inc(S_.rt_ok, 1)
            dve.wait_ge(S_.rt_ok, 11)
            dve.tensor_reduce(slot_f[:, NT:], pick, AX.X, ALU.add).then_inc(S_.rt_ok, 1)
            dve.tensor_copy(tab_i[:], tab_f).then_inc(S_.tab_ok, 1)
            dve.wait_ge(S_.rt_ok, 12)
            dve.tensor_copy(slot_i[:], slot_f).then_inc(S_.slot_ok, 1)
            dve.wait_ge(S_.slot_ok, 1)
            dve.tensor_scalar(hl_i[:, 0:2 * NT], slot_i[:], P.bit_length() - 1, None, ALU.logical_shift_right)
            dve.tensor_scalar(hl_i[:, 2 * NT:], slot_i[:], P - 1, None, ALU.bitwise_and).then_inc(S_.hl_ok, 1)
            dve.wait_ge(S_.hl_ok, 1)
            dve.tensor_copy(hl_f, hl_i[:]).then_inc(S_.hl_ok, 1)
            dve.wait_ge(S_.hl_ok, 2)
            dve.tensor_tensor(oh_hi, rc[:, R_TILE:R_TILE + ET].unsqueeze(1).broadcast_to([P, 2 * NT, ET]),
                              hl_f[:, 0:2 * NT].unsqueeze(2).broadcast_to([P, 2 * NT, ET]), ALU.is_equal).then_inc(S_.hl_ok, 1)
            dve.tensor_tensor(oh_lo, rc[:, R_POS:R_POS + P].unsqueeze(1).broadcast_to([P, 2 * NT, P]),
                              hl_f[:, 2 * NT:].unsqueeze(2).broadcast_to([P, 2 * NT, P]), ALU.is_equal)
            dve.wait_ge(S_.hl_ok, 3)
            for k in range(2):
                q = dve.tensor_tensor(oh_hi[:, k * NT:(k + 1) * NT], oh_hi[:, k * NT:(k + 1) * NT],
                                      rc[:, R_TOK:R_TOK + NT].unsqueeze(2).broadcast_to([P, NT, ET]), ALU.mult)
            q.then_inc(S_.oh2_ok, 1)
            dve.wait_ge(S_.tok_mm, 1)
            dve.tensor_copy(tok_i[:], ps_s[:, 0, 512:512 + ET]).then_inc(S_.tok_ok, 1)

            def copy_in(i, par, n):
                dve.wait_ge(S_.yt2_mm, i + 1)
                if n >= 2:
                    dve.wait_ge(S_.ug_mm, 2 * i - 2)
                dve.tensor_copy(y_tt[:, par].rearrange("p c t -> p (c t)"), ps_o[:, 0:D]).then_inc(S_.ytt_ok, 1)

            def gated(i, par, j, n):
                dve.wait_ge(S_.silu_ok, 2 * i + j + 1)
                if j == 0 and n >= 2:
                    dve.wait_ge(S_.th_b, i - 1)
                t = slice(j * DEH, (j + 1) * DEH)
                dve.tensor_tensor(h_sb[:, par, t], s_up[:, t], ps_s[:, 1, j * HALF:j * HALF + DEH], ALU.mult).then_inc(S_.hm_ok, 1)

            def copy_h(i, par, n):
                dve.wait_ge(S_.th_b, i + 1)
                if n >= 2:
                    dve.wait_ge(S_.w3_mm, i - 1)
                m = DE - (NC - 1) * P
                dve.tensor_copy(h_tt[:, par, 4], ps_p[:, 4 * P:5 * P])
                dve.tensor_copy(h_tt[0:m, par, 5], ps_p[0:m, 5 * P:6 * P]).then_inc(S_.htd_ok, 1)

            def expert_tile(i, par, n, last=False):
                gated(i, par, 0, n)
                if n >= 1:
                    copy_h(i - 1, 1 - par, n - 1)
                gated(i, par, 1, n)
                if not last:
                    copy_in(i + 1, 1 - par, n + 1)

            copy_in(0, 0, 0)
            expert_tile(0, 0, 0)
            expert_tile(1, 1, 1)
            expert_tile(2, 0, 2)
            expert_tile(3, 1, 3)
            with dve.Fori(2, ET // 2 - 1) as k:
                expert_tile(2 * k, 0, 3)
                expert_tile(2 * k + 1, 1, 3)
            expert_tile(ET - 2, 0, 3)
            expert_tile(ET - 1, 1, 3, last=True)
            copy_h(ET - 1, 1, 3)

            dve.wait_ge(S_.base_ok, NT)
            dve.wait_ge(S_.pw_ok, 3)
            for c in range(4):
                dve.wait_ge((S_.og0, S_.og1, S_.og2, S_.og3)[c], 16 * 2 * NT // 4)
                for k in range(2):
                    for i in range(c * NT // 4, (c + 1) * NT // 4):
                        q = dve.scalar_tensor_tensor(out=x_sb[:, i], in0=o_tok[:, k, i], scalar=pw[:, 3 + k, i:i + 1],
                                                     in1=x_sb[:, i], op0=ALU.mult, op1=ALU.add)
                    q.then_inc(S_.sum_ok if k == 0 else S_.acc_ok, 1)
                    if k == 0:
                        dve.wait_ge(S_.sum_ok, c + 1)

        @block.scalar
        def _(act):
            act.wait_ge(S_.eps_ok, 1)
            act.wait_ge(S_.aggr_ok, 1)
            act.activation(std[:], mean_var[:, :, 1], ACT.Sqrt, bias=eps_ln[:, 0:1]).then_inc(S_.std_ok, 1)

            def chunk(par, c):
                return wts[:, par, 2 * c:2 * c + 2, :].rearrange("p b t -> p (b t)")

            def rows(g, par, first):
                act.wait_ge(S_.av_done, g + 1)
                if not first:
                    act.wait_ge(S_.gr_ok, g)
                act.activation(rinv[64:128], ps_o[rs_rows(par)], ACT.Ln, bias=eps_d[rs_rows(par), 0:1]).then_inc(S_.rln_ok, 1)
                act.wait_ge(S_.rln_ok, g + 1)
                act.activation(rinv[64:128], rinv[64:128], ACT.Exp, scale=-1.0).then_inc(S_.r_ok, 1)

            def head(g, par, n):
                for c in range(4):
                    act.wait_ge(S_.max_ok, 8 * g + 2 * c + 2)
                    act.activation(chunk(par, c), chunk(par, c), ACT.Sqrt).then_inc(S_.sqrt_ok, 1)
                act.preload_act_table_set("natural_log_exp_and_others")
                if n >= 1:
                    rows(g - 1, 1 - par, n == 1)

                def ln(c):
                    act.wait_ge(S_.sqrt_ok, 4 * g + c + 1)
                    act.activation(chunk(par, c), chunk(par, c), ACT.Ln, bias=eps_d[:, 0:1]).then_inc(S_.ln_ok, 1)

                def exp(c):
                    act.wait_ge(S_.ln_ok, 4 * g + c + 1)
                    act.activation(chunk(par, c), chunk(par, c), ACT.Exp, scale=-2.0).then_inc(S_.w_ok, 1)

                ln(0)
                for c in range(4):
                    if c < 3:
                        ln(c + 1)
                    exp(c)

            head(0, 0, 0)
            head(1, 1, 1)
            with act.Fori(1, PAIRS) as p:
                head(2 * p, 0, 2)
                head(2 * p + 1, 1, 2)
            rows(G - 1, 1, False)

            def probs_t(i, k, n):
                act.wait_ge(S_.pt_mm, 4 * i + k + 1)
                if n >= 1:
                    act.wait_ge(S_.avx_mm, i)
                act.activation(p_t[:, HPB * k:HPB * (k + 1), :].rearrange("p h t -> p (h t)"), ps_p[0:KC, 0:HALF],
                               ACT.Copy).then_inc(S_.pta_ok, 1)

            def rstd_of(i, src, dst, scale, eps, logged, ready):
                act.activation(dst, src, ACT.Ln, bias=eps[:, 0:1], scale=scale).then_inc(logged, 1)
                act.wait_ge(logged, i + 1)
                act.activation(dst, dst, ACT.Exp, scale=-0.5).then_inc(ready, 1)

            def tile(i, n, first=True, second=True):
                if second:
                    probs_t(i - 1, 0, n - 1)
                if first:
                    act.wait_ge(S_.mv_ok, i + 1)
                    if n >= 1:
                        act.wait_ge(S_.xn2_ok, i)
                    rstd_of(i, mv2[:, 0, 1:2], r2[:, 0:1], 1.0, eps_ln, S_.lr1, S_.r1_ok)
                if second:
                    probs_t(i - 1, 2, n - 1)
                    act.wait_ge(S_.mv2_ok, i)
                    if n >= 2:
                        act.wait_ge(S_.xin_ok, i - 1)
                    rstd_of(i - 1, mv2[:, 1, 1:2], r2[:, 1:2], 1.0, eps_ln, S_.lr2, S_.r2_ok)
                if first:
                    act.wait_ge(S_.sub_ok, i + 1)
                    act.activation(lg, lg, ACT.Exp).then_inc(S_.exp_ok, 1)
                if second:
                    act.wait_ge(S_.xin_ok, i)
                    if n >= 2:
                        act.wait_ge(S_.y_ok, i - 1)
                    act.activation(sq_junk, xin, ACT.Square, accum_out=r2[:, 3:4]).then_inc(S_.ms_ok, 1)
                    act.wait_ge(S_.ms_ok, i)
                    rstd_of(i - 1, r2[:, 3:4], r2[:, 2:3], 1.0 / D, eps_rms, S_.lr3, S_.r3_ok)

            tile(0, 0, second=False)
            tile(1, 1)
            with act.Fori(2, NT) as i:
                tile(i, 2)
            tile(NT, 2, first=False)

            act.wait_ge(S_.dlt_ok, 1)
            act.activation(pw[:, 1], pw[:, 0], ACT.Exp).then_inc(S_.pe_ok, 1)

            def silu(i, j, n):
                act.wait_ge(S_.ug_mm, 2 * i + j + 1)
                if n >= 1:
                    act.wait_ge(S_.hm_ok, 2 * i + j - 1)
                act.activation(s_up[:, j * DEH:(j + 1) * DEH], ps_s[:, 0, j * HALF:j * HALF + DEH],
                               ACT.Silu).then_inc(S_.silu_ok, 1)

            def copy_h(i, par, n):
                act.wait_ge(S_.th_a, i + 1)
                if n >= 2:
                    act.wait_ge(S_.w3_mm, i - 1)
                act.activation(h_tt[:, par, 0:4].rearrange("p n t -> p (n t)"), ps_p[:, 0:4 * P], ACT.Copy).then_inc(S_.hta_ok, 1)

            def copy_out(i, par, k, n):
                act.wait_ge(S_.w3_mm, i + 1)
                if n >= 2:
                    act.wait_ge((S_.os_even, S_.os_odd)[par], 16 * k)
                act.activation(o_sb[:, par], ps_o[:, HALF:HALF + D], ACT.Copy).then_inc(S_.o_ok2, 1)

            def expert_tile(i, par, k, n):
                silu(i, 0, n)
                if n >= 1:
                    copy_h(i - 1, 1 - par, n - 1)
                silu(i, 1, n)
                if n >= 1:
                    copy_out(i - 1, 1 - par, k if par else k - 1, n - 1)

            expert_tile(0, 0, 0, 0)
            expert_tile(1, 1, 0, 1)
            expert_tile(2, 0, 1, 2)
            expert_tile(3, 1, 1, 3)
            with act.Fori(2, ET // 2) as k:
                expert_tile(2 * k, 0, k, 3)
                expert_tile(2 * k + 1, 1, k, 3)
            copy_h(ET - 1, 1, 3)
            copy_out(ET - 1, 1, ET // 2 - 1, 3)

        @block.gpsimd
        def _(pool):
            def squares(g, first, gated=True):
                pool.wait_ge(S_.qk_ok, g + 1)
                if not first:
                    pool.wait_ge(S_.norm_mm, g)
                if gated:
                    pool.wait_ge(S_.gr_ok, g - 2)
                pool.tensor_tensor(qk_sq[:], qk[:], qk[:], ALU.mult).then_inc(S_.sq_ok, 1)

            def gate_rows(g, par, first, after):
                pool.wait_ge(S_.r_ok, g + 1)
                pool.wait_ge(S_.sq_ok, after)
                if not first:
                    pool.wait_ge(S_.h_ok, g)
                pool.tensor_tensor(g_r[64:128], vg[64:128, par], rinv[64:128], ALU.mult).then_inc(S_.gr_ok, 1)

            pool.wait_ge(S_.xn_ok, 1)
            pool.wait_ge(S_.c_in, 272)
            pool.tensor_tensor(x_sb[:], x_sb[:], brow[:, 0:1].broadcast_to([P, NT, D]), ALU.add).then_inc(S_.xb_ok, 1)
            squares(0, True, gated=False)
            squares(1, False, gated=False)
            squares(2, False, gated=False)
            gate_rows(0, 0, True, 3)
            squares(3, False)
            gate_rows(1, 1, False, 4)
            with pool.Fori(2, PAIRS) as p:
                for par in range(2):
                    squares(2 * p + par, False)
                    gate_rows(2 * p + par - 2, par, False, 2 * p + par + 1)
            gate_rows(G - 2, 0, False, G)
            gate_rows(G - 1, 1, False, G)

            def tile(i, n, first=True, second=True):
                if first:
                    x1 = x_sb[:, bass.ds(i, 1), :].rearrange("p a d -> p (a d)")
                    pool.wait_ge(S_.xn2_ok, i + 1)
                    pool.tensor_tensor(x1, x1s[:], brow[:, 2], ALU.add).then_inc(S_.x1b_ok, 1)
                    pool.wait_ge(S_.lmax_ok, i + 1)
                    pool.tensor_tensor(lg, lg, lmax[:].unsqueeze(2).broadcast_to([P, XH, KC]), ALU.subtract).then_inc(S_.sub_ok, 1)
                if second:
                    x2 = x_sb[:, bass.ds(i - 1, 1), :].rearrange("p a d -> p (a d)")
                    pool.wait_ge(S_.xin_ok, i)
                    pool.tensor_tensor(x2, x2s[:], xin, ALU.add).then_inc(S_.base_ok, 1)

            tile(0, 0, second=False)
            tile(1, 1)
            with pool.Fori(2, NT) as i:
                tile(i, 2)
            tile(NT, 2, first=False)

            def fetch(k, par, n):
                i = 2 * k + par
                q = (S_.yg_even, S_.yg_odd)[par]
                now = (S_.now_even, S_.now_odd)[par] if n else S_.now_first
                pool.wait_ge(S_.tok_ok, 1)
                if n >= 1:
                    pool.wait_ge(q, 16 * k)
                    pool.wait_ge(S_.yt2_mm, i - 1)
                pool.tensor_copy(tok_now[:, par:par + 1], tok_i[:, bass.ds(i, 1)]).then_inc(now, 1)
                pool.wait_ge(S_.slot_ok, 1)
                pool.wait_ge(now, k if n else par + 1)
                pool.indirect_dma_start(out=y_in[:, par], out_offset=None, in_=y_rows,
                                        in_offset=bass.IndirectOffsetOnAxis(ap=tok_now[:, par:par + 1], axis=0)).then_inc(q, 16)

            def store(k, par):
                i = 2 * k + par
                pool.wait_ge(S_.tab_ok, 1)
                pool.wait_ge(S_.o_ok2, i + 1)
                pool.dma_start(o_rows[bass.ds(i * P, P)], o_sb[:, par]).then_inc((S_.os_even, S_.os_odd)[par], 16)

            pool.wait_ge(S_.yr_out, 16 * NT)
            fetch(0, 0, 0)
            fetch(0, 1, 0)
            with pool.Fori(1, ET // 2) as k:
                for par in range(2):
                    fetch(k, par, 1)
                    store(k - 1, par)
            for par in range(2):
                store(ET // 2 - 1, par)
            pool.wait_ge(S_.os_even, 8 * ET)
            pool.wait_ge(S_.os_odd, 8 * ET)
            for i in range(NT):
                for k in range(2):
                    r = k * NT + i
                    pool.indirect_dma_start(out=o_tok[:, k, i], out_offset=None, in_=o_rows,
                                            in_offset=bass.IndirectOffsetOnAxis(ap=slot_i[:, r:r + 1], axis=0)).then_inc(
                        (S_.og0, S_.og1, S_.og2, S_.og3)[i * 4 // NT], 16)


def kernel(x, ctx_1024, mask_BxS2_ik0, L0_attn_W_in, L0_attn_b_in, L0_attn_W_out, L0_attn_b_out,
           L0_xattn_Wq, L0_xattn_bq, L0_xattn_Wk, L0_xattn_bk, L0_xattn_Wv, L0_xattn_bv, L0_xattn_Wo, L0_xattn_bo,
           L0_ffn_gate_w, L0_ffn_rms_w, L0_ffn_W1, L0_ffn_W2, L0_ffn_W3):
    import numpy as np
    import concourse.bacc as bacc
    from concourse.bass_utils import run_bass_kernel_spmd

    a = np.asarray
    laid_out = {
        "x": a(x),
        "ctx_t": a(ctx_1024).transpose(2, 0, 1).reshape(D, B * KC),
        "mask": a(mask_BxS2_ik0).reshape(1, B * KC),
        "w_in": a(L0_attn_W_in),
        "b_in": a(L0_attn_b_in).reshape(H, 2, P).transpose(1, 2, 0),
        "w_out": a(L0_attn_W_out),
        "w_x": np.stack([a(w).T for w in (L0_xattn_Wq, L0_xattn_Wk, L0_xattn_Wv, L0_xattn_Wo)]),
        "b_cols": np.concatenate([a(b).reshape(DC, P).T for b in (L0_xattn_bq, L0_xattn_bk)], axis=1),
        "rows_in": np.stack([a(b) for b in (L0_attn_b_out, L0_xattn_bv, L0_xattn_bo, L0_ffn_rms_w)]),
        "gate_w": a(L0_ffn_gate_w).T,
        "w1": a(L0_ffn_W1).transpose(0, 2, 1),
        "w2": a(L0_ffn_W2).transpose(0, 2, 1),
        "w3": a(L0_ffn_W3).transpose(0, 2, 1),
        "consts": constants(np),
        "r_consts": router_constants(np),
    }
    nc = bacc.Bacc("TRN2", target_bir_lowering=False, num_devices=1)
    laid_out = {n: np.ascontiguousarray(v) for n, v in laid_out.items()}
    args = [nc.dram_tensor(f"in_{n}", v.shape, mybir.dt.from_np(v.dtype), kind="ExternalInput").ap() for n, v in laid_out.items()]
    out = nc.dram_tensor("out_y", (B, T, D), F32, kind="ExternalOutput").ap()
    program(nc, *args, out)
    r = run_bass_kernel_spmd(nc, [{f"in_{n}": v for n, v in laid_out.items()}], core_ids=[0])
    return r.results[0]["out_y"]
```

```python
from contextlib import ExitStack

import concourse.bass as bass
from concourse import mybir

ALU = mybir.AluOpType
ACT = mybir.ActivationFunctionType
AX = mybir.AxisListType
F32 = mybir.dt.float32
F32R = mybir.dt.float32r
U32 = mybir.dt.uint32

P = 128
B, T, D = 2, 1024, 256
H, DH = 16, 64
DC = D // P
NT = B * T // P
SB = T // P
HALF = T // 2
G = B * H
PAIRS = G // 2
EPS_D, EPS_LN, EPS_RMS = 1e-4, 1e-5, 1e-6
XH, XD = 16, D // 16
KC = 77
HPB = 4
HPC = XH // DC
LOGITS = ((0, 0, 0, 6), (1, 0, 6, 2), (1, 2, 8, 4), (2, 0, 12, 4))
LBANKS = ((0, 0, 6), (1, 6, 6), (2, 12, 4))
E, DE = 8, 704
NC = -(-DE // P)
DEH = DE // 2
ET = 2 * NT + E
NEG = -1e9

C_ID, C_SEL, C_SCALE, C_ONE, C_LO, C_HM, C_IOTA, C_UNIT, C_W = 0, 128, 192, 193, 194, 195, 203, 211, 212
R_TRI, R_ONES, R_POS, R_TILE, R_STEP, R_EXCL, R_SIGN, R_TOK = 0, P, 2 * P, 3 * P, 3 * P + ET, 3 * P + ET + NT, 3 * P + ET + NT + 9 * E, 3 * P + ET + NT + 10 * E
R_W = R_TOK + NT


def constants(np):
    c = np.zeros((P, C_W), np.float32)
    c[:, C_ID:C_ID + P] = np.eye(P)
    c[0:64, C_SEL:C_SEL + 2] = 0.25
    c[64:128, C_SEL + 34:C_SEL + 36] = 1.0
    c[0:64, C_SCALE] = -2.0
    c[64:128, C_SCALE] = 1.0
    c[[66, 67, 96, 97], C_ONE] = 1.0
    c[[65, 99], C_LO] = -1.0
    c[np.arange(P), C_HM + np.arange(P) // XD] = 1.0
    c[:, C_IOTA:C_IOTA + E] = np.arange(E)
    c[:, C_UNIT] = 1.0
    return c


def router_constants(np):
    c = np.zeros((P, R_W), np.float32)
    c[:, R_TRI:R_TRI + P] = np.triu(np.ones((P, P)), 1)
    c[:, R_ONES:R_ONES + P] = 1.0
    c[:, R_POS:R_POS + P] = np.arange(P)
    c[:, R_TILE:R_TILE + ET] = np.arange(ET)
    c[:, R_STEP:R_STEP + NT] = np.arange(NT) * P
    c[:, R_STEP] = -1.0
    c[:, R_EXCL:R_EXCL + 9 * E] = np.tril(np.ones((9, E)), -1).reshape(-1)
    c[:, R_SIGN:R_SIGN + E - 1] = [(-1) ** k for k in range(E - 1)]
    c[:, R_TOK:R_TOK + NT] = np.arange(P)[:, None] + P * np.arange(NT)
    return c


def program(nc, x, ctx_t, mask, w_in, b_in, w_out, w_x, b_cols, rows_in, gate_w, w1, w2, w3, consts, r_consts, out):
    with ExitStack() as ctx:
        def sb(name, shape, dt=F32):
            return ctx.enter_context(nc.sbuf_tensor(name, shape, dt))

        def psum(name, shape, dt=F32):
            return ctx.enter_context(nc.psum_tensor(name, shape, dt))

        def sem(name):
            return ctx.enter_context(nc.semaphore(name))

        ps_s = psum("ps_s", [P, 2, T])
        ps_o = psum("ps_o", [P, T])
        ps_p = psum("ps_p", [P, T])

        h_t = nc.dram_tensor("h_t", [PAIRS, P, T], F32, kind="Internal").ap()
        y_rows = nc.dram_tensor("y_rows", [NT * P, D], F32, kind="Internal").ap()
        o_rows = nc.dram_tensor("o_rows", [ET * P, D], F32, kind="Internal").ap()

        cst = sb("cst", [P, C_W])
        x_sb = sb("x_sb", [P, NT, D])
        xn_t = sb("xn_t", [P, DC, B * T])
        stats = sb("stats", [P, NT, 6])
        mean_var = sb("mean_var", [P, NT, 2])
        std = sb("std", [P, NT])
        rstd = sb("rstd", [P, NT])
        w_head = sb("w_head", [P, 2, DC, 4 * DH])
        b_qk = sb("b_qk", [P, H])
        b_vg = sb("b_vg", [P, H])
        qk = sb("qk", [P, T])
        qk_sq = sb("qk_sq", [P, T])
        qa = sb("qa", [P, T], F32R)
        ka = sb("ka", [P, T], F32R)
        qb = sb("qb", [96, T], F32R)
        kb = sb("kb", [96, T], F32R)
        norms = sb("norms", [P, T])
        norms_hi = sb("norms_hi", [P, T], F32R)
        vg = sb("vg", [P, 2, T])
        v_aug = sb("v_aug", [P, 2, SB, P])
        wts = sb("wts", [P, 2, SB, T])
        o_raw = sb("o_raw", [P, T])
        rinv = sb("rinv", [P, T])
        g_r = sb("g_r", [P, T])
        h_pair = sb("h_pair", [P, T])
        eps_d = sb("eps_d", [P, 1])
        eps_ln = sb("eps_ln", [P, 1])

        w_x_sb = sb("w_x_sb", [P, 4, DC, D])
        ctx_sb = sb("ctx_sb", [P, DC, B * KC])
        b_qk_x = sb("b_qk_x", [P, 2 * DC])
        brow = sb("brow", [P, 4, D])
        mask_i = sb("mask_i", [P, B * KC], mybir.dt.int32)
        mask_f = sb("mask_f", [P, B, KC])
        k_raw = sb("k_raw", [P, B * DC, KC])
        k_blk = sb("k_blk", [P, B * DC, HPC, KC])
        v_x = sb("v_x", [KC, B, XH, XD + 1])
        gate_sb = sb("gate_sb", [P, DC, E])
        h_tile = qk[:].rearrange("p (q t) -> p q t", t=P)
        x1s = sb("x1s", [P, D])
        x2s = sb("x2s", [P, D])
        st2 = sb("st2", [P, 2, 6])
        mv2 = sb("mv2", [P, 2, 2])
        r2 = sb("r2", [P, 4])
        xn2 = norms[:, 0:D]
        xn2_t = norms[:, D:2 * D].rearrange("p (c t) -> p c t", t=P)
        q_t = norms[:, 2 * D:3 * D].rearrange("p (c t) -> p c t", t=P)
        o_x = norms[:, 3 * D:4 * D].rearrange("p (h d) -> p h d", d=XD)
        lg = v_aug[:].rearrange("p a b t -> p (a b t)")[:, 0:XH * KC].rearrange("p (h k) -> p h k", k=KC)
        lmax = sb("lmax", [P, XH])
        p_t = vg[0:KC].rearrange("p a t -> p (a t)").rearrange("p (h t) -> p h t", t=P)
        den = sb("den", [P, XH])
        o_t = qk_sq[:, 0:D].rearrange("p (c t) -> p c t", t=P)
        xin = qk_sq[:, D:2 * D]
        sq_junk = qk_sq[:, 2 * D:3 * D]
        y_n = qk_sq[:, 3 * D:4 * D]
        y_tile = rinv[:, 0:D].rearrange("p (c t) -> p c t", t=P)
        gl = sb("gl", [P, NT, E])
        top = sb("top", [P, NT, 8])
        top_i = sb("top_i", [P, NT, 8], U32)
        top_f = sb("top_f", [P, NT, 2])
        pw = sb("pw", [P, 5, NT])
        w_full = sb("w_full", [P, 2, NT, E])
        eps_rms = sb("eps_rms", [P, 1])
        room = wts[:].rearrange("p a b t -> p (a b t)")
        room_at = [0]

        def take(n):
            room_at[0] += n
            return room[:, room_at[0] - n:room_at[0]]

        W12, W3 = 2 * DC * DE, NC * D
        w12 = take(2 * W12).rearrange("p (s k c n) -> p s k c n", s=2, k=2, c=DC)
        w3_sb = take(2 * W3).rearrange("p (s n d) -> p s n d", s=2, n=NC)
        w_end = room_at[0]
        y_in = take(2 * D).rearrange("p (s d) -> p s d", s=2)
        y_tt = take(2 * D).rearrange("p (s c t) -> p s c t", s=2, c=DC)
        s_up = take(DE)
        h_sb = take(2 * DE).rearrange("p (s n) -> p s n", s=2)
        h_tt = take(2 * NC * P).rearrange("p (s n t) -> p s n t", s=2, n=NC)
        o_sb = take(2 * D).rearrange("p (s d) -> p s d", s=2)
        zeros = wts[:, 1, 0:E * D // T, :].rearrange("p a (b d) -> p (a b) d", d=D)
        w_o = room[:, w_end:w_end + H // 2 * D].rearrange("p (q n) -> p q n", n=D)
        room_at[0] = w_end
        oh_lo = take(2 * NT * P).rearrange("p (r s) -> p r s", s=P)
        oh_hi = take(2 * NT * ET).rearrange("p (r e) -> p r e", e=ET)
        rc = take(R_W)
        a17 = take((NT + 1) * E).rearrange("p (n e) -> p n e", e=E)
        over = take(E * NT).rearrange("p (e n) -> p e n", e=E)
        nt_e = take(E)
        ex_t = take(9 * E).rearrange("p (k e) -> p k e", e=E)
        starts = take(9)
        st128 = take(E)
        past = take(ET * (E - 1)).rearrange("p (i e) -> p i e", e=E - 1)
        tab_f = take(2 * ET + 10)
        base = take(NT * E).rearrange("p (n e) -> p n e", e=E)
        pick = take(NT * E).rearrange("p (n e) -> p n e", e=E)
        slot_f = take(2 * NT)
        hl_f = take(4 * NT)
        o_tok = room[:, 0:2 * NT * D].rearrange("p (k n d) -> p k n d", k=2, n=NT)
        pairs_i = sb("pairs_i", [P, 1], mybir.dt.int32)
        slot_n = sb("slot_n", [P, 2 * NT], U32)
        tab_i = sb("tab_i", [P, 2 * ET + 10], mybir.dt.int32)
        slot_i = sb("slot_i", [P, 2 * NT], U32)
        hl_i = sb("hl_i", [P, 4 * NT], U32)
        tok_i = sb("tok_i", [P, ET], U32)
        tok_now = sb("tok_now", [P, 2], U32)

        names = ("x_in", "c_in", "stats_ok", "aggr_ok", "std_ok", "rstd_ok", "xn_ok", "tr_ok", "xnt_ok",
                 "w_even", "w_odd", "qk_proj", "vg_proj", "norm_mm", "v_turned", "s_ready", "av_done",
                 "qk_ok", "hi_ok", "vg_ok", "norms_ok", "norms_hi_ok", "split_ok", "v_ok", "max_ok", "h_ok",
                 "sq_ok", "gr_ok", "sqrt_ok", "ln_ok", "w_ok", "rln_ok", "r_ok", "h_out", "eps_ok", "oraw_ok", "wo_in", "hi2_ok",
                 "kv_mm", "k_ok", "kv_ok", "mask_ok", "xb_ok",
                 "ht_in", "y_mm", "pt_mm", "xt_mm", "avx_mm", "q_mm", "ot_mm", "lg_mm", "out_mm", "yt_mm", "gl_mm",
                 "x1_ok", "st_ok", "mv_ok", "xn2_ok", "xnt2_ok", "ptd_ok", "den_ok", "o_ok", "qt_ok", "ot_ok", "l_ok",
                 "lmax_ok", "x2_ok", "st2_ok", "mv2_ok", "xin_ok", "y_ok", "yt_ok", "gl_ok", "yr_out",
                 "pta_ok", "lr1", "r1_ok", "lr2", "r2_ok", "ms_ok", "lr3", "r3_ok", "exp_ok",
                 "x1b_ok", "sub_ok", "base_ok", "top_ok", "topi_ok", "topf_ok", "dlt_ok", "pe_ok", "pw_ok", "wf_ok",
                 "rc_in", "oh_ok", "a_ok", "rank_mm", "rt_ok", "tab_ok", "slot_ok", "hl_ok", "oh2_ok", "tok_mm", "tok_ok",
                 "e_in", "now_first", "now_even", "now_odd", "yg_even", "yg_odd", "yt2_mm", "ytt_ok", "ug_mm", "silu_ok", "hm_ok", "th_a", "th_b",
                 "hta_ok", "htd_ok", "w3_mm", "o_ok2", "os_even", "os_odd", "og0", "og1", "og2", "og3", "zero_ok", "zero_out", "slotn_ok", "acc_ok", "sum_ok", "done")
        s = {n: sem(n) for n in names}
        S_ = type("Sems", (), s)

        ident = cst[:, C_ID:C_ID + P]
        xn = wts[:, 0, 0:4, :].rearrange("p a (b d) -> p (a b) d", d=D)

        block = ctx.enter_context(nc.Block())

        def rs_rows(par):
            return slice(64, 128) if par == 0 else slice(0, 64)

        def v_rows(par):
            return slice(0, 64) if par == 0 else slice(64, 128)

        @block.sync
        def _(sp):
            sp.dma_start(x_sb[:], x.rearrange("b (n p) d -> p (b n) d", p=P)).then_inc(S_.x_in, 16)
            sp.dma_start(cst[:], consts).then_inc(S_.c_in, 16)
            sp.dma_start(b_qk[:], b_in[0]).then_inc(S_.c_in, 16)
            sp.dma_start(b_vg[:], b_in[1]).then_inc(S_.c_in, 16)
            for c in range(DC):
                sp.dma_start(ctx_sb[:, c], ctx_t[c * P:(c + 1) * P]).then_inc(S_.c_in, 16)
            for k in range(4):
                sp.dma_start(w_x_sb[:, k], w_x[k].rearrange("(c p) n -> p c n", p=P)).then_inc(S_.c_in, 16)
            sp.dma_start(b_qk_x[:], b_cols).then_inc(S_.c_in, 16)
            for k in range(4):
                sp.dma_start(brow[:, k], rows_in[k:k + 1].partition_broadcast(P)).then_inc(S_.c_in, 16)
            sp.dma_start(mask_i[:], mask.partition_broadcast(P)).then_inc(S_.c_in, 16)
            sp.dma_start(gate_sb[:], gate_w.rearrange("(c p) e -> p c e", p=P)).then_inc(S_.c_in, 16)

            def load_head(col, par):
                src = w_in.rearrange("(c p) n -> p c n", p=P)[:, :, bass.ds(col, 4 * DH)]
                sp.dma_start(w_head[:, par], src).then_inc((S_.w_even, S_.w_odd)[par], 16)

            def store_pair(p):
                sp.wait_ge(S_.x_in, 16)
                sp.wait_ge(S_.h_ok, 2 * p + 2)
                sp.dma_start(h_t[bass.ds(p, 1)].rearrange("a p t -> p (a t)"), h_pair[:]).then_inc(S_.h_out, 16)

            load_head(0, 0)
            load_head(4 * DH, 1)
            sp.wait_ge(S_.zero_ok, 1)
            sp.dma_start(o_rows[2 * NT * P:].rearrange("(n p) d -> p n d", p=P), zeros).then_inc(S_.zero_out, 16)
            for par in range(2):
                sp.wait_ge(S_.vg_proj, par + 1)
                load_head((2 + par) * 4 * DH, par)
            for b in range(B):
                p0 = b * H // 2
                with sp.Fori(max(p0, 2), p0 + H // 2) as p:
                    for par in range(2):
                        sp.wait_ge(S_.vg_proj, 2 * p + par - 1)
                        load_head(((p - p0) * 2 + par) * 4 * DH, par)
                    store_pair(p - 2)
            store_pair(PAIRS - 2)
            sp.wait_ge(S_.av_done, G)
            sp.dma_start(w_o, w_out.rearrange("(q p) n -> p q n", p=P)).then_inc(S_.wo_in, 16)
            store_pair(PAIRS - 1)
            sp.wait_ge(S_.h_out, 16 * PAIRS)

            def load_tile(i):
                src = h_t.rearrange("(b q) p t -> b p q t", b=B)[bass.ds((i >> 3) & 1, 1), :, :, bass.ds((i & 7) * P, P)]
                sp.dma_start(h_tile, src.rearrange("b p q t -> p (b q) t")).then_inc(S_.ht_in, 16)

            def store_rows(i):
                sp.wait_ge(S_.x_in, 16)
                sp.wait_ge(S_.y_ok, i + 1)
                sp.dma_start(y_rows[bass.ds(i * P, P)], y_n).then_inc(S_.yr_out, 16)

            def load_expert(e, slot):
                for k, w in enumerate((w1, w2)):
                    sp.dma_start(w12[:, slot, k], w[bass.ds(e, 1)].rearrange("e (c p) n -> p (e c) n", p=P)).then_inc(S_.e_in, 16)
                sp.dma_start(w3_sb[:, slot, 0:NC - 1], w3[bass.ds(e, 1), 0:(NC - 1) * P].rearrange(
                    "e (n p) d -> p (e n) d", p=P)).then_inc(S_.e_in, 16)
                sp.dma_start(w3_sb[0:DE - (NC - 1) * P, slot, NC - 1], w3[bass.ds(e, 1), (NC - 1) * P:DE].rearrange(
                    "e p d -> p (e d)")).then_inc(S_.e_in, 16)

            load_tile(0)
            sp.dma_start(rc, r_consts).then_inc(S_.rc_in, 16)
            load_expert(0, 0)
            sp.wait_ge(S_.e_in, 64)
            load_expert(1, 1)
            for i in range(1, 4):
                sp.wait_ge(S_.y_mm, i)
                load_tile(i)
            with sp.Fori(4, NT) as i:
                store_rows(i - 4)
                sp.wait_ge(S_.x_in, 16)
                sp.wait_ge(S_.y_mm, i)
                load_tile(i)
            for i in range(NT - 4, NT):
                store_rows(i)

            sp.wait_ge(S_.tab_ok, 1)
            with sp.Fori(1, E // 2) as e2:
                for slot in range(2):
                    used = sp.value_load(tab_i[0:1, bass.ds(2 * ET + 2 * e2 + slot - 1, 1)], min_val=1, max_val=ET)
                    sp.wait_ge(S_.x_in, 16)
                    sp.wait_ge(S_.e_in, 64 * (2 * e2 + slot))
                    sp.wait_ge(S_.w3_mm, used)
                    load_expert(2 * e2 + slot, slot)
            for k in range(4):
                t = slice(k * NT // 4, (k + 1) * NT // 4)
                sp.wait_ge(S_.acc_ok, k + 1)
                sp.dma_start(out.rearrange("b (n p) d -> p (b n) d", p=P)[:, t], x_sb[:, t]).then_inc(S_.done, 16)
            sp.wait_ge(S_.done, 64)

        @block.tensor
        def _(pe):
            pe.wait_ge(S_.c_in, 256)
            for b in range(B):
                for c in range(DC):
                    for cc in range(DC):
                        pe.matmul(ps_o[:, (b * DC + c) * KC:(b * DC + c + 1) * KC], w_x_sb[:, 1, cc, c * P:(c + 1) * P],
                                  ctx_sb[:, cc, b * KC:(b + 1) * KC], start=cc == 0, stop=cc == DC - 1)
            for b in range(B):
                for cc in range(DC):
                    mm = pe.matmul(ps_o[0:KC, HALF + b * D:HALF + (b + 1) * D], ctx_sb[:, cc, b * KC:(b + 1) * KC],
                                   w_x_sb[:, 2, cc, :], start=cc == 0, stop=cc == DC - 1)
            mm.then_inc(S_.kv_mm, 1)
            pe.wait_ge(S_.xn_ok, 1)
            for n in range(NT // 4):
                for c in range(DC):
                    k = n * DC + c
                    if k >= 4:
                        pe.wait_ge(S_.xnt_ok, k - 3)
                    dst = ps_s[:, (k % 4) // 2, (k % 2) * 512:(k % 2) * 512 + 512]
                    for i in range(4):
                        mm = pe.transpose(dst[:, i * P:(i + 1) * P], xn[:, 4 * n + i, c * P:(c + 1) * P], ident)
                    mm.then_inc(S_.tr_ok, 1)
            pe.wait_ge(S_.xnt_ok, NT // 4 * DC)

            def project(g, p, par, k):
                tok = ((p >> 3) & 1) * T
                for th in range(2):
                    for c in range(DC):
                        mm = pe.matmul(ps_p[:, th * HALF:(th + 1) * HALF], w_head[:, par, c, k * P:(k + 1) * P],
                                       xn_t[:, c, bass.ds(tok + th * HALF, HALF)], start=c == 0, stop=c == DC - 1)
                mm.then_inc((S_.qk_proj, S_.vg_proj)[k], 1)

            def project_qk(g, p, par, first):
                pe.wait_ge((S_.w_even, S_.w_odd)[par], 16 * (p + 1))
                if not first:
                    pe.wait_ge(S_.v_ok, g - 1)
                project(g, p, par, 0)

            def square_norms(g):
                pe.wait_ge(S_.qk_ok, g + 1)
                pe.wait_ge(S_.sq_ok, g + 1)
                for th in range(2):
                    mm = pe.matmul(ps_p[64:128, th * HALF:(th + 1) * HALF], cst[:, C_SEL:C_SEL + 64],
                                   qk_sq[:, th * HALF:(th + 1) * HALF], start=True, stop=True)
                mm.then_inc(S_.norm_mm, 1)

            def project_vg(g, p, par, last):
                if last:
                    pe.wait_ge(S_.v_ok, g)
                else:
                    pe.wait_ge(S_.norms_ok, g + 2)
                project(g, p, par, 1)

            def turn_v(g, par):
                pe.wait_ge(S_.c_in, 256)
                pe.wait_ge(S_.vg_ok, g + 1)
                for b in range(SB):
                    mm = pe.transpose(ps_p[:, b * DH:(b + 1) * DH], vg[0:64, par, b * P:(b + 1) * P],
                                      cst[0:64, C_ID:C_ID + 64])
                mm.then_inc(S_.v_turned, 1)

            def distances(g, b, first):
                if b == 0:
                    pe.wait_ge(S_.split_ok, g + 1)
                    pe.wait_ge(S_.hi2_ok, 2 * g + 2)
                if not first or b >= 2:
                    pe.wait_ge(S_.max_ok, 8 * g + b - 1)
                for th in range(2):
                    t = slice(th * HALF, (th + 1) * HALF)
                    pe.matmul(ps_s[:, b % 2, t], ka[:, b * P:(b + 1) * P], qa[:, t], start=True, stop=False)
                    mm = pe.matmul(ps_s[:, b % 2, t], kb[:, b * P:(b + 1) * P], qb[:, t], start=False, stop=True)
                mm.then_inc(S_.s_ready, 1)

            def values(g, par, b, first):
                if b == 0:
                    pe.wait_ge(S_.v_ok, g + 1)
                    if first:
                        pe.wait_ge(S_.kv_ok, 1)
                    if not first:
                        pe.wait_ge(S_.oraw_ok, g)
                if b % 2 == 0:
                    pe.wait_ge(S_.w_ok, 4 * g + b // 2 + 1)
                for th in range(2):
                    t = slice(th * HALF, (th + 1) * HALF)
                    mm = pe.matmul(ps_o[:, t], v_aug[:, par, b, :], wts[:, par, b, t], start=b == 0, stop=b == SB - 1)
                if b == SB - 1:
                    mm.then_inc(S_.av_done, 1)

            def head(g, p, par, n, last=False):
                for b in range(SB):
                    distances(g, b, n == 0)
                    if b == 1 and not last:
                        project_qk(g + 1, p + par, 1 - par, n == 0)
                    if n >= 1 and 2 <= b <= 5:
                        values(g - 1, 1 - par, b - 2, n == 1)
                    if b == 3 and not last:
                        square_norms(g + 1)
                    if b == 4:
                        project_vg(g, p, par, last)
                if n >= 1:
                    values(g - 1, 1 - par, 4, False)
                turn_v(g, par)
                for b in range(5, SB):
                    if n >= 1:
                        values(g - 1, 1 - par, b, False)

            project_qk(0, 0, 0, True)
            square_norms(0)
            head(0, 0, 0, 0)
            head(1, 0, 1, 1)
            with pe.Fori(1, PAIRS - 1) as p:
                head(2 * p, p, 0, 2)
                head(2 * p + 1, p, 1, 2)
            head(G - 2, PAIRS - 1, 0, 2)
            head(G - 1, PAIRS - 1, 1, 2, last=True)
            for b in range(SB):
                values(G - 1, 1, b, False)

            bank_a, bank_b, bank_x = ps_o[:, 0:512], ps_o[:, 512:1024], ps_s[:, 1, 512:1024]

            def attn_out(i, part, n):
                if part == 0:
                    if n == 0:
                        pe.wait_ge(S_.oraw_ok, G)
                        pe.wait_ge(S_.wo_in, 16)
                    else:
                        pe.wait_ge(S_.x1_ok, i)
                    pe.wait_ge(S_.ht_in, 16 * (i + 1))
                for q in range(part * H // 4, (part + 1) * H // 4):
                    mm = pe.matmul(bank_a[:, 0:D], h_tile[:, q, :], w_o[:, q, :], start=q == 0, stop=q == H // 2 - 1)
                if part:
                    mm.then_inc(S_.y_mm, 1)

            def turn_x(i, n):
                pe.wait_ge(S_.xn2_ok, i + 1)
                if 1 <= n <= 2:
                    pe.wait_ge(S_.qt_ok, i)
                if n >= 3:
                    pe.wait_ge(S_.gl_ok, i - 2)
                for c in range(DC):
                    mm = pe.transpose(bank_b[:, c * P:(c + 1) * P], xn2[:, c * P:(c + 1) * P], ident)
                mm.then_inc(S_.xt_mm, 1)

            def query(i):
                pe.wait_ge(S_.xnt2_ok, i + 1)
                for c in range(DC):
                    for cc in range(DC):
                        mm = pe.matmul(bank_b[:, c * P:(c + 1) * P], w_x_sb[:, 0, cc, c * P:(c + 1) * P], xn2_t[:, cc, :],
                                       start=cc == 0, stop=cc == DC - 1)
                mm.then_inc(S_.q_mm, 1)

            def logits(i, n):
                pe.wait_ge(S_.qt_ok, i + 1)
                if n == 0:
                    pe.wait_ge(S_.max_ok, 8 * G)
                else:
                    pe.wait_ge(S_.l_ok, i)
                for bank, at, h, heads in LOGITS:
                    c, h0 = h // HPC, h % HPC
                    rhs = k_blk[:, bass.ds(((i >> 3) & 1) * DC + c, 1), h0:h0 + heads, :].rearrange("p a h k -> p (a h k)")
                    at = (bank % 2) * HALF + at * KC
                    mm = pe.matmul(ps_s[:, bank // 2, at:at + heads * KC], q_t[:, c, :], rhs, start=True, stop=True)
                mm.then_inc(S_.lg_mm, 1)

            def turn_p(i, k, n):
                if k == 0:
                    pe.wait_ge(S_.exp_ok, i + 1)
                if n >= 1 or k >= 2:
                    pe.wait_ge((S_.pta_ok, S_.ptd_ok)[k % 2], 2 * i + k // 2)
                for j in range(HPB):
                    mm = pe.transpose(ps_p[0:KC, (k % 2) * HALF + j * P:(k % 2) * HALF + (j + 1) * P], lg[:, HPB * k + j, :], ident)
                mm.then_inc(S_.pt_mm, 1)

            def x_values(i, n):
                if n >= 1:
                    pe.wait_ge(S_.x2_ok, i)
                pe.wait_ge(S_.pta_ok, 2 * i + 2)
                pe.wait_ge(S_.ptd_ok, 2 * i + 2)
                for h in range(XH):
                    mm = pe.matmul(bank_x[:, h * (XD + 1):(h + 1) * (XD + 1)], p_t[:, h, :],
                                   v_x[:, bass.ds((i >> 3) & 1, 1), h, :], start=True, stop=True)
                mm.then_inc(S_.avx_mm, 1)

            def turn_o(i):
                pe.wait_ge(S_.o_ok, i + 1)
                for c in range(DC):
                    mm = pe.transpose(bank_x[:, c * P:(c + 1) * P], o_x.rearrange("p h d -> p (h d)")[:, c * P:(c + 1) * P], ident)
                mm.then_inc(S_.ot_mm, 1)

            def x_out(i):
                pe.wait_ge(S_.ot_ok, i + 1)
                for c in range(DC):
                    mm = pe.matmul(bank_x[:, 0:D], o_t[:, c, :], w_x_sb[:, 3, c, :], start=c == 0, stop=c == DC - 1)
                mm.then_inc(S_.out_mm, 1)

            def turn_y(i, queries):
                pe.wait_ge(S_.y_ok, i + 1)
                if queries:
                    pe.wait_ge(S_.qt_ok, i + 3)
                for c in range(DC):
                    mm = pe.transpose(bank_b[:, c * P:(c + 1) * P], y_n[:, c * P:(c + 1) * P], ident)
                mm.then_inc(S_.yt_mm, 1)

            def gates(i):
                pe.wait_ge(S_.yt_ok, i + 1)
                for c in range(DC):
                    mm = pe.matmul(bank_b[:, 0:E], y_tile[:, c, :], gate_sb[:, c, :], start=c == 0, stop=c == DC - 1)
                mm.then_inc(S_.gl_mm, 1)

            def step(t, n, s1=True, s2=True, s3=True, s4=True):
                if s3:
                    turn_p(t - 2, 0, n - 2)
                    turn_p(t - 2, 1, n - 2)
                if s2:
                    turn_x(t - 1, n - 1)
                if s3:
                    turn_p(t - 2, 2, n - 2)
                    turn_p(t - 2, 3, n - 2)
                if s2:
                    query(t - 1)
                    logits(t - 1, n - 1)
                if s3:
                    x_values(t - 2, n - 2)
                if s1:
                    attn_out(t, 0, n)
                if s4:
                    turn_y(t - 3, s2)
                if s3:
                    turn_o(t - 2)
                if s1:
                    attn_out(t, 1, n)
                if s4:
                    gates(t - 3)
                if s3:
                    x_out(t - 2)

            for t in range(4):
                step(t, t, s2=t >= 1, s3=t >= 2, s4=t >= 3)
            with pe.Fori(4, NT) as t:
                step(t, 4)
            for t in range(NT, NT + 3):
                step(t, 4, s1=False, s2=t <= NT, s3=t <= NT + 1)

            pe.wait_ge(S_.rc_in, 16)
            pe.wait_ge(S_.a_ok, 1)
            pe.wait_ge(S_.l_ok, NT)
            rank = ps_s[:, 0, 0:(NT + 1) * E]
            a_flat = a17.rearrange("p n e -> p (n e)")
            pe.matmul(rank, rc[:, R_TRI:R_TRI + P], a_flat, start=True, stop=True)
            for j in range(1, NT + 1):
                mm = pe.matmul(rank[:, j * E:], rc[:, R_ONES:R_ONES + P], a_flat[:, 0:(NT + 1 - j) * E], start=False,
                               stop=True, skip_group_check=True)
            mm.then_inc(S_.rank_mm, 1)
            pe.wait_ge(S_.oh2_ok, 1)
            for r in range(2 * NT):
                mm = pe.matmul(ps_s[:, 0, 512:512 + ET], oh_lo[:, r], oh_hi[:, r], start=r == 0, stop=r == 2 * NT - 1)
            mm.then_inc(S_.tok_mm, 1)

            def turn_in(i, par, k):
                pe.wait_ge((S_.yg_even, S_.yg_odd)[par], 16 * (k + 1))
                if not (isinstance(i, int) and i == 0):
                    pe.wait_ge(S_.ytt_ok, i)
                for c in range(DC):
                    mm = pe.transpose(ps_o[:, c * P:(c + 1) * P], y_in[:, par, c * P:(c + 1) * P], ident)
                mm.then_inc(S_.yt2_mm, 1)

            def up_gate(i, par, j, slot, lead):
                if not lead:
                    pe.wait_ge(S_.hm_ok, 2 * i + j - 1)
                for k in range(2):
                    for c in range(DC):
                        mm = pe.matmul(ps_s[:, k, j * HALF:j * HALF + DEH], y_tt[:, par, c],
                                       w12[:, bass.ds(slot, 1), k, c, j * DEH:(j + 1) * DEH], start=c == 0, stop=c == DC - 1)
                mm.then_inc(S_.ug_mm, 1)

            def turn_h(i, par, lead):
                pe.wait_ge(S_.c_in, 256)
                pe.wait_ge(S_.hm_ok, 2 * i + 2)
                for n in range(NC):
                    m = min(P, DE - n * P)
                    if n == 0 and not lead:
                        pe.wait_ge(S_.hta_ok, i)
                    if n == 4 and not lead:
                        pe.wait_ge(S_.htd_ok, i)
                    mm = pe.transpose(ps_p[0:m, n * P:(n + 1) * P], h_sb[:, par, n * P:n * P + m], ident)
                    if n == 3:
                        mm.then_inc(S_.th_a, 1)
                mm.then_inc(S_.th_b, 1)

            def down(i, par, slot, lead):
                pe.wait_ge(S_.hta_ok, i + 1)
                pe.wait_ge(S_.htd_ok, i + 1)
                if not lead:
                    pe.wait_ge(S_.o_ok2, i)
                for n in range(NC):
                    m = min(P, DE - n * P)
                    mm = pe.matmul(ps_o[:, HALF:HALF + D], h_tt[0:m, par, n], w3_sb[0:m, bass.ds(slot, 1), n],
                                   start=n == 0, stop=n == NC - 1)
                mm.then_inc(S_.w3_mm, 1)

            def slot_of(i):
                return pe.value_load(tab_i[0:1, bass.ds(ET + i, 1)], min_val=0, max_val=1)

            def expert_tile(i, par, k, n, last=False):
                slot = slot_of(i)
                count = pe.value_load(tab_i[0:1, bass.ds(i, 1)], min_val=64, max_val=64 * E)
                pe.wait_ge(S_.e_in, count)
                pe.wait_ge(S_.ytt_ok, i + 1)
                up_gate(i, par, 0, slot, n == 0)
                if n >= 1:
                    turn_h(i - 1, 1 - par, n == 1)
                up_gate(i, par, 1, slot, n == 0)
                if not last:
                    turn_in(i + 1, 1 - par, k + par)
                if n >= 1:
                    down(i - 1, 1 - par, slot_of(i - 1), n == 1)

            pe.wait_ge(S_.tab_ok, 1)
            pe.wait_ge(S_.gl_ok, NT)
            pairs = pe.value_load(pairs_i[0:1, 0:1], min_val=NT - 2, max_val=ET // 2 - 2) + 2
            turn_in(0, 0, 0)
            expert_tile(0, 0, 0, 0)
            expert_tile(1, 1, 0, 1)
            with pe.Fori(1, pairs - 1) as k:
                expert_tile(2 * k, 0, k, 2)
                expert_tile(2 * k + 1, 1, k, 2)
            expert_tile(2 * pairs - 2, 0, pairs - 1, 2)
            expert_tile(2 * pairs - 1, 1, pairs - 1, 2, last=True)
            turn_h(2 * pairs - 1, 1, False)
            down(2 * pairs - 1, 1, slot_of(2 * pairs - 1), False)

        @block.vector
        def _(dve):
            dve.memset(zeros, 0.0).then_inc(S_.zero_ok, 1)
            dve.memset(eps_d[:], EPS_D)
            dve.memset(eps_ln[:], EPS_LN)
            dve.memset(eps_rms[:], EPS_RMS)
            dve.memset(v_x[:], 1.0)
            dve.memset(v_aug[:], 1.0).then_inc(S_.eps_ok, 1)
            dve.wait_ge(S_.x_in, 16)
            for i in range(NT):
                bn = dve.bn_stats(stats[:, i, :], x_sb[:, i, :])
            bn.then_inc(S_.stats_ok, 1)
            dve.wait_ge(S_.stats_ok, 1)
            for i in range(NT):
                bn = dve.bn_aggr(mean_var[:, i, :], stats[:, i, :])
            bn.then_inc(S_.aggr_ok, 1)
            dve.wait_ge(S_.std_ok, 1)
            dve.reciprocal(rstd[:], std[:]).then_inc(S_.rstd_ok, 1)
            dve.wait_ge(S_.rstd_ok, 1)
            for i in range(NT):
                bn = dve.tensor_scalar(xn[:, i, :], x_sb[:, i, :], mean_var[:, i, 0:1], rstd[:, i:i + 1],
                                       ALU.subtract, ALU.mult)
            bn.then_inc(S_.xn_ok, 1)
            for k in range(NT // 4 * DC):
                n, c = k // DC, k % DC
                dve.wait_ge(S_.tr_ok, k + 1)
                dve.tensor_copy(xn_t[:, c, n * 512:(n + 1) * 512],
                                ps_s[:, (k % 4) // 2, (k % 2) * 512:(k % 2) * 512 + 512]).then_inc(S_.xnt_ok, 1)
            dve.wait_ge(S_.c_in, 256)

            def head_of(p, par):
                return (p & (H // 2 - 1)) * 2 + par

            def copy_qk(g, p, par, first):
                dve.wait_ge(S_.qk_proj, g + 1)
                if not first:
                    dve.wait_ge(S_.hi2_ok, 2 * g)
                dve.tensor_scalar(qk[:], ps_p[:], b_qk[:, bass.ds(head_of(p, par), 1)], cst[:, C_SCALE:C_SCALE + 1],
                                  ALU.add, ALU.mult).then_inc(S_.qk_ok, 1)

            def split(g, first):
                if not first:
                    dve.wait_ge(S_.s_ready, 8 * g)
                dve.wait_ge(S_.qk_ok, g + 1)
                dve.tensor_copy(qa[0:64], qk[0:64])
                dve.tensor_copy(ka[64:128], qk[64:128]).then_inc(S_.hi_ok, 1)
                dve.wait_ge(S_.hi_ok, g + 1)
                dve.tensor_tensor(qa[64:128], qk[0:64], qa[0:64], ALU.subtract)
                dve.tensor_tensor(kb[0:64], qk[64:128], ka[64:128], ALU.subtract)

            def copy_norms(g):
                dve.wait_ge(S_.norm_mm, g + 1)
                dve.tensor_scalar(norms[64:128], ps_p[64:128], cst[64:128, C_ONE:C_ONE + 1], None,
                                  ALU.add).then_inc(S_.norms_ok, 1)
                dve.wait_ge(S_.norms_ok, g + 1)
                dve.tensor_copy(norms_hi[64:128], norms[64:128]).then_inc(S_.norms_hi_ok, 1)

            def low_norms(g):
                dve.wait_ge(S_.norms_hi_ok, g + 1)
                dve.scalar_tensor_tensor(out=qb[64:96], in0=norms_hi[64:96].bitcast(F32), scalar=cst[64:96, C_LO:C_LO + 1],
                                         in1=norms[64:96], op0=ALU.mult, op1=ALU.add)
                dve.scalar_tensor_tensor(out=kb[64:96], in0=norms_hi[96:128].bitcast(F32), scalar=cst[96:128, C_LO:C_LO + 1],
                                         in1=norms[96:128], op0=ALU.mult, op1=ALU.add).then_inc(S_.split_ok, 1)

            def copy_vg(g, p, par, n):
                dve.wait_ge(S_.vg_proj, g + 1)
                if n >= 2:
                    dve.wait_ge(S_.gr_ok, g - 1)
                dve.tensor_scalar(vg[:, par], ps_p[:], b_vg[:, bass.ds(head_of(p, par), 1)], None, ALU.add).then_inc(S_.vg_ok, 1)

            def copy_v(g, par):
                dve.wait_ge(S_.v_turned, g + 1)
                dve.tensor_copy(v_aug[:, par, :, v_rows(par)],
                                ps_p[:, 0:SB * DH].rearrange("p (b d) -> p b d", d=DH)).then_inc(S_.v_ok, 1)

            def copy_values(g):
                dve.wait_ge(S_.av_done, g + 1)
                dve.tensor_copy(o_raw[:], ps_o[:]).then_inc(S_.oraw_ok, 1)

            def guard(g, par, b):
                dve.wait_ge(S_.s_ready, 8 * g + b + 1)
                dve.tensor_scalar(wts[:, par, b, :], ps_s[:, b % 2, :], 0.0, None, ALU.max).then_inc(S_.max_ok, 1)

            def gate(g, p, par, first):
                dve.wait_ge(S_.gr_ok, g + 1)
                if par == 0 and not first:
                    dve.wait_ge(S_.h_out, 16 * p)
                dve.tensor_tensor(h_pair[v_rows(par)], o_raw[v_rows(par)], g_r[64:128], ALU.mult).then_inc(S_.h_ok, 1)

            def head(g, p, par, n, last=False):
                if n >= 2:
                    copy_values(g - 2)
                for b in range(SB):
                    guard(g, par, b)
                    if b == 1 and not last:
                        copy_qk(g + 1, p + par, 1 - par, False)
                    if b == 3 and not last:
                        copy_norms(g + 1)
                    if b == 4:
                        copy_vg(g, p, par, n)
                        if n >= 2:
                            gate(g - 2, p - 1, par, False if not isinstance(p, int) else p == 1)
                if not last:
                    split(g + 1, False)
                    low_norms(g + 1)
                copy_v(g, par)

            def context():
                dve.tensor_scalar(mask_f[:].rearrange("p b k -> p (b k)"), mask_i[:], NEG, None, ALU.mult)
                dve.wait_ge(S_.kv_mm, 1)
                for b in range(B):
                    for c in range(DC):
                        kk = dve.tensor_scalar(k_raw[:, b * DC + c], ps_o[:, (b * DC + c) * KC:(b * DC + c + 1) * KC],
                                               b_qk_x[:, DC + c:DC + c + 1], None, ALU.add)
                kk.then_inc(S_.k_ok, 1)
                dve.wait_ge(S_.k_ok, 1)
                for bc in range(B * DC):
                    dve.tensor_tensor(k_blk[:, bc], k_raw[:, bc].unsqueeze(1).broadcast_to([P, HPC, KC]),
                                      cst[:, C_HM:C_HM + HPC].unsqueeze(2).broadcast_to([P, HPC, KC]), ALU.mult)
                for b in range(B):
                    vv = dve.tensor_tensor(v_x[:, b, :, 0:XD], ps_o[0:KC, HALF + b * D:HALF + (b + 1) * D].rearrange("p (h d) -> p h d", d=XD),
                                           brow[0:KC, 1].rearrange("p (h d) -> p h d", d=XD), ALU.add)
                vv.then_inc(S_.kv_ok, 1)

            copy_qk(0, 0, 0, True)
            split(0, True)
            copy_norms(0)
            low_norms(0)
            context()
            head(0, 0, 0, 0)
            dve.wait_ge(S_.zero_out, 16)
            head(1, 0, 1, 1)
            head(2, 1, 0, 2)
            head(3, 1, 1, 2)
            with dve.Fori(2, PAIRS - 1) as p:
                head(2 * p, p, 0, 2)
                head(2 * p + 1, p, 1, 2)
            head(G - 2, PAIRS - 1, 0, 2)
            head(G - 1, PAIRS - 1, 1, 2, last=True)
            for par in range(2):
                dve.wait_ge(S_.h_ok, G - 2 + par)
                copy_values(G - 2 + par)
                gate(G - 2 + par, PAIRS - 1, par, False)

            bank_a, bank_b, bank_x = ps_o[:, 0:512], ps_o[:, 512:1024], ps_s[:, 1, 512:1024]

            def xt(i):
                return x_sb[:, bass.ds(i, 1), :].rearrange("p a d -> p (a d)")

            def residual(i, n):
                dve.wait_ge(S_.y_mm, i + 1)
                if n == 0:
                    dve.wait_ge(S_.xb_ok, 1)
                else:
                    dve.wait_ge(S_.x1b_ok, i)
                dve.tensor_tensor(x1s[:], xt(i), bank_a[:, 0:D], ALU.add).then_inc(S_.x1_ok, 1)
                dve.wait_ge(S_.x1_ok, i + 1)
                dve.bn_stats(st2[:, 0, :], x1s[:]).then_inc(S_.st_ok, 1)
                dve.wait_ge(S_.xb_ok, 1)
                if n >= 1:
                    dve.wait_ge(S_.r1_ok, i)
                dve.wait_ge(S_.st_ok, i + 1)
                dve.bn_aggr(mv2[:, 0, :], st2[:, 0, :]).then_inc(S_.mv_ok, 1)

            def norm_x(i, n):
                dve.wait_ge(S_.r1_ok, i + 1)
                dve.wait_ge(S_.mv_ok, i + 1)
                if n >= 1:
                    dve.wait_ge(S_.xt_mm, i)
                dve.tensor_scalar(xn2, x1s[:], mv2[:, 0, 0:1], r2[:, 0:1], ALU.subtract, ALU.mult).then_inc(S_.xn2_ok, 1)

            def copy_xt(i):
                dve.wait_ge(S_.xt_mm, i + 1)
                dve.tensor_copy(xn2_t.rearrange("p c t -> p (c t)"), bank_b[:, 0:D]).then_inc(S_.xnt2_ok, 1)

            def copy_q(i):
                dve.wait_ge(S_.q_mm, i + 1)
                for c in range(DC):
                    q = dve.tensor_scalar(q_t[:, c], bank_b[:, c * P:(c + 1) * P], b_qk_x[:, c:c + 1], XD ** -0.5, ALU.add, ALU.mult)
                q.then_inc(S_.qt_ok, 1)

            def mask_max(i, n):
                dve.wait_ge(S_.lg_mm, i + 1)
                if n >= 1:
                    dve.wait_ge(S_.pt_mm, 4 * i)
                m = mask_f[:, bass.ds((i >> 3) & 1, 1), :]
                for bank, h, heads in LBANKS:
                    at = (bank % 2) * HALF
                    q = dve.tensor_tensor(lg[:, h:h + heads, :],
                                          ps_s[:, bank // 2, at:at + heads * KC].rearrange("p (h k) -> p h k", k=KC),
                                          m.broadcast_to([P, heads, KC]), ALU.add)
                q.then_inc(S_.l_ok, 1)
                dve.wait_ge(S_.l_ok, i + 1)
                if n >= 1:
                    dve.wait_ge(S_.sub_ok, i)
                dve.tensor_reduce(lmax[:], lg, AX.X, ALU.max).then_inc(S_.lmax_ok, 1)

            def probs_t(i, k, n):
                dve.wait_ge(S_.pt_mm, 4 * i + k + 1)
                if n >= 1:
                    dve.wait_ge(S_.avx_mm, i)
                dve.tensor_copy(p_t[:, HPB * k:HPB * (k + 1), :].rearrange("p h t -> p (h t)"),
                                ps_p[0:KC, HALF:2 * HALF]).then_inc(S_.ptd_ok, 1)

            def divide(i):
                dve.wait_ge(S_.avx_mm, i + 1)
                av = bank_x[:, 0:XH * (XD + 1)].rearrange("p (h d) -> p h d", d=XD + 1)
                dve.reciprocal(den[:], av[:, :, XD]).then_inc(S_.den_ok, 1)
                dve.wait_ge(S_.den_ok, i + 1)
                dve.tensor_tensor(o_x, av[:, :, 0:XD], den[:].unsqueeze(2).broadcast_to([P, XH, XD]), ALU.mult).then_inc(S_.o_ok, 1)

            def copy_o(i):
                dve.wait_ge(S_.ot_mm, i + 1)
                dve.tensor_copy(o_t.rearrange("p c t -> p (c t)"), bank_x[:, 0:D]).then_inc(S_.ot_ok, 1)

            def residual2(i, n):
                dve.wait_ge(S_.out_mm, i + 1)
                if n >= 1:
                    dve.wait_ge(S_.base_ok, i)
                dve.wait_ge(S_.x1b_ok, i + 1)
                dve.tensor_tensor(x2s[:], xt(i), bank_x[:, 0:D], ALU.add).then_inc(S_.x2_ok, 1)
                dve.wait_ge(S_.x2_ok, i + 1)
                dve.bn_stats(st2[:, 1, :], x2s[:]).then_inc(S_.st2_ok, 1)

            def moments2(i):
                dve.wait_ge(S_.xb_ok, 1)
                dve.wait_ge(S_.st2_ok, i + 1)
                dve.bn_aggr(mv2[:, 1, :], st2[:, 1, :]).then_inc(S_.mv2_ok, 1)

            def norm_x2(i, n):
                dve.wait_ge(S_.r2_ok, i + 1)
                if n >= 1:
                    dve.wait_ge(S_.base_ok, i)
                dve.tensor_scalar(xin, x2s[:], mv2[:, 1, 0:1], r2[:, 1:2], ALU.subtract, ALU.mult).then_inc(S_.xin_ok, 1)

            def expert_in(i, n):
                dve.wait_ge(S_.r3_ok, i + 1)
                if n >= 1:
                    dve.wait_ge(S_.yr_out, 16 * i)
                dve.scalar_tensor_tensor(out=y_n, in0=xin, scalar=r2[:, 2:3], in1=brow[:, 3], op0=ALU.mult,
                                         op1=ALU.mult).then_inc(S_.y_ok, 1)

            def copy_y(i):
                dve.wait_ge(S_.yt_mm, i + 1)
                dve.tensor_copy(y_tile.rearrange("p c t -> p (c t)"), bank_b[:, 0:D]).then_inc(S_.yt_ok, 1)

            def copy_gates(i):
                dve.wait_ge(S_.gl_mm, i + 1)
                dve.tensor_copy(gl[:, bass.ds(i, 1), :].rearrange("p a e -> p (a e)"), bank_b[:, 0:E]).then_inc(S_.gl_ok, 1)

            def step(t, n, s1=True, s2=True, s3=True, s4=True):
                if s3:
                    probs_t(t - 2, 1, n - 2)
                if s2:
                    copy_xt(t - 1)
                if s4:
                    norm_x2(t - 3, n - 3)
                if s3:
                    probs_t(t - 2, 3, n - 2)
                if s2:
                    copy_q(t - 1)
                if s4:
                    expert_in(t - 3, n - 3)
                if s2:
                    mask_max(t - 1, n - 1)
                if s3:
                    divide(t - 2)
                if s4:
                    copy_y(t - 3)
                if s3:
                    copy_o(t - 2)
                if s1:
                    residual(t, n)
                if s4:
                    copy_gates(t - 3)
                if s3:
                    residual2(t - 2, n - 2)
                if s1:
                    norm_x(t, n)
                if s3:
                    moments2(t - 2)

            for t in range(4):
                step(t, t, s2=t >= 1, s3=t >= 2, s4=t >= 3)
            with dve.Fori(4, NT) as t:
                step(t, 4)
            for t in range(NT, NT + 3):
                step(t, 4, s1=False, s2=t <= NT, s3=t <= NT + 1)

            dve.wait_ge(S_.gl_ok, NT)
            for i in range(NT):
                q = dve.max(top[:, i, :], gl[:, i, :])
            q.then_inc(S_.top_ok, 1)
            dve.wait_ge(S_.top_ok, 1)
            dve.tensor_tensor(pw[:, 0], top[:, :, 1], top[:, :, 0], ALU.subtract).then_inc(S_.dlt_ok, 1)
            for i in range(NT):
                q = dve.max_index(top_i[:, i, :], top[:, i, :], gl[:, i, :])
            q.then_inc(S_.topi_ok, 1)
            dve.wait_ge(S_.topi_ok, 1)
            dve.tensor_copy(top_f[:], top_i[:, :, 0:2]).then_inc(S_.topf_ok, 1)
            dve.wait_ge(S_.pe_ok, 1)
            dve.tensor_scalar(pw[:, 2], pw[:, 1], 1.0, None, ALU.add).then_inc(S_.pw_ok, 1)
            dve.wait_ge(S_.pw_ok, 1)
            dve.reciprocal(pw[:, 3], pw[:, 2]).then_inc(S_.pw_ok, 1)
            dve.wait_ge(S_.pw_ok, 2)
            dve.tensor_tensor(pw[:, 4], pw[:, 3], pw[:, 1], ALU.mult).then_inc(S_.pw_ok, 1)
            dve.wait_ge(S_.topf_ok, 1)
            for k in range(2):
                q = dve.tensor_tensor(w_full[:, k], cst[:, C_IOTA:C_IOTA + E].unsqueeze(1).broadcast_to([P, NT, E]),
                                      top_f[:, :, k:k + 1].broadcast_to([P, NT, E]), ALU.is_equal)
            q.then_inc(S_.oh_ok, 1)
            dve.wait_ge(S_.oh_ok, 1)
            dve.memset(a17[:, NT], 0.0)
            dve.tensor_tensor(a17[:, 0:NT], w_full[:, 0], w_full[:, 1], ALU.add).then_inc(S_.a_ok, 1)
            dve.wait_ge(S_.rc_in, 16)
            dve.wait_ge(S_.rank_mm, 1)
            dve.tensor_tensor(over, ps_s[:, 0, NT * E:(NT + 1) * E].unsqueeze(2).broadcast_to([P, E, NT]),
                              rc[:, R_STEP:R_STEP + NT].unsqueeze(1).broadcast_to([P, E, NT]), ALU.is_gt).then_inc(S_.rt_ok, 1)
            dve.wait_ge(S_.rt_ok, 1)
            dve.tensor_reduce(nt_e, over, AX.X, ALU.add).then_inc(S_.rt_ok, 1)
            dve.wait_ge(S_.rt_ok, 2)
            dve.tensor_tensor(ex_t, nt_e.unsqueeze(1).broadcast_to([P, 9, E]),
                              rc[:, R_EXCL:R_EXCL + 9 * E].rearrange("p (k e) -> p k e", e=E), ALU.mult).then_inc(S_.rt_ok, 1)
            dve.wait_ge(S_.rt_ok, 3)
            dve.tensor_reduce(starts, ex_t, AX.X, ALU.add).then_inc(S_.rt_ok, 1)
            dve.wait_ge(S_.rt_ok, 4)
            dve.tensor_scalar(st128, starts[:, 0:E], float(P), None, ALU.mult).then_inc(S_.rt_ok, 1)
            dve.tensor_tensor(past, rc[:, R_TILE:R_TILE + ET].unsqueeze(2).broadcast_to([P, ET, E - 1]),
                              starts[:, 1:E].unsqueeze(1).broadcast_to([P, ET, E - 1]), ALU.is_ge).then_inc(S_.rt_ok, 1)
            dve.wait_ge(S_.rt_ok, 5)
            dve.tensor_tensor(base, ps_s[:, 0, 0:NT * E].rearrange("p (n e) -> p n e", e=E),
                              st128.unsqueeze(1).broadcast_to([P, NT, E]), ALU.add).then_inc(S_.rt_ok, 1)
            dve.wait_ge(S_.rt_ok, 7)
            dve.tensor_reduce(tab_f[:, 0:ET], past, AX.X, ALU.add).then_inc(S_.rt_ok, 1)
            dve.tensor_tensor(pick, w_full[:, 0], base, ALU.mult).then_inc(S_.rt_ok, 1)
            dve.wait_ge(S_.rt_ok, 9)
            dve.tensor_scalar(tab_f[:, 0:ET], tab_f[:, 0:ET], 1.0, 64.0, ALU.add, ALU.mult)
            dve.tensor_tensor(past, past, rc[:, R_SIGN:R_SIGN + E - 1].unsqueeze(1).broadcast_to([P, ET, E - 1]), ALU.mult)
            dve.tensor_reduce(slot_f[:, 0:NT], pick, AX.X, ALU.add).then_inc(S_.rt_ok, 1)
            dve.wait_ge(S_.rt_ok, 10)
            dve.tensor_reduce(tab_f[:, ET:2 * ET], past, AX.X, ALU.add)
            dve.tensor_copy(tab_f[:, 2 * ET:2 * ET + 9], starts)
            dve.tensor_scalar(tab_f[:, 2 * ET + 9:], starts[:, E:E + 1], -3.0, None, ALU.add)
            dve.tensor_tensor(pick, w_full[:, 1], base, ALU.mult).then_inc(S_.rt_ok, 1)
            dve.wait_ge(S_.rt_ok, 11)
            dve.tensor_reduce(slot_f[:, NT:], pick, AX.X, ALU.add).then_inc(S_.rt_ok, 1)
            dve.tensor_copy(tab_i[:], tab_f).then_inc(S_.rt_ok, 1)
            dve.wait_ge(S_.rt_ok, 13)
            dve.tensor_scalar(pairs_i[:], tab_i[:, 2 * ET + 9:], 1, None, ALU.logical_shift_right).then_inc(S_.tab_ok, 1)
            dve.tensor_copy(slot_i[:], slot_f).then_inc(S_.slot_ok, 1)
            dve.wait_ge(S_.slot_ok, 1)
            dve.tensor_scalar(hl_i[:, 0:2 * NT], slot_i[:], P.bit_length() - 1, None, ALU.logical_shift_right)
            dve.tensor_scalar(hl_i[:, 2 * NT:], slot_i[:], P - 1, None, ALU.bitwise_and).then_inc(S_.hl_ok, 1)
            dve.wait_ge(S_.hl_ok, 1)
            dve.tensor_copy(hl_f, hl_i[:]).then_inc(S_.hl_ok, 1)
            dve.wait_ge(S_.hl_ok, 2)
            dve.tensor_tensor(oh_hi, rc[:, R_TILE:R_TILE + ET].unsqueeze(1).broadcast_to([P, 2 * NT, ET]),
                              hl_f[:, 0:2 * NT].unsqueeze(2).broadcast_to([P, 2 * NT, ET]), ALU.is_equal).then_inc(S_.hl_ok, 1)
            dve.tensor_tensor(oh_lo, rc[:, R_POS:R_POS + P].unsqueeze(1).broadcast_to([P, 2 * NT, P]),
                              hl_f[:, 2 * NT:].unsqueeze(2).broadcast_to([P, 2 * NT, P]), ALU.is_equal)
            dve.wait_ge(S_.hl_ok, 3)
            for k in range(2):
                q = dve.tensor_tensor(oh_hi[:, k * NT:(k + 1) * NT], oh_hi[:, k * NT:(k + 1) * NT],
                                      rc[:, R_TOK:R_TOK + NT].unsqueeze(2).broadcast_to([P, NT, ET]), ALU.mult)
            q.then_inc(S_.oh2_ok, 1)
            dve.wait_ge(S_.tok_mm, 1)
            dve.tensor_copy(tok_i[:], ps_s[:, 0, 512:512 + ET]).then_inc(S_.tok_ok, 1)

            def copy_in(i, par, n):
                dve.wait_ge(S_.yt2_mm, i + 1)
                if n >= 2:
                    dve.wait_ge(S_.ug_mm, 2 * i - 2)
                dve.tensor_copy(y_tt[:, par].rearrange("p c t -> p (c t)"), ps_o[:, 0:D]).then_inc(S_.ytt_ok, 1)

            def gated(i, par, j, n):
                dve.wait_ge(S_.silu_ok, 2 * i + j + 1)
                if j == 0 and n >= 2:
                    dve.wait_ge(S_.th_b, i - 1)
                t = slice(j * DEH, (j + 1) * DEH)
                dve.tensor_tensor(h_sb[:, par, t], s_up[:, t], ps_s[:, 1, j * HALF:j * HALF + DEH], ALU.mult).then_inc(S_.hm_ok, 1)

            def copy_h(i, par, n):
                dve.wait_ge(S_.th_b, i + 1)
                if n >= 2:
                    dve.wait_ge(S_.w3_mm, i - 1)
                m = DE - (NC - 1) * P
                dve.tensor_copy(h_tt[:, par, 4], ps_p[:, 4 * P:5 * P])
                dve.tensor_copy(h_tt[0:m, par, 5], ps_p[0:m, 5 * P:6 * P]).then_inc(S_.htd_ok, 1)

            def expert_tile(i, par, n, last=False):
                gated(i, par, 0, n)
                if n >= 1:
                    copy_h(i - 1, 1 - par, n - 1)
                gated(i, par, 1, n)
                if not last:
                    copy_in(i + 1, 1 - par, n + 1)

            copy_in(0, 0, 0)
            expert_tile(0, 0, 0)
            expert_tile(1, 1, 1)
            expert_tile(2, 0, 2)
            expert_tile(3, 1, 3)
            dve.wait_ge(S_.tab_ok, 1)
            pairs = dve.value_load(pairs_i[0:1, 0:1], min_val=NT - 2, max_val=ET // 2 - 2) + 2
            with dve.Fori(2, pairs - 1) as k:
                expert_tile(2 * k, 0, 3)
                expert_tile(2 * k + 1, 1, 3)
            expert_tile(2 * pairs - 2, 0, 3)
            expert_tile(2 * pairs - 1, 1, 3, last=True)
            copy_h(2 * pairs - 1, 1, 3)
            dve.wait_ge(S_.slot_ok, 1)
            dve.wait_ge(S_.os_even, 16 * pairs)
            dve.wait_ge(S_.os_odd, 16 * pairs)
            dve.tensor_copy(slot_n[:], slot_i[:]).then_inc(S_.slotn_ok, 1)

            dve.wait_ge(S_.base_ok, NT)
            dve.wait_ge(S_.pw_ok, 3)
            for c in range(4):
                dve.wait_ge((S_.og0, S_.og1, S_.og2, S_.og3)[c], 16 * 2 * NT // 4)
                for k in range(2):
                    for i in range(c * NT // 4, (c + 1) * NT // 4):
                        q = dve.scalar_tensor_tensor(out=x_sb[:, i], in0=o_tok[:, k, i], scalar=pw[:, 3 + k, i:i + 1],
                                                     in1=x_sb[:, i], op0=ALU.mult, op1=ALU.add)
                    q.then_inc(S_.sum_ok if k == 0 else S_.acc_ok, 1)
                    if k == 0:
                        dve.wait_ge(S_.sum_ok, c + 1)

        @block.scalar
        def _(act):
            act.wait_ge(S_.eps_ok, 1)
            act.wait_ge(S_.aggr_ok, 1)
            act.activation(std[:], mean_var[:, :, 1], ACT.Sqrt, bias=eps_ln[:, 0:1]).then_inc(S_.std_ok, 1)

            def chunk(par, c):
                return wts[:, par, 2 * c:2 * c + 2, :].rearrange("p b t -> p (b t)")

            def rows(g, par, first):
                act.wait_ge(S_.oraw_ok, g + 1)
                if not first:
                    act.wait_ge(S_.gr_ok, g)
                act.activation(rinv[64:128], o_raw[rs_rows(par)], ACT.Ln, bias=eps_d[rs_rows(par), 0:1]).then_inc(S_.rln_ok, 1)
                act.wait_ge(S_.rln_ok, g + 1)
                act.activation(rinv[64:128], rinv[64:128], ACT.Exp, scale=-1.0).then_inc(S_.r_ok, 1)

            def head(g, par, n):
                for c in range(4):
                    act.wait_ge(S_.max_ok, 8 * g + 2 * c + 2)
                    act.activation(chunk(par, c), chunk(par, c), ACT.Sqrt).then_inc(S_.sqrt_ok, 1)
                act.preload_act_table_set("natural_log_exp_and_others")

                def ln(c):
                    act.wait_ge(S_.sqrt_ok, 4 * g + c + 1)
                    act.activation(chunk(par, c), chunk(par, c), ACT.Ln, bias=eps_d[:, 0:1]).then_inc(S_.ln_ok, 1)

                def exp(c):
                    act.wait_ge(S_.ln_ok, 4 * g + c + 1)
                    act.activation(chunk(par, c), chunk(par, c), ACT.Exp, scale=-2.0).then_inc(S_.w_ok, 1)

                ln(0)
                for c in range(4):
                    if c < 3:
                        ln(c + 1)
                    if n >= 1 and c == 3:
                        rows(g - 1, 1 - par, n == 1)
                    exp(c)
                if n >= 1 and 3 == 4:
                    rows(g - 1, 1 - par, n == 1)

            head(0, 0, 0)
            head(1, 1, 1)
            with act.Fori(1, PAIRS) as p:
                head(2 * p, 0, 2)
                head(2 * p + 1, 1, 2)
            rows(G - 1, 1, False)

            def probs_t(i, k, n):
                act.wait_ge(S_.pt_mm, 4 * i + k + 1)
                if n >= 1:
                    act.wait_ge(S_.avx_mm, i)
                act.activation(p_t[:, HPB * k:HPB * (k + 1), :].rearrange("p h t -> p (h t)"), ps_p[0:KC, 0:HALF],
                               ACT.Copy).then_inc(S_.pta_ok, 1)

            def rstd_of(i, src, dst, scale, eps, logged, ready):
                act.activation(dst, src, ACT.Ln, bias=eps[:, 0:1], scale=scale).then_inc(logged, 1)
                act.wait_ge(logged, i + 1)
                act.activation(dst, dst, ACT.Exp, scale=-0.5).then_inc(ready, 1)

            def step(t, n, s1=True, s2=True, s3=True, s4=True):
                if s3:
                    probs_t(t - 2, 0, n - 2)
                if s4:
                    i = t - 3
                    act.wait_ge(S_.mv2_ok, i + 1)
                    if n >= 4:
                        act.wait_ge(S_.xin_ok, i)
                    rstd_of(i, mv2[:, 1, 1:2], r2[:, 1:2], 1.0, eps_ln, S_.lr2, S_.r2_ok)
                if s3:
                    probs_t(t - 2, 2, n - 2)
                if s4:
                    act.wait_ge(S_.xin_ok, i + 1)
                    if n >= 4:
                        act.wait_ge(S_.y_ok, i)
                    act.activation(sq_junk, xin, ACT.Square, accum_out=r2[:, 3:4]).then_inc(S_.ms_ok, 1)
                    act.wait_ge(S_.ms_ok, i + 1)
                    rstd_of(i, r2[:, 3:4], r2[:, 2:3], 1.0 / D, eps_rms, S_.lr3, S_.r3_ok)
                if s2:
                    act.wait_ge(S_.sub_ok, t)
                    act.activation(lg, lg, ACT.Exp).then_inc(S_.exp_ok, 1)
                if s1:
                    act.wait_ge(S_.mv_ok, t + 1)
                    if n >= 1:
                        act.wait_ge(S_.xn2_ok, t)
                    rstd_of(t, mv2[:, 0, 1:2], r2[:, 0:1], 1.0, eps_ln, S_.lr1, S_.r1_ok)

            for t in range(4):
                step(t, t, s2=t >= 1, s3=t >= 2, s4=t >= 3)
            with act.Fori(4, NT) as t:
                step(t, 4)
            for t in range(NT, NT + 3):
                step(t, 4, s1=False, s2=t <= NT, s3=t <= NT + 1)

            act.wait_ge(S_.dlt_ok, 1)
            act.activation(pw[:, 1], pw[:, 0], ACT.Exp).then_inc(S_.pe_ok, 1)

            def silu(i, j, n):
                act.wait_ge(S_.ug_mm, 2 * i + j + 1)
                if n >= 1:
                    act.wait_ge(S_.hm_ok, 2 * i + j - 1)
                act.activation(s_up[:, j * DEH:(j + 1) * DEH], ps_s[:, 0, j * HALF:j * HALF + DEH],
                               ACT.Silu).then_inc(S_.silu_ok, 1)

            def copy_h(i, par, n):
                act.wait_ge(S_.th_a, i + 1)
                if n >= 2:
                    act.wait_ge(S_.w3_mm, i - 1)
                act.activation(h_tt[:, par, 0:4].rearrange("p n t -> p (n t)"), ps_p[:, 0:4 * P], ACT.Copy).then_inc(S_.hta_ok, 1)

            def copy_out(i, par, k, n):
                act.wait_ge(S_.w3_mm, i + 1)
                if n >= 2:
                    act.wait_ge((S_.os_even, S_.os_odd)[par], 16 * k)
                act.activation(o_sb[:, par], ps_o[:, HALF:HALF + D], ACT.Copy).then_inc(S_.o_ok2, 1)

            def expert_tile(i, par, k, n):
                silu(i, 0, n)
                if n >= 1:
                    copy_h(i - 1, 1 - par, n - 1)
                silu(i, 1, n)
                if n >= 1:
                    copy_out(i - 1, 1 - par, k if par else k - 1, n - 1)

            expert_tile(0, 0, 0, 0)
            expert_tile(1, 1, 0, 1)
            expert_tile(2, 0, 1, 2)
            expert_tile(3, 1, 1, 3)
            act.wait_ge(S_.tab_ok, 1)
            pairs = act.value_load(pairs_i[0:1, 0:1], min_val=NT - 2, max_val=ET // 2 - 2) + 2
            with act.Fori(2, pairs) as k:
                expert_tile(2 * k, 0, k, 3)
                expert_tile(2 * k + 1, 1, k, 3)
            copy_h(2 * pairs - 1, 1, 3)
            copy_out(2 * pairs - 1, 1, pairs - 1, 3)

        @block.gpsimd
        def _(pool):
            unit = cst[:, C_UNIT:C_UNIT + 1].broadcast_to([P, T])

            def squares(g, first):
                pool.wait_ge(S_.qk_ok, g + 1)
                if not first:
                    pool.wait_ge(S_.hi2_ok, 2 * g)
                    pool.wait_ge(S_.norm_mm, g)
                pool.tensor_tensor(qk_sq[:], qk[:], qk[:], ALU.mult).then_inc(S_.sq_ok, 1)

            def gate_rows(g, par, first, after):
                pool.wait_ge(S_.sq_ok, after)
                pool.wait_ge(S_.r_ok, g + 1)
                if not first:
                    pool.wait_ge(S_.h_ok, g)
                pool.tensor_tensor(g_r[64:128], vg[64:128, par], rinv[64:128], ALU.mult).then_inc(S_.gr_ok, 1)

            def high(g, first, after_gate):
                if after_gate:
                    pool.wait_ge(S_.gr_ok, g - 2)
                else:
                    pool.wait_ge(S_.sq_ok, g + 1)
                if not first:
                    pool.wait_ge(S_.s_ready, 8 * g)
                pool.tensor_tensor(qb[0:64], qk[0:64], unit[0:64], ALU.mult).then_inc(S_.hi2_ok, 1)
                pool.wait_ge(S_.hi2_ok, 2 * g + 1)
                pool.tensor_tensor(ka[0:64], qk[64:128], unit[64:128], ALU.mult).then_inc(S_.hi2_ok, 1)

            pool.wait_ge(S_.xn_ok, 1)
            pool.wait_ge(S_.c_in, 256)
            pool.tensor_tensor(x_sb[:], x_sb[:], brow[:, 0:1].broadcast_to([P, NT, D]), ALU.add).then_inc(S_.xb_ok, 1)
            for g in range(3):
                squares(g, g == 0)
                high(g, g == 0, False)
            squares(3, False)
            gate_rows(0, 0, True, 4)
            high(3, False, True)
            squares(4, False)
            gate_rows(1, 1, False, 5)
            high(4, False, True)
            with pool.Fori(2, PAIRS - 1) as p:
                for par in range(2):
                    g = 2 * p + par
                    squares(g + 1, False)
                    gate_rows(g - 2, par, False, g + 2)
                    high(g + 1, False, True)
            squares(G - 1, False)
            gate_rows(G - 4, 0, False, G)
            high(G - 1, False, True)
            gate_rows(G - 3, 1, False, G)
            gate_rows(G - 2, 0, False, G)
            gate_rows(G - 1, 1, False, G)

            def step(t, s1=True, s2=True, s4=True):
                if s4:
                    i = t - 3
                    x2 = x_sb[:, bass.ds(i, 1), :].rearrange("p a d -> p (a d)")
                    pool.wait_ge(S_.xin_ok, i + 1)
                    pool.tensor_tensor(x2, x2s[:], xin, ALU.add).then_inc(S_.base_ok, 1)
                if s2:
                    pool.wait_ge(S_.lmax_ok, t)
                    pool.tensor_tensor(lg, lg, lmax[:].unsqueeze(2).broadcast_to([P, XH, KC]), ALU.subtract).then_inc(S_.sub_ok, 1)
                if s1:
                    x1 = x_sb[:, bass.ds(t, 1), :].rearrange("p a d -> p (a d)")
                    pool.wait_ge(S_.xn2_ok, t + 1)
                    pool.tensor_tensor(x1, x1s[:], brow[:, 2], ALU.add).then_inc(S_.x1b_ok, 1)

            for t in range(4):
                step(t, s2=t >= 1, s4=t >= 3)
            with pool.Fori(4, NT) as t:
                step(t)
            for t in range(NT, NT + 3):
                step(t, s1=False, s2=t <= NT)

            def fetch(k, par, n):
                i = 2 * k + par
                q = (S_.yg_even, S_.yg_odd)[par]
                now = (S_.now_even, S_.now_odd)[par] if n else S_.now_first
                pool.wait_ge(S_.tok_ok, 1)
                if n >= 1:
                    pool.wait_ge(q, 16 * k)
                    pool.wait_ge(S_.yt2_mm, i - 1)
                pool.tensor_copy(tok_now[:, par:par + 1], tok_i[:, bass.ds(i, 1)]).then_inc(now, 1)
                pool.wait_ge(S_.slot_ok, 1)
                pool.wait_ge(now, k if n else par + 1)
                pool.indirect_dma_start(out=y_in[:, par], out_offset=None, in_=y_rows,
                                        in_offset=bass.IndirectOffsetOnAxis(ap=tok_now[:, par:par + 1], axis=0)).then_inc(q, 16)

            def store(k, par):
                i = 2 * k + par
                pool.wait_ge(S_.x_in, 16)
                pool.wait_ge(S_.o_ok2, i + 1)
                pool.dma_start(o_rows[bass.ds(i * P, P)], o_sb[:, par]).then_inc((S_.os_even, S_.os_odd)[par], 16)

            pool.wait_ge(S_.yr_out, 16 * NT)
            fetch(0, 0, 0)
            fetch(0, 1, 0)
            pool.wait_ge(S_.tab_ok, 1)
            pairs = pool.value_load(pairs_i[0:1, 0:1], min_val=NT - 2, max_val=ET // 2 - 2) + 2
            with pool.Fori(1, pairs) as k:
                for par in range(2):
                    fetch(k, par, 1)
                    store(k - 1, par)
            for par in range(2):
                store(pairs - 1, par)
            pool.wait_ge(S_.slotn_ok, 1)
            for i in range(NT):
                for k in range(2):
                    r = k * NT + i
                    pool.indirect_dma_start(out=o_tok[:, k, i], out_offset=None, in_=o_rows,
                                            in_offset=bass.IndirectOffsetOnAxis(ap=slot_n[:, r:r + 1], axis=0)).then_inc(
                        (S_.og0, S_.og1, S_.og2, S_.og3)[i * 4 // NT], 16)


def kernel(x, ctx_1024, mask_BxS2_ik0, L0_attn_W_in, L0_attn_b_in, L0_attn_W_out, L0_attn_b_out,
           L0_xattn_Wq, L0_xattn_bq, L0_xattn_Wk, L0_xattn_bk, L0_xattn_Wv, L0_xattn_bv, L0_xattn_Wo, L0_xattn_bo,
           L0_ffn_gate_w, L0_ffn_rms_w, L0_ffn_W1, L0_ffn_W2, L0_ffn_W3):
    import numpy as np
    import concourse.bacc as bacc
    from concourse.bass_utils import run_bass_kernel_spmd

    a = np.asarray
    laid_out = {
        "x": a(x),
        "ctx_t": a(ctx_1024).transpose(2, 0, 1).reshape(D, B * KC),
        "mask": a(mask_BxS2_ik0).reshape(1, B * KC),
        "w_in": a(L0_attn_W_in),
        "b_in": a(L0_attn_b_in).reshape(H, 2, P).transpose(1, 2, 0),
        "w_out": a(L0_attn_W_out),
        "w_x": np.stack([a(w).T for w in (L0_xattn_Wq, L0_xattn_Wk, L0_xattn_Wv, L0_xattn_Wo)]),
        "b_cols": np.concatenate([a(b).reshape(DC, P).T for b in (L0_xattn_bq, L0_xattn_bk)], axis=1),
        "rows_in": np.stack([a(b) for b in (L0_attn_b_out, L0_xattn_bv, L0_xattn_bo, L0_ffn_rms_w)]),
        "gate_w": a(L0_ffn_gate_w).T,
        "w1": a(L0_ffn_W1).transpose(0, 2, 1),
        "w2": a(L0_ffn_W2).transpose(0, 2, 1),
        "w3": a(L0_ffn_W3).transpose(0, 2, 1),
        "consts": constants(np),
        "r_consts": router_constants(np),
    }
    nc = bacc.Bacc("TRN2", target_bir_lowering=False, num_devices=1)
    laid_out = {n: np.ascontiguousarray(v) for n, v in laid_out.items()}
    args = [nc.dram_tensor(f"in_{n}", v.shape, mybir.dt.from_np(v.dtype), kind="ExternalInput").ap() for n, v in laid_out.items()]
    out = nc.dram_tensor("out_y", (B, T, D), F32, kind="ExternalOutput").ap()
    program(nc, *args, out)
    r = run_bass_kernel_spmd(nc, [{f"in_{n}": v for n, v in laid_out.items()}], core_ids=[0])
    return r.results[0]["out_y"]
```
